# Optimizing a Trainium2 kernel written in Bass

```python
import numpy as np
import jax
import jax.numpy as jnp

def _softmax(x, axis=-1):
    return jax.nn.softmax(x, axis=axis)

def _gelu(x):
    return jax.nn.gelu(x, approximate=True)

def _silu(x):
    return jax.nn.silu(x)

def _sigmoid(x):
    return jax.nn.sigmoid(x)

def _layernorm(x, axis=-1, eps=1e-05):
    m = jnp.mean(x, axis=axis, keepdims=True)
    v = jnp.var(x, axis=axis, keepdims=True)
    return (x - m) / jnp.sqrt(v + eps)

def _scatter_add(tgt, idx, src, axis=0):
    return tgt.at[idx].add(src)

def _segment_sum(src, seg, n):
    return jax.ops.segment_sum(src, seg, n)
kernel_name = 'mk_gnn_preln_d2_gnn_r16_f1004d'

def setup_inputs(seed: int=0):
    np.random.seed(seed)
    _w = jnp.asarray

    def _rec_inputs():
        import jax
        import jax.numpy as jnp
        _gk = jax.random.key(seed)
        x = 8.953e-05 + 1 * jax.random.normal(jax.random.fold_in(_gk, 1), (6250, 32), jnp.float32)
        src = jax.random.randint(jax.random.fold_in(_gk, 2), (200000,), 0, 6250, jnp.int32)
        dst = jax.random.randint(jax.random.fold_in(_gk, 3), (200000,), 0, 6250, jnp.int32)
        _o = jnp.argsort(dst, stable=True)
        src = src[_o]
        dst = dst[_o]
        edge_attr_3 = jax.random.uniform(jax.random.fold_in(_gk, 11), (200000, 3), jnp.float32, 0.0, 0.999998)
        edge_weight1 = jax.random.uniform(jax.random.fold_in(_gk, 13), (200000, 1), jnp.float32, 0.0, 1)
        return (x, src, dst, edge_attr_3, edge_weight1)
    x, src, dst, edge_attr_3, edge_weight1 = _rec_inputs()

    def _L0_gnn_setup():
        import jax, jax.numpy as jnp
        import numpy as np
        D = 3
        KS = 5
        K = KS ** D
        S = 2 ** D
        _COMBOS = np.array([[s >> d & 1 for d in range(D)] for s in range(S)], dtype=np.int32)
        _STRIDES = np.array([KS ** (D - 1 - d) for d in range(D)], dtype=np.int32)

        def spline_basis(pseudo):
            pos = pseudo * (KS - 1)
            i0 = jnp.clip(jnp.floor(pos), 0, KS - 2).astype(jnp.int32)
            frac = pos - i0
            combos = jnp.asarray(_COMBOS)
            basis = jnp.prod(jnp.where(combos[None] == 1, frac[:, None, :], 1.0 - frac[:, None, :]), axis=-1)
            idx = jnp.sum((i0[:, None, :] + combos[None]) * jnp.asarray(_STRIDES)[None, None, :], axis=-1)
            return (basis, idx)

        def spline_conv(x, row, col, basis, idx, W, b):
            N = x.shape[0]
            Fout = W.shape[2]
            z = jnp.einsum('ni,kio->nko', x, W).reshape(N * K, Fout)
            gathered = z[col[:, None] * K + idx]
            msg = jnp.einsum('es,eso->eo', basis, gathered)
            out = jax.ops.segment_sum(msg, row, num_segments=N)
            deg = jax.ops.segment_sum(jnp.ones_like(msg[:, 0]), row, num_segments=N)
            return out / jnp.maximum(deg, 1.0)[:, None] + b
        key = jax.random.key(seed)
        ks = jax.random.split(key, 13)
        N, E, Fin, Fout = (1250, 20000, 32, 32)

        def u(k, shape, size):
            bound = 1.0 / np.sqrt(size)
            return jax.random.uniform(k, shape, jnp.float32, -bound, bound)
        return dict(x=jax.random.normal(ks[0], (N, Fin), jnp.float32), edge_index=jax.random.randint(ks[1], (2, E), 0, N, dtype=jnp.int32), pseudo=jax.random.uniform(ks[2], (E, D), jnp.float32), stn1_w=u(ks[3], (K, 1, 64), 1 * S), stn1_b=u(ks[4], (64,), 1 * S), stn2_w=u(ks[5], (K, 64, 64), 64 * S), stn2_b=u(ks[6], (64,), 64 * S), stn3_w=u(ks[7], (64, 64), 64), stn3_b=u(ks[8], (64,), 64), stn4_w=u(ks[9], (64, 3), 64), stn4_b=u(ks[10], (3,), 64), conv_w=u(ks[11], (K, Fin, Fout), Fin * S), conv_b=u(ks[12], (Fout,), Fin * S))
    _L0_gnn_all = _L0_gnn_setup()
    _L0_gnn_in = {k: v for k, v in _L0_gnn_all.items() if k in ('stn1_w', 'stn1_b', 'stn2_w', 'stn2_b', 'stn3_w', 'stn3_b', 'stn4_w', 'stn4_b', 'conv_w', 'conv_b')}
    del _L0_gnn_all

    def _L1_gnn_setup():
        import jax, jax.numpy as jnp
        import numpy as np
        N = 3125
        E = 100000
        D = 32
        H = 32
        key = jax.random.key(seed)
        ks = jax.random.split(key, 12)
        inputs = jax.random.normal(ks[0], (N, D), dtype=jnp.float32)
        e = jax.random.uniform(ks[1], (E, 1), dtype=jnp.float32)
        edge_index = jax.random.randint(ks[2], (2, E), 0, N, dtype=jnp.int64)
        s = 0.05
        W1 = jax.random.normal(ks[3], (3 * D, H), dtype=jnp.float32) * s
        b1 = jnp.zeros((H,), dtype=jnp.float32)
        W2 = jax.random.normal(ks[4], (H, H), dtype=jnp.float32) * s
        b2 = jnp.zeros((H,), dtype=jnp.float32)
        W3 = jax.random.normal(ks[5], (H, H), dtype=jnp.float32) * s
        b3 = jnp.zeros((H,), dtype=jnp.float32)
        W4 = jax.random.normal(ks[6], (H, H), dtype=jnp.float32) * s
        b4 = jnp.zeros((H,), dtype=jnp.float32)
        return {'inputs': inputs, 'e': e, 'edge_index': edge_index, 'W1': W1, 'b1': b1, 'W2': W2, 'b2': b2, 'W3': W3, 'b3': b3, 'W4': W4, 'b4': b4}
    _L1_gnn_all = _L1_gnn_setup()
    _L1_gnn_in = {k: v for k, v in _L1_gnn_all.items() if k in ('W1', 'b1', 'W2', 'b2', 'W3', 'b3', 'W4', 'b4')}
    del _L1_gnn_all
    return {'x': x, 'src': src, 'dst': dst, 'edge_attr_3': edge_attr_3, 'edge_weight1': edge_weight1, 'L0_gnn_stn1_w': _L0_gnn_in['stn1_w'], 'L0_gnn_stn1_b': _L0_gnn_in['stn1_b'], 'L0_gnn_stn2_w': _L0_gnn_in['stn2_w'], 'L0_gnn_stn2_b': _L0_gnn_in['stn2_b'], 'L0_gnn_stn3_w': _L0_gnn_in['stn3_w'], 'L0_gnn_stn3_b': _L0_gnn_in['stn3_b'], 'L0_gnn_stn4_w': _L0_gnn_in['stn4_w'], 'L0_gnn_stn4_b': _L0_gnn_in['stn4_b'], 'L0_gnn_conv_w': _L0_gnn_in['conv_w'], 'L0_gnn_conv_b': _L0_gnn_in['conv_b'], 'L1_gnn_W1': _L1_gnn_in['W1'], 'L1_gnn_b1': _L1_gnn_in['b1'], 'L1_gnn_W2': _L1_gnn_in['W2'], 'L1_gnn_b2': _L1_gnn_in['b2'], 'L1_gnn_W3': _L1_gnn_in['W3'], 'L1_gnn_b3': _L1_gnn_in['b3'], 'L1_gnn_W4': _L1_gnn_in['W4'], 'L1_gnn_b4': _L1_gnn_in['b4']}

def reference(x, src, dst, edge_attr_3, edge_weight1, L0_gnn_stn1_w, L0_gnn_stn1_b, L0_gnn_stn2_w, L0_gnn_stn2_b, L0_gnn_stn3_w, L0_gnn_stn3_b, L0_gnn_stn4_w, L0_gnn_stn4_b, L0_gnn_conv_w, L0_gnn_conv_b, L1_gnn_W1, L1_gnn_b1, L1_gnn_W2, L1_gnn_b2, L1_gnn_W3, L1_gnn_b3, L1_gnn_W4, L1_gnn_b4):
    import jax
    import jax.numpy as jnp

    def _L0_gnn_ref(x, edge_index, pseudo, stn1_w, stn1_b, stn2_w, stn2_b, stn3_w, stn3_b, stn4_w, stn4_b, conv_w, conv_b):
        import jax, jax.numpy as jnp
        import numpy as np
        D = 3
        KS = 5
        K = KS ** D
        S = 2 ** D
        _COMBOS = np.array([[s >> d & 1 for d in range(D)] for s in range(S)], dtype=np.int32)
        _STRIDES = np.array([KS ** (D - 1 - d) for d in range(D)], dtype=np.int32)

        def spline_basis(pseudo):
            pos = pseudo * (KS - 1)
            i0 = jnp.clip(jnp.floor(pos), 0, KS - 2).astype(jnp.int32)
            frac = pos - i0
            combos = jnp.asarray(_COMBOS)
            basis = jnp.prod(jnp.where(combos[None] == 1, frac[:, None, :], 1.0 - frac[:, None, :]), axis=-1)
            idx = jnp.sum((i0[:, None, :] + combos[None]) * jnp.asarray(_STRIDES)[None, None, :], axis=-1)
            return (basis, idx)

        def spline_conv(x, row, col, basis, idx, W, b):
            N = x.shape[0]
            Fout = W.shape[2]
            z = jnp.einsum('ni,kio->nko', x, W).reshape(N * K, Fout)
            gathered = z[col[:, None] * K + idx]
            msg = jnp.einsum('es,eso->eo', basis, gathered)
            out = jax.ops.segment_sum(msg, row, num_segments=N)
            deg = jax.ops.segment_sum(jnp.ones_like(msg[:, 0]), row, num_segments=N)
            return out / jnp.maximum(deg, 1.0)[:, None] + b
        N = x.shape[0]
        row, col = (edge_index[0], edge_index[1])
        basis, idx = spline_basis(pseudo)
        h = jnp.ones((N, 1), x.dtype)
        h = jax.nn.elu(spline_conv(h, row, col, basis, idx, stn1_w, stn1_b))
        h = jax.nn.elu(spline_conv(h, row, col, basis, idx, stn2_w, stn2_b))
        h = jax.nn.elu(h @ stn3_w + stn3_b)
        t = h @ stn4_w + stn4_b
        new_pseudo = jnp.clip(pseudo + t[col] - t[row], 0.0, 1.0)
        basis2, idx2 = spline_basis(new_pseudo)
        return spline_conv(x, row, col, basis2, idx2, conv_w, conv_b)

    def _L1_gnn_ref(inputs, e, edge_index, W1, b1, W2, b2, W3, b3, W4, b4):
        import jax, jax.numpy as jnp
        import numpy as np
        N = 3125
        E = 100000
        D = 32
        H = 32
        x = inputs
        src = edge_index[0]
        dst = edge_index[1]
        ex1 = e * x[src]
        ex2 = e * x[dst]
        mi = jnp.zeros_like(x).at[dst].add(ex1)
        mo = jnp.zeros_like(x).at[src].add(ex2)
        h = jnp.concatenate([mi, mo, x], axis=1)
        h = jnp.tanh(h @ W1 + b1)
        h = jnp.tanh(h @ W2 + b2)
        h = jnp.tanh(h @ W3 + b3)
        return jnp.tanh(h @ W4 + b4)
    edge_index = jnp.stack([src, dst])
    h = jnp.maximum(_layernorm(x, axis=-1), 0.0)
    x = x + _L0_gnn_ref(h, edge_index, edge_attr_3, L0_gnn_stn1_w, L0_gnn_stn1_b, L0_gnn_stn2_w, L0_gnn_stn2_b, L0_gnn_stn3_w, L0_gnn_stn3_b, L0_gnn_stn4_w, L0_gnn_stn4_b, L0_gnn_conv_w, L0_gnn_conv_b)
    h = jnp.maximum(_layernorm(x, axis=-1), 0.0)
    x = x + _L1_gnn_ref(h, edge_weight1, edge_index, L1_gnn_W1, L1_gnn_b1, L1_gnn_W2, L1_gnn_b2, L1_gnn_W3, L1_gnn_b3, L1_gnn_W4, L1_gnn_b4)
    return x

_drawn_inputs = setup_inputs


def setup_inputs(seed=0):
    import zlib

    import numpy as np

    out = dict(_drawn_inputs(seed))
    spreads = {'L1_gnn_b1': (0.0, 2.0),
     'L1_gnn_b2': (0.0, 0.8),
     'L1_gnn_b3': (0.0, 0.34),
     'L1_gnn_b4': (0.0, 0.1)}
    factors = {'edge_attr_3': 4.112,
     'edge_weight1': 8.0,
     'L0_gnn_stn1_w': 8.0,
     'L0_gnn_stn1_b': 200.0,
     'L0_gnn_stn2_w': 8.0,
     'L0_gnn_stn2_b': 8.0,
     'L0_gnn_stn3_w': 8.0,
     'L0_gnn_stn3_b': 8.0,
     'L0_gnn_stn4_w': 8.0,
     'L0_gnn_stn4_b': 8.0,
     'L0_gnn_conv_w': 3.577,
     'L1_gnn_W1': 2.744,
     'L1_gnn_W2': 4.171,
     'L1_gnn_W3': 3.167}
    for name, (base, spread) in spreads.items():
        noise = np.random.default_rng([zlib.crc32(name.encode()), seed]).standard_normal(out[name].shape)
        drawn = base * np.exp(spread * noise) if base else spread * noise
        out[name] = jnp.asarray(drawn.astype(out[name].dtype))
    for name, factor in factors.items():
        out[name] = (out[name] * factor).astype(out[name].dtype)
    return out
```

```python
from contextlib import ExitStack

import numpy as np
import concourse.bass as bass
from concourse import mybir

F32 = mybir.dt.float32
F16 = mybir.dt.float16
BF16 = mybir.dt.bfloat16
I32 = mybir.dt.int32
U32 = mybir.dt.uint32
ALU = mybir.AluOpType
ACT = mybir.ActivationFunctionType
AX = mybir.AxisListType.X
PE, DVE = mybir.EngineType.PE, mybir.EngineType.DVE
ds = bass.ds

P = 128
N, F, H = 6250, 32, 64
E = 200000
EP, ET = 125, 1600
SRC_SB, DST_SB = 256, 512
SRC_SHIFT, DST_SHIFT = 8, 9
NA, ND = -(-N // SRC_SB), -(-N // DST_SB)
NBUCK = NA * ND
NBUCK2 = NBUCK + NBUCK % 2
NBLK = ND * DST_SB // P
FULL_BLK, REST = N // P, N % P
KS, K3 = 5, 125
NCELL = 64
CH = 16
CHAINS = 4
PER = CH // CHAINS


def chunks_for(buckets):
    tiles = (E + (P - 1) * buckets) // P
    step = 2 * CH
    return -(-tiles // step) * 2


NCHK_B = chunks_for(NBUCK)
NCHK_C = chunks_for(NCELL)
NT, NTC = NCHK_B * CH, NCHK_C * CH
EDGE_W = 8
C1_W, C2_W = H + 4, F + 4
NOWHERE = 1.0e7
NQ = -(-NT // P)
NQC = -(-NTC // P)
EPS = 1e-5


class Program:

    def __init__(self, nc):
        self.nc = nc


class NormBuffers:

    def __init__(self, mean, var, std, sq):
        self.mean, self.var, self.std, self.sq = mean, var, std, sq


class TableBuffers:

    def __init__(self, ones, t_i, hit):
        self.ones, self.t_i, self.hit = ones, t_i, hit


class Steps:

    def __init__(self, eng, sem, base=0, turns=None):
        self.eng, self.sem, self.base, self.n, self.turns = eng, sem, base, 0, turns

    def add(self, ins):
        ins.then_inc(self.sem, 1)
        self.n += 1

    def wait(self):
        self.eng.wait_ge(self.sem, self.base + self.n)
        if self.turns is not None:
            self.eng.sem_inc(self.turns, 1)

    def do(self, ins):
        self.add(ins)
        self.wait()


def load_values(nc, engine, ap, most):
    _, values = nc.values_load_multi_w_load_instructions(
        ap, engines=(engine,), min_val=0, max_val=most,
        skip_runtime_bounds_check_because="the tables are clamped where they are made")
    return values


def layer_norm(dve, act_sqrt, st, v, xin, out):
    st.do(dve.tensor_reduce(v.mean[:, :], xin[:, :, :], AX, ALU.add))
    st.do(dve.tensor_scalar(v.mean[:, :], v.mean[:, :], 1.0 / F, None, ALU.mult))
    st.do(dve.tensor_tensor(out[:, :, :], xin[:, :, :],
                            v.mean[:, :].unsqueeze(2).to_broadcast([P, NBLK, F]), ALU.subtract))
    st.do(dve.tensor_tensor(v.sq[:, :, :], out[:, :, :], out[:, :, :], ALU.mult))
    st.do(dve.tensor_reduce(v.var[:, :], v.sq[:, :, :], AX, ALU.add))
    st.do(dve.tensor_scalar(v.var[:, :], v.var[:, :], 1.0 / F, EPS, ALU.mult, ALU.add))
    act_sqrt()
    st.do(dve.reciprocal(v.var[:, :], v.std[:, :]))
    st.do(dve.tensor_tensor(out[:, :, :], out[:, :, :],
                            v.var[:, :].unsqueeze(2).to_broadcast([P, NBLK, F]), ALU.mult))


def split_parts(dve, st, parts, val, rest):
    st.do(dve.tensor_copy(parts[0], val))
    st.do(dve.tensor_tensor(rest, val, parts[0], ALU.subtract))
    st.do(dve.tensor_copy(parts[1], rest))
    st.do(dve.tensor_tensor(rest, rest, parts[1], ALU.subtract))
    st.do(dve.tensor_copy(parts[2], rest))


def cell_and_fraction(eng, st, pos, base, frac, tmp, base_only_steps=False):
    st.do(eng.tensor_scalar(base, pos, 1.0, None, ALU.is_ge))
    for knot in (2.0, 3.0):
        st.do(eng.tensor_scalar(tmp, pos, knot, None, ALU.is_ge))
        st.do(eng.tensor_tensor(base, base, tmp, ALU.add))
    st.do(eng.tensor_tensor(frac, pos, base, ALU.subtract))


def program(nc, x, src, dst, attr, wt, stn1_w, stn1_b, stn2_w, stn2_b, stn3_w, stn3_b, stn4_w,
            stn4_b, conv_w, conv_b, W1, b1, W2, b2, W3, b3, W4, b4, out, stop_after=99):
    root = ExitStack()
    with root:
        g = Program(nc=nc)

        def sb(name, shape, dt=F32, ctx=root):
            return ctx.enter_context(nc.sbuf_tensor(name, shape, dt))

        used = []

        def sem(name):
            used.append(nc.alloc_semaphore(name=name))
            return used[-1]

        def recycle():
            done = [s for s in used if "sent" not in s.name]
            used.clear()
            nc.all_engine_barrier()
            nc.clear_and_free_semaphores(done)
            nc.all_engine_barrier()

        g.sb, g.sem = sb, sem
        g.edges_b = nc.dram_tensor("edges_b", (P * NT, EDGE_W), F32).ap()
        g.rows_c1 = nc.dram_tensor("rows_c1", (P * NTC, C1_W), F32).ap()
        g.rows_c2 = nc.dram_tensor("rows_c2", (P * NTC, C2_W), F32).ap()
        g.msg1 = nc.dram_tensor("msg1", (P * NT, H), F32).ap()
        g.msg2 = nc.dram_tensor("msg2", (P * NT, F), F32).ap()
        g.local_rows = nc.dram_tensor("local_rows", (2, NQ * P, P), F16).ap()
        g.tab_b = nc.dram_tensor("tab_b", (2, NQ * P), I32).ap()
        g.tab_c1 = nc.dram_tensor("tab_c1", (1, NQC * P), I32).ap()
        g.tab_c2 = nc.dram_tensor("tab_c2", (1, NQC * P), I32).ap()
        g.iota = sb("iota", [P, DST_SB], I32)
        g.iota16 = sb("iota16", [P, DST_SB], F16)
        g.iotaf = sb("iotaf", [P, DST_SB])
        g.nodecol_i = sb("nodecol_i", [P, NQ], I32)
        g.nodecol = sb("nodecol", [P, NQ])
        g.ident = sb("ident", [P, P])
        g.before = sb("before", [P, P], F16)
        g.from_on = sb("from_on", [P, P], F16)
        g.ones16 = sb("ones16", [P, P], F16)
        g.onesf = sb("onesf", [1, P])
        g.zero512 = sb("zero512", [P, 512])
        g.x = sb("x_nodes", [P, NBLK, F])
        g.h = sb("h_nodes", [P, NBLK, F])
        g.rdeg = sb("rdeg", [P, NBLK])
        g.hparts = sb("hparts", [P, NBLK, 3, F], BF16)
        g.table_b = sb("table_b", [1, 2, NQ * P], I32)
        g.table_c = sb("table_c", [1, NQC * P], I32)
        g.mean, g.var, g.std = (sb(n, [P, NBLK]) for n in ("ln_mean", "ln_var", "ln_std"))
        g.stop_after = stop_after
        with ExitStack() as c:
            order_edges(g, c, x, src, dst, attr, wt)
        if stop_after < 2:
            return finish(g, out)
        with ExitStack() as c:
            g.edges = sb("edges", [P, NT, EDGE_W], F32, c)
            g.tparts = sb("tparts", [P, NBLK, 3, 3], BF16, c)
            g.tparts_neg = sb("tparts_neg", [P, NBLK, 3, 3], BF16, c)
            with ExitStack() as c1:
                g.h1parts = sb("h1parts", [P, NBLK, 3, H], BF16, c1)
                with ExitStack() as c2:
                    degree_and_first_conv(g, c2, stn1_w, stn1_b)
                if stop_after < 3:
                    return finish(g, out)
                with ExitStack() as c2:
                    to_cells_1(g, c2)
            if stop_after < 4:
                return finish(g, out)
            with ExitStack() as c2:
                cell_products(g, c2, "c1", g.rows_c1, g.tab_c1, g.msg1, stn2_w, H)
            if stop_after < 5:
                return finish(g, out)
            with ExitStack() as c2:
                shift_network(g, c2, stn2_b, stn3_w, stn3_b, stn4_w, stn4_b)
            if stop_after < 6:
                return finish(g, out)
            recycle()
            with ExitStack() as c2:
                to_cells_2(g, c2)
            if stop_after < 7:
                return finish(g, out)
            with ExitStack() as c2:
                cell_products(g, c2, "c2", g.rows_c2, g.tab_c2, g.msg2, conv_w, F)
            if stop_after < 8:
                return finish(g, out)
            with ExitStack() as c2:
                end_first_layer(g, c2, conv_b)
            if stop_after < 9:
                return finish(g, out)
            with ExitStack() as c2:
                second_layer(g, c2, W1, b1, W2, b2, W3, b3, W4, b4, out)


def finish(g, out):
    nc = g.nc
    s = g.sem("s_fin")
    with nc.Block() as block:
        @block.sync
        def _(sp):
            sp.dma_start(out[0:FULL_BLK * P, :].rearrange("(b p) f -> p b f", p=P),
                         g.h[:, 0:FULL_BLK, :]).then_inc(s, 16)
            sp.wait_ge(s, 16)


def order_edges(g, c, x, src, dst, attr, wt):
    nc, sem = g.nc, g.sem
    sb = lambda n, s, d=F32: g.sb(n, s, d, c)
    edge = sb("edge", [EP, ET, 6])
    bucket, cell = sb("bucket", [EP, ET]), sb("cell", [EP, ET])
    no_edge = sb("no_edge", [P, NT // 32, EDGE_W])
    no_c1 = sb("no_c1", [P, NTC // 96, C1_W])
    no_c2 = sb("no_c2", [P, NTC // 48, C2_W])
    zeros = sb("zeros", [P, NT, 1])
    loads = ExitStack()
    src_i, dst_i, tmp_i = (g.sb(n, [EP, ET], I32, loads) for n in ("src_i", "dst_i", "tmp_i"))
    attr_in, base3 = (g.sb(n, [EP, ET, 3], F32, loads) for n in ("attr_in", "base3"))
    wt_in = g.sb("wt_in", [EP, ET], F32, loads)
    ln = NormBuffers(mean=g.mean, var=g.var, std=g.std, sq=g.sb("ln_sq", [P, NBLK, F], F32, loads))

    s_load, s_nodes, s_id = sem("s_edge_loads"), sem("s_node_loads"), sem("s_iota")
    s_dve, s_pool, s_fill = sem("s_dve_a"), sem("s_pool_a"), sem("s_fill")
    s_var, s_std, s_copied, s_blank = sem("s_var"), sem("s_std"), sem("s_copied"), sem("s_blank")
    s_xz = sem("s_x_zeroed")

    with nc.Block() as block:
        @block.sync
        def _(sp):
            sp.dma_start(src_i[:, :], src.rearrange("(p t) -> p t", p=EP)).then_inc(s_load, 16)
            sp.dma_start(dst_i[:, :], dst.rearrange("(p t) -> p t", p=EP)).then_inc(s_load, 16)
            sp.dma_start(attr_in[:, :, :], attr.rearrange("(p t) k -> p t k", p=EP)).then_inc(s_load, 16)
            sp.dma_start(wt_in[:, :], wt.rearrange("(p t) k -> p (t k)", p=EP)).then_inc(s_load, 16)
            sp.wait_ge(s_xz, 1)
            sp.dma_start(g.x[:, 0:FULL_BLK, :],
                         x[0:FULL_BLK * P, :].rearrange("(b p) f -> p b f", p=P)).then_inc(s_nodes, 16)
            sp.dma_start(g.x[0:REST, FULL_BLK, :], x[FULL_BLK * P:N, :]).then_inc(s_nodes, 16)
            sp.wait_ge(s_blank, 1)
            for buf, blank, times in ((g.edges_b, no_edge, 32), (g.rows_c1, no_c1, 96),
                                      (g.rows_c2, no_c2, 48)):
                view = buf.rearrange("(p t) w -> p t w", p=P)
                n = blank.shape[1]
                for k in range(times):
                    sp.dma_start(view[:, k * n:(k + 1) * n, :], blank[:, :, :]).then_inc(s_fill, 16)
            for buf, width in ((g.msg1, H), (g.msg2, F)):
                view = buf.rearrange("(p t) w -> p (t w)", p=P)
                for k in range(width):
                    sp.dma_start(view[:, k * NT:(k + 1) * NT], zeros[:, :, 0]).then_inc(s_fill, 16)

        @block.gpsimd
        def _(pool):
            pool.iota(g.iota[:, :], [[1, DST_SB]], 0, 0).then_inc(s_id, 1)
            pool.iota(g.nodecol_i[:, :], [[P, NQ]], 0, 1).then_inc(s_id, 1)
            st = Steps(pool, s_pool)
            st.add(pool.memset(g.onesf[:, :], 1.0))
            st.add(pool.memset(g.zero512[:, :], 0.0))
            st.add(pool.memset(g.ones16[:, :], 1.0))
            st.add(pool.memset(no_edge[:, :, :], 0.0))
            st.add(pool.memset(no_c1[:, :, :], 0.0))
            st.add(pool.memset(no_c2[:, :, :], 0.0))
            st.do(pool.memset(zeros[:, :, :], 0.0))
            st.add(pool.memset(no_edge[:, :, 0:2], -1.0))
            st.add(pool.memset(no_edge[:, :, 6:7], NOWHERE))
            st.add(pool.memset(no_c1[:, :, C1_W - 1:C1_W], NOWHERE))
            st.do(pool.memset(no_c2[:, :, C2_W - 1:C2_W], NOWHERE))
            pool.sem_inc(s_blank, 1)

        @block.scalar
        def _(act):
            act.wait_ge(s_load, 64)
            act.activation(edge[:, :, 2:5], attr_in[:, :, :], ACT.Copy).then_inc(s_copied, 1)
            act.activation(edge[:, :, 5], wt_in[:, :], ACT.Copy).then_inc(s_copied, 1)
            act.wait_ge(s_var, 1)
            act.activation(g.std[:, :], g.var[:, :], ACT.Sqrt).then_inc(s_std, 1)

        @block.vector
        def _(dve):
            st = Steps(dve, s_dve)
            st.do(dve.memset(g.x[:, :, :], 0.0))
            dve.sem_inc(s_xz, 1)
            dve.wait_ge(s_id, 2)
            st.add(dve.tensor_copy(g.iota16[:, :], g.iota[:, :]))
            st.add(dve.tensor_copy(g.nodecol[:, :], g.nodecol_i[:, :]))
            st.do(dve.tensor_copy(g.iotaf[:, :], g.iota[:, :]))
            st.add(dve.tensor_scalar(g.ident[:, :], g.iotaf[:, 0:P], g.nodecol[:, 0:1], None, ALU.is_equal))
            st.add(dve.tensor_scalar(g.before[:, :], g.iotaf[:, 0:P], g.nodecol[:, 0:1], None, ALU.is_gt))
            st.add(dve.tensor_scalar(g.from_on[:, :], g.iotaf[:, 0:P], g.nodecol[:, 0:1], None, ALU.is_le))
            dve.wait_ge(s_load, 64)
            st.do(dve.tensor_scalar(tmp_i[:, :], src_i[:, :], SRC_SB - 1, None, ALU.bitwise_and))
            st.do(dve.tensor_copy(edge[:, :, 0], tmp_i[:, :]))
            st.do(dve.tensor_scalar(src_i[:, :], src_i[:, :], SRC_SHIFT, None, ALU.logical_shift_right))
            st.do(dve.tensor_scalar(tmp_i[:, :], dst_i[:, :], DST_SB - 1, None, ALU.bitwise_and))
            st.do(dve.tensor_copy(edge[:, :, 1], tmp_i[:, :]))
            st.do(dve.tensor_scalar(dst_i[:, :], dst_i[:, :], DST_SHIFT, None, ALU.logical_shift_right))
            st.do(dve.scalar_tensor_tensor(bucket[:, :], src_i[:, :], float(ND), dst_i[:, :], ALU.mult, ALU.add))
            dve.wait_ge(s_copied, 2)
            st.do(dve.tensor_scalar(attr_in[:, :, :], attr_in[:, :, :], float(KS - 1), None, ALU.mult))
            st.do(dve.tensor_scalar(base3[:, :, :], attr_in[:, :, :], 1.0, None, ALU.is_ge))
            for knot in (2.0, 3.0):
                st.do(dve.scalar_tensor_tensor(base3[:, :, :], attr_in[:, :, :], knot, base3[:, :, :],
                                               ALU.is_ge, ALU.add))
            st.do(dve.scalar_tensor_tensor(cell[:, :], base3[:, :, 0], 4.0, base3[:, :, 1], ALU.mult, ALU.add))
            st.do(dve.scalar_tensor_tensor(cell[:, :], cell[:, :], 4.0, base3[:, :, 2], ALU.mult, ALU.add))
            dve.wait_ge(s_nodes, 32)

            def root():
                dve.sem_inc(s_var, 1)
                dve.wait_ge(s_std, 1)
            layer_norm(dve, root, st, ln, g.x, g.h)
            st.do(dve.tensor_scalar(g.h[:, :, :], g.h[:, :, :], 0.0, None, ALU.max))
            split_parts(dve, st, [g.hparts[:, :, k, :] for k in range(3)], g.h[:, :, :], ln.sq[:, :, :])

    loads.close()

    LOOP = ET // CH // 2
    chain_len = ET // CHAINS
    BOTH = NBUCK2 + NCELL
    hot = sb("hot", [EP, 2, CH, BOTH], F16)
    acc = c.enter_context(nc.psum_tensor("acc", [P, CHAINS, 512], F32))
    s_hot, s_hot_free, s_tot = sem("s_hot"), sem("s_hot_free"), sem("s_totals")

    def tile_of(k, q):
        return (q // PER) * chain_len + k * PER + q % PER

    def make_hot(dve, k, half):
        for q in range(CH):
            t = tile_of(k, q)
            dve.tensor_scalar(hot[:, half, q, 0:NBUCK2], g.iota16[0:EP, 0:NBUCK2], bucket[:, ds(t, 1)],
                              None, ALU.is_equal)
            last = dve.tensor_scalar(hot[:, half, q, NBUCK2:BOTH], g.iota16[0:EP, 0:NCELL],
                                     cell[:, ds(t, 1)], None, ALU.is_equal)
        return last

    with nc.Block() as block:
        @block.vector
        def _(dve):
            with dve.Fori(0, LOOP) as i:
                for half in range(2):
                    k = i * 2 + half
                    dve.wait_ge(s_hot_free, k + 1)
                    make_hot(dve, k, half).then_inc(s_hot, 1)

        @block.tensor
        def _(pe):
            for ch in range(CHAINS):
                pe.matmul(acc[:, ch, :], g.ident[:, :], g.zero512[:, :], start=True, stop=True)
            pe.sem_inc(s_hot_free, 2)
            with pe.Fori(0, LOOP) as i:
                for half in range(2):
                    pe.wait_ge(s_hot, i * 2 + half + 1)
                    for q in range(CH):
                        last = pe.matmul(acc[:, q // PER, 0:BOTH], g.ones16[0:EP, :],
                                         hot[:, half, q, :], start=False, stop=True,
                                         skip_group_check=True)
                    last.then_inc(s_hot_free, 1)

    tot_b, tot_c = sb("tot_b", [P, CHAINS, NBUCK2]), sb("tot_c", [P, CHAINS, NCELL])
    start = sb("start", [P, CHAINS, BOTH])
    start_b, start_c = start[:, :, 0:NBUCK2], start[:, :, NBUCK2:BOTH]
    cum_b, cum_c = sb("cum_b", [P, NBUCK2]), sb("cum_c", [P, NCELL])
    t_i = sb("t_i", [P, NBUCK2], I32)
    ones_b = sb("ones_b", [P, NBUCK2])
    count_b, count_a, count_c = sb("count_b", [P, NQ]), sb("count_a", [P, NQ]), sb("count_c", [P, NQC])
    count_i = sb("count_i", [P, 2, NQ], I32)
    count_ci = sb("count_ci", [P, NQC], I32)
    tab = TableBuffers(ones=ones_b, t_i=t_i, hit=sb("hit_b", [P, NBUCK2]))
    s_start, s_init, s_tabs, s_tab_out = sem("s_starts"), sem("s_chains_init"), sem("s_tables"), sem("s_tables_out")
    s_dve_b = sem("s_dve_b")
    with nc.Block() as block:
        @block.vector
        def _(dve):
            st = Steps(dve, s_dve_b)
            st.add(dve.memset(ones_b[:, :], 1.0))
            st.add(dve.tensor_copy(tot_b[:, :, :], acc[:, :, 0:NBUCK2]))
            st.do(dve.tensor_copy(tot_c[:, :, :], acc[:, :, NBUCK2:BOTH]))
            bucket_starts(dve, st, tab, tot_b, start_b, cum_b, NBUCK2)
            bucket_starts(dve, st, tab, tot_c, start_c, cum_c, NCELL)
            dve.sem_inc(s_start, 1)
            for q in range(NQ):
                st.do(dve.tensor_scalar(tab.hit[:, 0:NBUCK], cum_b[:, 0:NBUCK], g.nodecol[:, q:q + 1], None,
                                        ALU.is_le, ALU.add, accum_out=count_b[:, q:q + 1]))
                st.do(dve.tensor_scalar(tab.hit[:, 0:NA], cum_b[:, ND - 1:NBUCK:ND], g.nodecol[:, q:q + 1],
                                        None, ALU.is_le, ALU.add, accum_out=count_a[:, q:q + 1]))
            st.do(dve.tensor_scalar(count_b[:, :], count_b[:, :], float(NBUCK - 1), None, ALU.min))
            st.do(dve.tensor_scalar(count_a[:, :], count_a[:, :], float(NA - 1), None, ALU.min))
            st.do(dve.tensor_copy(count_i[:, 0, :], count_a[:, :]))
            st.do(dve.scalar_tensor_tensor(count_i[:, 1, :], count_a[:, :], -float(ND), count_b[:, :],
                                           ALU.mult, ALU.add))
            cell_table(dve, st, g, tab, cum_c, count_c, count_ci)
            dve.sem_inc(s_tabs, 1)

        @block.tensor
        def _(pe):
            pe.wait_ge(s_start, 1)
            for ch in range(CHAINS):
                pe.matmul(acc[:, ch, 0:BOTH], g.onesf[:, :], start[0:1, ch, :], start=True, stop=True)

        @block.sync
        def _(sp):
            sp.wait_ge(s_tabs, 1)
            with nc.allow_non_contiguous_dma(reason="small tables"):
                sp.dma_start(g.tab_b.rearrange("k (q p) -> p k q", p=P), count_i[:, :, :]).then_inc(s_tab_out, 16)
                sp.dma_start(g.tab_c1[0, :].rearrange("(q p) -> p q", p=P), count_ci[:, :]).then_inc(s_tab_out, 16)
            sp.wait_ge(s_tab_out, 32)
            sp.dma_start(g.table_b[0:1, :, :], g.tab_b.rearrange("(o k) n -> o k n", o=1)).then_inc(s_tab_out, 16)
            sp.wait_ge(s_tab_out, 48)
            sp.wait_ge(s_fill, 16 * (32 + 96 + 48 + H + F))

    place = sb("place", [EP, 2, CH])
    place_i, low_i, high_i = (sb(n, [EP, 2, CH], I32) for n in ("place_i", "low_i", "high_i"))
    hit = sb("hit", [EP, CHAINS, BOTH], BF16)
    row_stage = sb("row_stage", [EP, 2, CH, EDGE_W])
    idx_stage = sb("idx_stage", [EP, 2, CH], U32)
    s_hot2, s_pe_done = sem("s_hot2"), sem("s_hot2_free")
    s_before = [sem(f"s_before{j}") for j in range(2)]
    s_read = [sem(f"s_read{j}") for j in range(2)]
    s_rows, s_sent = sem("s_rows_ready"), [sem(f"s_rows_sent{j}") for j in range(2)]
    s_dve_c, s_tick = sem("s_dve_c"), sem("s_pool_turns")
    STEPS_C = 6
    PAIRS = CHAINS // 2
    with nc.Block() as block:
        @block.vector
        def _(dve):
            dve.memset(row_stage[:, :, :, :], 0.0).then_inc(s_dve_c, 1)
            dve.wait_ge(s_dve_c, 1)
            with dve.Fori(0, LOOP) as i:
                for half in range(2):
                    st = Steps(dve, s_dve_c, i * (2 * STEPS_C) + half * STEPS_C + 1)
                    k = i * 2 + half
                    dve.wait_ge(s_pe_done, k + 1)
                    make_hot(dve, k, half).then_inc(s_hot2, 1)
                    dve.wait_ge(s_hot2, k + 1)
                    for step in range(PER):
                        for j in range(2):
                            dve.wait_ge(s_before[j], k * PER + step + 1)
                            dve.wait_ge(s_read[j], k * PER + step)
                            for ch in (2 * j, 2 * j + 1):
                                q = ch * PER + step
                                dve.scalar_tensor_tensor(
                                    hit[:, ch, 0:NBUCK2], hot[:, half, q, 0:NBUCK2], 1.0, acc[0:EP, ch, 0:NBUCK2],
                                    ALU.mult, ALU.mult, accum_out=place[:, 0, q:q + 1])
                                last = dve.scalar_tensor_tensor(
                                    hit[:, ch, NBUCK2:BOTH], hot[:, half, q, NBUCK2:BOTH], 1.0,
                                    acc[0:EP, ch, NBUCK2:BOTH],
                                    ALU.mult, ALU.mult, accum_out=place[:, 1, q:q + 1])
                            last.then_inc(s_read[j], 1)
                    dve.wait_ge(s_sent[half], i * CH * 16)
                    for j in range(2):
                        dve.wait_ge(s_read[j], (k + 1) * PER)
                    st.do(dve.tensor_copy(place_i[:, :, :], place[:, :, :]))
                    st.add(dve.tensor_scalar(low_i[:, :, :], place_i[:, :, :], P - 1, None, ALU.bitwise_and))
                    st.do(dve.tensor_scalar(high_i[:, :, :], place_i[:, :, :], 7, None, ALU.logical_shift_right))
                    st.add(dve.scalar_tensor_tensor(idx_stage[:, half, :], low_i[:, 0, :], float(NT),
                                                    high_i[:, 0, :], ALU.mult, ALU.add))
                    st.add(dve.scalar_tensor_tensor(row_stage[:, half, :, 7], low_i[:, 0, :], float(NT),
                                                    high_i[:, 0, :], ALU.mult, ALU.add))
                    st.add(dve.scalar_tensor_tensor(row_stage[:, half, :, 6], low_i[:, 1, :], float(NTC),
                                                    high_i[:, 1, :], ALU.mult, ALU.add))
                    for ch in range(CHAINS):
                        last = dve.tensor_copy(row_stage[:, half, ch * PER:(ch + 1) * PER, 0:6],
                                               edge[:, ds(ch * chain_len + k * PER, PER), :])
                    last.then_inc(s_rows, 1)
                    assert st.n == STEPS_C

        @block.tensor
        def _(pe):
            pe.sem_inc(s_pe_done, 2)
            with pe.Fori(0, LOOP) as i:
                for half in range(2):
                    k = i * 2 + half
                    pe.wait_ge(s_hot2, k + 1)

                    def add_up(j, step, matrix):
                        for ch in (2 * j, 2 * j + 1):
                            q = ch * PER + step
                            last = pe.matmul(acc[:, ch, 0:BOTH], matrix[0:EP, :], hot[:, half, q, :],
                                             start=False, stop=True, skip_group_check=True)
                        return last

                    for j in range(2):
                        add_up(j, 0, g.before).then_inc(s_before[j], 1)
                    for step in range(PER):
                        for j in range(2):
                            pe.wait_ge(s_read[j], k * PER + step + 1)
                            last = add_up(j, step, g.from_on)
                            if step + 1 < PER:
                                add_up(j, step + 1, g.before).then_inc(s_before[j], 1)
                    last.then_inc(s_pe_done, 1)

        @block.gpsimd
        def _(pool):
            with pool.Fori(0, LOOP) as i:
                for half in range(2):
                    pool.wait_ge(s_rows, i * 2 + half + 1)
                    pool.sem_inc(s_tick, 1)
                    for q in range(CH):
                        pool.indirect_dma_start(
                            g.edges_b, bass.IndirectOffsetOnAxis(idx_stage[:, half, q:q + 1], 0),
                            row_stage[:, half, q, :], None,
                            bounds_check=P * NT - 1, oob_is_err=False).then_inc(s_sent[half], 16)
            for half in range(2):
                pool.wait_ge(s_sent[half], LOOP * CH * 16)


def bucket_starts(dve, st, tab, tot, start, cum, n):
    count = tab.hit[:, 0:n]
    st.do(dve.tensor_tensor(count, tot[:, 0, :], tot[:, 1, :], ALU.add))
    for ch in range(2, CHAINS):
        st.do(dve.tensor_tensor(count, count, tot[:, ch, :], ALU.add))
    st.do(dve.tensor_scalar(tab.t_i[:, 0:n], count, float(P - 1), None, ALU.add))
    st.do(dve.tensor_scalar(tab.t_i[:, 0:n], tab.t_i[:, 0:n], 7, None, ALU.logical_shift_right))
    st.do(dve.tensor_copy(count, tab.t_i[:, 0:n]))
    st.do(dve.tensor_tensor_scan(cum[:, :], tab.ones[:, 0:n], count, 0.0, ALU.mult, ALU.add))
    st.do(dve.tensor_tensor(start[:, 0, :], cum[:, :], count, ALU.subtract))
    st.do(dve.tensor_scalar(start[:, 0, :], start[:, 0, :], float(P), None, ALU.mult))
    for ch in range(1, CHAINS):
        st.do(dve.tensor_tensor(start[:, ch, :], start[:, ch - 1, :], tot[:, ch - 1, :], ALU.add))


def cell_table(dve, st, g, tab, cum, count, count_i):
    for q in range(NQC):
        st.do(dve.tensor_scalar(tab.hit[:, 0:NCELL], cum[:, :], g.nodecol[:, q:q + 1], None,
                                ALU.is_le, ALU.add, accum_out=count[:, q:q + 1]))
    st.do(dve.tensor_scalar(count[:, :], count[:, :], float(NCELL - 1), None, ALU.min))
    hi = tab.t_i[:, 0:NQC]
    st.do(dve.tensor_copy(count_i[:, :], count[:, :]))
    st.do(dve.tensor_scalar(hi, count_i[:, :], 2, None, ALU.logical_shift_right))
    st.do(dve.tensor_tensor(count[:, :], count[:, :], hi, ALU.add))
    st.do(dve.tensor_scalar(hi, count_i[:, :], 4, None, ALU.logical_shift_right))
    st.do(dve.scalar_tensor_tensor(count_i[:, :], hi, 5.0, count[:, :], ALU.mult, ALU.add))



def elu_nodes(dve, st, z, e, exp):
    st.do(dve.tensor_scalar(e, z, 0.0, None, ALU.min))
    exp()
    st.do(dve.tensor_scalar(e, e, -1.0, None, ALU.add))
    st.do(dve.scalar_tensor_tensor(z, z, 0.0, e, ALU.max, ALU.add))


def degree_and_first_conv(g, c, stn1_w, stn1_b):
    nc, sem = g.nc, g.sem
    sb = lambda n, s, d=F32: g.sb(n, s, d, c)
    KB = K3 + 1
    sums = sb("basis_sums", [KB, NBLK * P])
    w1x = sb("w1x", [KB, H + 1])
    b1v = sb("b1v", [P, H])
    loop_bufs = ExitStack()
    sbl = lambda n, s, d=F32: g.sb(n, s, d, loop_bufs)
    hot = sbl("src_hot", [P, CH, SRC_SB])
    basis = sbl("basis", [P, 2, CH, KB])
    coord = sbl("coord", [P, CH, 3])
    ramp, hats = sbl("ramp", [P, CH * 3, KS + 1]), sbl("hats", [P, CH * 3, KS])
    outer = sbl("outer", [P, CH, KS * KS])
    rows16 = sbl("rows16", [P, 2, P], F16)
    s_pool_turns = sem("s_pool_turns_d")
    s_edges, s_w, s_dve, s_pool = sem("s_edges"), sem("s_w1"), sem("s_dve_d"), sem("s_pool_d")
    s_tr, s_tr16, s_rows_out = sem("s_transposed"), sem("s_rows16"), sem("s_rows_out")
    s_hot, s_basis, s_prod, s_added = sem("s_src_hot"), sem("s_basis"), sem("s_basis_prod"), sem("s_basis_added")
    LOOP = NCHK_B // 2
    QUART = CH // 4
    with ExitStack() as c_ps:
        ptr = c_ps.enter_context(nc.psum_tensor("ptr", [P, 2, 512], F32))
        pprod = c_ps.enter_context(nc.psum_tensor("pprod", [P, 4, 512], F32))
        with nc.Block() as block:
            @block.sync
            def _(sp):
                sp.dma_start(g.edges[:, :, :], g.edges_b.rearrange("(p t) w -> p t w", p=P)).then_inc(s_edges, 16)
                sp.dma_start(w1x[0:K3, 0:H], stn1_w.rearrange("k o f -> k (o f)")).then_inc(s_w, 16)
                sp.dma_start(b1v[:, :], stn1_b.rearrange("(o f) -> o f", o=1).to_broadcast([P, H])).then_inc(s_w, 16)
                for m in range(2 * NQ):
                    q, kind = m // 2, m % 2
                    n = min(P, NT - q * P)
                    sp.wait_ge(s_tr16, m + 1)
                    sp.dma_start(g.local_rows[kind, q * P:q * P + n, :], rows16[0:n, m % 2, :]).then_inc(s_rows_out, 16)
                    sp.wait_ge(s_rows_out, (m + 1) * 16)
                sp.wait_ge(s_w, 32)

            @block.scalar
            def _(act):
                for m in range(2 * NQ):
                    n = min(P, NT - m // 2 * P)
                    act.wait_ge(s_tr, m + 1)
                    if m >= 2:
                        act.wait_ge(s_rows_out, (m - 1) * 16)
                    act.activation(rows16[0:n, m % 2, :], ptr[0:n, m % 2, 0:P], ACT.Copy).then_inc(s_tr16, 1)

            @block.gpsimd
            def _(pool):
                st = Steps(pool, s_pool)
                st.add(pool.memset(ramp[:, :, 0:1], 1.0))
                st.add(pool.memset(ramp[:, :, KS:KS + 1], 0.0))
                st.do(pool.memset(basis[:, :, :, K3:KB], 1.0))
                pool.wait_ge(s_edges, 16)
                BASE, S = 3, 10
                assert st.n == BASE

                with pool.Fori(0, LOOP) as i:
                    for half in range(2):
                        k = i * 2 + half
                        st = Steps(pool, s_pool, i * (2 * S) + half * S + BASE, s_pool_turns)
                        st.do(pool.tensor_copy(coord[:, :, :], g.edges[:, ds(k * CH, CH), 2:5]))
                        p1 = coord[:, :, :].rearrange("p t d -> p (t d)")
                        st.add(pool.tensor_scalar(ramp[:, :, 1], p1, float(KS - 1), 1.0, ALU.mult, ALU.min))
                        for n in (2, 3, 4):
                            st.add(pool.tensor_scalar(ramp[:, :, n], p1, float(KS - 1), 1.0 - n, ALU.mult, ALU.add))
                        st.wait()
                        for n in (2, 3):
                            st.add(pool.tensor_scalar(ramp[:, :, n], ramp[:, :, n], 1.0, 0.0, ALU.min, ALU.max))
                        st.do(pool.tensor_scalar(ramp[:, :, 4], ramp[:, :, 4], 0.0, None, ALU.max))
                        hat = hats[:, :, :].rearrange("p (t d) k -> p t d k", d=3)
                        st.do(pool.tensor_tensor(hats[:, :, :], ramp[:, :, 0:KS], ramp[:, :, 1:KS + 1], ALU.subtract))
                        st.do(pool.tensor_tensor(
                            outer[:, :, :].rearrange("p t (a b) -> p t a b", a=KS),
                            hat[:, :, 0, :].unsqueeze(3).to_broadcast([P, CH, KS, KS]),
                            hat[:, :, 1, :].unsqueeze(2).to_broadcast([P, CH, KS, KS]), ALU.mult))
                        pool.wait_ge(s_added, i * (2 * CH) + half * CH)
                        pool.tensor_tensor(
                            basis[:, half, :, 0:K3].rearrange("p t (a b) -> p t a b", b=KS),
                            outer[:, :, :].unsqueeze(3).to_broadcast([P, CH, KS * KS, KS]),
                            hat[:, :, 2, :].unsqueeze(2).to_broadcast([P, CH, KS * KS, KS]),
                            ALU.mult).then_inc(s_basis, 1)
                        pool.wait_ge(s_basis, k + 1)
                        assert st.n == S

            @block.vector
            def _(dve):
                st = Steps(dve, s_dve)
                st.do(dve.memset(sums[:, :], 0.0))
                dve.wait_ge(s_edges, 16)
                dve.sem_inc(s_added, 4)
                with dve.Fori(0, LOOP) as i:
                    for half in range(2):
                        k = i * 2 + half
                        for q in range(CH):
                            last = dve.tensor_scalar(hot[:, q, :], g.iotaf[:, 0:SRC_SB],
                                                     g.edges[:, ds(k * CH + q, 1), 0:1].rearrange("p a b -> p (a b)"), None, ALU.is_equal)
                            if q % QUART == QUART - 1:
                                last.then_inc(s_hot, 1)
                        src_sb = load_values(nc, DVE, g.table_b[0:1, 0, ds(k * CH, CH)], NA - 1)
                        for q in range(CH):
                            n = k * CH + q
                            a = src_sb[q]
                            dve.wait_ge(s_prod, n + 1)
                            dve.wait_ge(s_added, n + 4)
                            part = sums[:, ds(a * SRC_SB, SRC_SB)]
                            dve.tensor_tensor(part, part, pprod[0:KB, q % 4, 0:SRC_SB], ALU.add).then_inc(s_added, 1)

            @block.tensor
            def _(pe):
                pe.wait_ge(s_edges, 16)
                for m in range(2 * NQ):
                    q, kind = m // 2, m % 2
                    n = min(P, NT - q * P)
                    if m >= 2:
                        pe.wait_ge(s_tr16, m - 1)
                    pe.transpose(ptr[0:n, m % 2, 0:P], g.edges[:, q * P:q * P + n, kind], g.ident[:, :]).then_inc(s_tr, 1)
                with pe.Fori(0, LOOP) as i:
                    for half in range(2):
                        k = i * 2 + half
                        pe.wait_ge(s_basis, k + 1)
                        for q in range(CH):
                            if q % QUART == 0:
                                pe.wait_ge(s_hot, k * 4 + q // QUART + 1)
                            pe.wait_ge(s_added, k * CH + q + 1)
                            pe.matmul(pprod[0:KB, q % 4, 0:SRC_SB], basis[:, half, q, :], hot[:, q, :],
                                      start=True, stop=True).then_inc(s_prod, 1)

    loop_bufs.close()
    z = sb("z1", [P, NBLK, H + 1])
    e1 = sb("e1", [P, NBLK, H])
    w1d = sb("w1d", [KB, H + 1])
    s_dve2, s_w1x, s_node, s_min, s_exp = sem("s_dve_e"), sem("s_w1x"), sem("s_node1"), sem("s_min1"), sem("s_exp1")
    BANK_BLKS = 512 // (H + 1)
    with ExitStack() as c_ps:
        pn = c_ps.enter_context(nc.psum_tensor("pn1", [P, 8, 512], F32))
        with nc.Block() as block:
            @block.vector
            def _(dve):
                st = Steps(dve, s_dve2)
                st.do(dve.memset(w1d[:, :], 0.0))
                st.add(dve.tensor_copy(w1d[0:K3, 0:H], w1x[0:K3, 0:H]))
                st.do(dve.tensor_scalar(w1d[:, H:H + 1], g.nodecol[0:KB, 0:1], float(K3), None, ALU.is_equal))
                dve.sem_inc(s_w1x, 1)
                dve.wait_ge(s_node, 1)
                for b0 in range(0, NBLK, BANK_BLKS):
                    n = min(BANK_BLKS, NBLK - b0)
                    st.do(dve.tensor_copy(z[:, b0:b0 + n, :],
                                          pn[:, b0 // BANK_BLKS, 0:n * (H + 1)].rearrange("p (b f) -> p b f", f=H + 1)))
                st.do(dve.tensor_scalar(g.rdeg[:, :], z[:, :, H], 1.0, None, ALU.max))
                st.do(dve.reciprocal(g.rdeg[:, :], g.rdeg[:, :]))
                zz = z[:, :, 0:H]
                st.do(dve.tensor_tensor(zz, zz, g.rdeg[:, :].unsqueeze(2).to_broadcast([P, NBLK, H]), ALU.mult))
                st.do(dve.tensor_tensor(zz, zz, b1v[:, :].unsqueeze(1).to_broadcast([P, NBLK, H]), ALU.add))

                def exp():
                    dve.sem_inc(s_min, 1)
                    dve.wait_ge(s_exp, 1)
                elu_nodes(dve, st, zz, e1[:, :, :], exp)
                split_parts(dve, st, [g.h1parts[:, :, k, :] for k in range(3)], zz, e1[:, :, :])

            @block.scalar
            def _(act):
                act.wait_ge(s_min, 1)
                act.activation(e1[:, :, :], e1[:, :, :], ACT.Exp).then_inc(s_exp, 1)

            @block.tensor
            def _(pe):
                pe.wait_ge(s_w1x, 1)
                for b in range(NBLK):
                    at = b % BANK_BLKS * (H + 1)
                    last = pe.matmul(pn[:, b // BANK_BLKS, at:at + H + 1], sums[:, b * P:(b + 1) * P],
                                     w1d[:, :], start=True, stop=True)
                last.then_inc(s_node, 1)


def to_cells_1(g, c):
    nc, sem = g.nc, g.sem
    sb = lambda n, s, d=F32: g.sb(n, s, d, c)
    NJ = DST_SB // P
    rows = sb("dst_rows", [P, 2, CH * P], F16)
    hot = sb("dst_hot", [P, 2, NJ, CH * P], BF16)
    stage = sb("c1_stage", [P, 2, CH, C1_W])
    idx = sb("c1_idx", [P, 2, CH], U32)
    pos, base = sb("c1_pos", [P, CH, 3]), sb("c1_base", [P, CH, 3])
    s_row, s_row_free = [sem(f"s_dst_rows{h}") for h in range(2)], sem("s_dst_rows_free")
    s_hot, s_gat, s_out = sem("s_dst_hot"), sem("s_gathered"), sem("s_gathered_out")
    s_rest, s_sent = sem("s_c1_rest"), [sem(f"s_c1_sent{h}") for h in range(2)]
    s_dve, s_tick = sem("s_dve_f"), sem("s_pool_turns_f")
    LOOP = NCHK_B // 2
    pg = c.enter_context(nc.psum_tensor("pg1", [P, 2, CH, H], F32))
    with nc.Block() as block:
        @block.sync
        def _(sp):
            with sp.Fori(0, LOOP) as i:
                for half in range(2):
                    k = i * 2 + half
                    sp.wait_ge(s_row_free, k + 1)
                    sp.dma_start(rows[:, half, :],
                                 g.local_rows[1:2, ds(k * CH, CH), :].rearrange("o t e -> o (t e)")
                                 .to_broadcast([P, CH * P])).then_inc(s_row[half], 16)

        @block.vector
        def _(dve):
            dve.sem_inc(s_row_free, 2)
            S = 5
            with dve.Fori(0, LOOP) as i:
                for half in range(2):
                    k = i * 2 + half
                    st = Steps(dve, s_dve, i * (2 * S) + half * S)
                    dve.wait_ge(s_row[half], i * 16 + 16)
                    dve.wait_ge(s_gat, k + 1)
                    for j in range(NJ):
                        last = dve.tensor_scalar(hot[:, half, j, :], rows[:, half, :], g.nodecol[:, j:j + 1],
                                                 None, ALU.is_equal)
                    last.then_inc(s_hot, 1)
                    dve.wait_ge(s_hot, k + 1)
                    dve.sem_inc(s_row_free, 1)
                    st.do(dve.tensor_scalar(pos[:, :, :], g.edges[:, ds(k * CH, CH), 2:5], float(KS - 1), None, ALU.mult))
                    st.do(dve.tensor_scalar(base[:, :, :], pos[:, :, :], 1.0, None, ALU.is_ge))
                    for knot in (2.0, 3.0):
                        st.do(dve.scalar_tensor_tensor(base[:, :, :], pos[:, :, :], knot, base[:, :, :],
                                                       ALU.is_ge, ALU.add))
                    dve.wait_ge(s_sent[half], i * CH * 16)
                    st.do(dve.tensor_tensor(stage[:, half, :, H:H + 3], pos[:, :, :], base[:, :, :], ALU.subtract))
                    dve.tensor_copy(stage[:, half, :, H + 3], g.edges[:, ds(k * CH, CH), 7])
                    dve.tensor_copy(idx[:, half, :], g.edges[:, ds(k * CH, CH), 6]).then_inc(s_rest, 1)
                    assert st.n == S

        @block.tensor
        def _(pe):
            pe.sem_inc(s_gat, 2)
            with pe.Fori(0, LOOP) as i:
                for half in range(2):
                    k = i * 2 + half
                    pe.wait_ge(s_hot, k + 1)
                    pe.wait_ge(s_out, k + 1)
                    dst_sb = load_values(nc, PE, g.table_b[0:1, 1, ds(k * CH, CH)], ND - 1)
                    for q in range(CH):
                        d = dst_sb[q]
                        for j in range(NJ):
                            for part in range(3):
                                last = pe.matmul(pg[:, half, q, :], hot[:, half, j, q * P:(q + 1) * P],
                                                 g.h1parts[:, ds(d * NJ + j, 1), part, :].rearrange("p a f -> p (a f)"),
                                                 start=(j == 0 and part == 0), stop=(j == NJ - 1 and part == 2))
                    last.then_inc(s_gat, 1)

        @block.scalar
        def _(act):
            act.sem_inc(s_out, 2)
            with act.Fori(0, LOOP) as i:
                for half in range(2):
                    k = i * 2 + half
                    act.wait_ge(s_gat, k + 3)
                    act.wait_ge(s_sent[half], i * CH * 16)
                    act.activation(stage[:, half, :, 0:H], pg[:, half, :, :], ACT.Copy).then_inc(s_out, 1)

        @block.gpsimd
        def _(pool):
            with pool.Fori(0, LOOP) as i:
                for half in range(2):
                    k = i * 2 + half
                    pool.wait_ge(s_rest, k + 1)
                    pool.wait_ge(s_out, k + 3)
                    pool.sem_inc(s_tick, 1)
                    for q in range(CH):
                        pool.indirect_dma_start(g.rows_c1, bass.IndirectOffsetOnAxis(idx[:, half, q:q + 1], 0),
                                                stage[:, half, q, :], None, bounds_check=P * NTC - 1,
                                                oob_is_err=False).then_inc(s_sent[half], 16)
            for half in range(2):
                pool.wait_ge(s_sent[half], LOOP * CH * 16)


def cell_products(g, c, tag, rows_dram, tab_dram, msg_dram, w_dram, width):
    nc, sem = g.nc, g.sem
    sb = lambda n, s, d=F32: g.sb(f"{tag}x_{n}", s, d, c)
    sm = lambda n: sem(f"s_{tag}x_{n}")
    shifts = [0, 1] if width == H else [0, 1, KS, KS + 1]
    pieces = [0, KS, KS * KS, KS * KS + KS] if width == H else [0, KS * KS]
    NP = len(pieces)
    KN = K3 - shifts[-1]
    W = width + 4
    weights = sb("weights", [P, KN, width])
    rows = sb("rows", [P, 2, CH, W])
    two = sb("two", [P, CH, 3, 2])
    four, eight = sb("four", [P, CH, 4]), sb("eight", [P, CH, 8])
    GR = 4
    scaled = sb("scaled", [P, 2, GR, 8, width])
    turned = sb("turned", [P, 4, NP * P])
    stage = sb("stage", [P, 2, CH, width])
    idx = sb("idx", [P, 2, CH], U32)
    s_w, s_rows, s_rows_free = sm("w"), [sm(f"rows{h}") for h in range(2)], sm("rows_free")
    s_scaled, s_tr, s_turned, s_mm = sm("scaled"), sm("transposed"), sm("turned"), sm("products")
    s_msg, s_idx, s_sent, s_dve, s_tick = sm("msg"), sm("idx"), [sm(f"sent{h}") for h in range(2)], sm("dve"), sm("turns")
    LOOP = NCHK_C // 2
    pt = c.enter_context(nc.psum_tensor(f"{tag}_pt", [P, 4, 512], F32))
    pm = c.enter_context(nc.psum_tensor(f"{tag}_pm", [P, 2, CH, width], F32))
    with nc.Block() as block:
        @block.sync
        def _(sp):
            sp.dma_start(g.table_c[:, :], tab_dram).then_inc(s_w, 16)
            for n, shift in enumerate(shifts):
                sp.dma_start(weights[n * width:(n + 1) * width, :, :],
                             w_dram[shift:shift + KN, :, :].rearrange("k i o -> i k o")).then_inc(s_w, 16)
            view = rows_dram.rearrange("(p t) w -> p t w", p=P)
            with sp.Fori(0, LOOP) as i:
                for half in range(2):
                    k = i * 2 + half
                    sp.wait_ge(s_rows_free, k + 1)
                    sp.dma_start(rows[:, half, :, :], view[:, ds(k * CH, CH), :]).then_inc(s_rows[half], 16)

        @block.vector
        def _(dve):
            dve.sem_inc(s_rows_free, 2)
            S = 4
            with dve.Fori(0, LOOP) as i:
                for half in range(2):
                    k = i * 2 + half
                    st = Steps(dve, s_dve, i * (2 * S) + half * S)
                    dve.wait_ge(s_rows[half], i * 16 + 16)
                    frac = rows[:, half, :, width:width + 3]
                    st.add(dve.tensor_scalar(two[:, :, :, 0], frac, -1.0, 1.0, ALU.mult, ALU.add))
                    st.do(dve.tensor_copy(two[:, :, :, 1], frac))
                    st.do(dve.tensor_tensor(four[:, :, :].rearrange("p t (a b) -> p t a b", a=2),
                                            two[:, :, 0, :].unsqueeze(3).to_broadcast([P, CH, 2, 2]),
                                            two[:, :, 1, :].unsqueeze(2).to_broadcast([P, CH, 2, 2]), ALU.mult))
                    st.do(dve.tensor_tensor(eight[:, :, :].rearrange("p t (a b) -> p t a b", a=4),
                                            four[:, :, :].unsqueeze(3).to_broadcast([P, CH, 4, 2]),
                                            two[:, :, 2, :].unsqueeze(2).to_broadcast([P, CH, 4, 2]), ALU.mult))
                    dve.wait_ge(s_sent[half], i * CH * 16)
                    dve.tensor_copy(idx[:, half, :], rows[:, half, :, width + 3]).then_inc(s_idx, 1)
                    for gr in range(CH // GR):
                        dve.wait_ge(s_tr, k * CH + gr * GR)
                        at = slice(gr * GR, (gr + 1) * GR)
                        last = dve.tensor_tensor(scaled[:, gr % 2, :, :, :],
                                                 rows[:, half, at, 0:width].unsqueeze(2).to_broadcast([P, GR, 8, width]),
                                                 eight[:, at, :].unsqueeze(3).to_broadcast([P, GR, 8, width]), ALU.mult)
                        last.then_inc(s_scaled, 1)
                    dve.wait_ge(s_scaled, (k + 1) * (CH // GR))
                    dve.sem_inc(s_rows_free, 1)
                    assert st.n == S

        @block.tensor
        def _(pe):
            pe.wait_ge(s_w, 16 * (len(shifts) + 1))
            pe.sem_inc(s_tr, GR)
            pe.sem_inc(s_mm, 4)
            with pe.Fori(0, LOOP) as i:
                for half in range(2):
                    k = i * 2 + half
                    pe.wait_ge(s_msg, k + 1)
                    bases = load_values(nc, PE, g.table_c[0:1, ds(k * CH, CH)], KN - 1 - pieces[-1])

                    def transposes(q):
                        if q % GR == 0:
                            pe.wait_ge(s_scaled, k * (CH // GR) + q // GR + 1)
                        flat = scaled[:, q // GR % 2, q % GR, :, :].rearrange("p s f -> p (s f)")
                        for n in range(NP):
                            last = pe.transpose(pt[:, q % 4, n * P:(n + 1) * P], flat[:, n * P:(n + 1) * P],
                                                g.ident[:, :])
                        last.then_inc(s_tr, 1)

                    def products(q):
                        base = bases[q]
                        pe.wait_ge(s_turned, k * CH + q + 1)
                        for n, piece in enumerate(pieces):
                            last = pe.matmul(pm[:, half, q, :], turned[:, q % 4, n * P:(n + 1) * P],
                                             weights[:, ds(base + piece, 1), :].rearrange("p a f -> p (a f)"),
                                             start=(n == 0), stop=(n == NP - 1))
                        last.then_inc(s_mm, 1)

                    for q in range(CH):
                        transposes(q)
                        if q:
                            products(q - 1)
                    products(CH - 1)

        @block.scalar
        def _(act):
            act.sem_inc(s_msg, 2)
            with act.Fori(0, LOOP) as i:
                for half in range(2):
                    k = i * 2 + half
                    for q in range(CH):
                        act.wait_ge(s_tr, k * CH + q + 1 + GR)
                        act.wait_ge(s_mm, k * CH + q + 1)
                        act.activation(turned[:, q % 4, :], pt[:, q % 4, 0:NP * P], ACT.Copy).then_inc(s_turned, 1)
                    act.wait_ge(s_mm, k * CH + CH + 4)
                    act.wait_ge(s_sent[half], i * CH * 16)
                    act.activation(stage[:, half, :, :], pm[:, half, :, :], ACT.Copy).then_inc(s_msg, 1)

        @block.gpsimd
        def _(pool):
            with pool.Fori(0, LOOP) as i:
                for half in range(2):
                    k = i * 2 + half
                    pool.wait_ge(s_idx, k + 1)
                    pool.wait_ge(s_msg, k + 3)
                    pool.sem_inc(s_tick, 1)
                    for q in range(CH):
                        pool.indirect_dma_start(msg_dram, bass.IndirectOffsetOnAxis(idx[:, half, q:q + 1], 0),
                                                stage[:, half, q, :], None, bounds_check=P * NT - 1,
                                                oob_is_err=False).then_inc(s_sent[half], 16)
            for half in range(2):
                pool.wait_ge(s_sent[half], LOOP * CH * 16)


def add_up_by_source(g, c, tag, msg_dram, width, acc):
    nc, sem = g.nc, g.sem
    sb = lambda n, s, d=F32: g.sb(f"{tag}x_{n}", s, d, c)
    sm = lambda n: sem(f"s_{tag}x_{n}")
    msg = sb("msg", [P, 2, CH, width])
    hot = sb("hot", [P, 2, CH, SRC_SB])
    s_in, s_hot, s_used = [sm(f"in{h}") for h in range(2)], sm("hot"), sm("used")
    LOOP = NCHK_B // 2
    NJ = SRC_SB // P
    with nc.Block() as block:
        @block.sync
        def _(sp):
            view = msg_dram.rearrange("(p t) w -> p t w", p=P)
            with sp.Fori(0, LOOP) as i:
                for half in range(2):
                    k = i * 2 + half
                    sp.wait_ge(s_used, k + 1)
                    sp.dma_start(msg[:, half, :, :], view[:, ds(k * CH, CH), :]).then_inc(s_in[half], 16)

        @block.vector
        def _(dve):
            with dve.Fori(0, LOOP) as i:
                for half in range(2):
                    k = i * 2 + half
                    dve.wait_ge(s_used, k + 1)
                    for q in range(CH):
                        last = dve.tensor_scalar(hot[:, half, q, :], g.iotaf[:, 0:SRC_SB],
                                                 g.edges[:, ds(k * CH + q, 1), 0:1].rearrange("p a b -> p (a b)"),
                                                 None, ALU.is_equal)
                        if q % 4 == 3:
                            last.then_inc(s_hot, 1)

        @block.tensor
        def _(pe):
            for b0 in range(0, NBLK * width, 512):
                n = min(512, NBLK * width - b0)
                pe.matmul(acc[:, b0:b0 + n], g.ident[:, :], g.zero512[:, 0:n], start=True, stop=True)
            pe.sem_inc(s_used, 2)
            with pe.Fori(0, LOOP) as i:
                for half in range(2):
                    k = i * 2 + half
                    pe.wait_ge(s_in[half], i * 16 + 16)
                    src_sb = load_values(nc, PE, g.table_b[0:1, 0, ds(k * CH, CH)], NA - 1)
                    for q in range(CH):
                        if q % 4 == 0:
                            pe.wait_ge(s_hot, k * 4 + q // 4 + 1)
                        a = src_sb[q]
                        for j in range(NJ):
                            last = pe.matmul(acc[:, ds((a * NJ + j) * width, width)],
                                             hot[:, half, q, j * P:(j + 1) * P], msg[:, half, q, :],
                                             start=False, stop=True, skip_group_check=True)
                    last.then_inc(s_used, 1)


def shift_network(g, c, stn2_b, stn3_w, stn3_b, stn4_w, stn4_b):
    nc, sem = g.nc, g.sem
    sb = lambda n, s, d=F32: g.sb(n, s, d, c)
    ph = sb("h2", [P, NBLK, H])
    with ExitStack() as c1:
        acc = c1.enter_context(nc.psum_tensor("acc_h2", [P, 7 * 512], F32))
        with ExitStack() as c2:
            add_up_by_source(g, c2, "r1", g.msg1, H, acc)
        e2, b2v = g.sb("e2", [P, NBLK, H], F32, c1), g.sb("b2v", [P, H], F32, c1)
        s_b, s_dve, s_min, s_exp = sem("s_b2"), sem("s_dve_g"), sem("s_min2"), sem("s_exp2")
        with nc.Block() as block:
            @block.sync
            def _(sp):
                sp.dma_start(b2v[:, :], stn2_b.rearrange("(o f) -> o f", o=1).to_broadcast([P, H])).then_inc(s_b, 16)

            @block.vector
            def _(dve):
                st = Steps(dve, s_dve)
                dve.wait_ge(s_b, 16)
                z = ph[:, :, :]
                st.do(dve.tensor_tensor(z, acc[:, 0:NBLK * H].rearrange("p (b f) -> p b f", f=H),
                                        g.rdeg[:, :].unsqueeze(2).to_broadcast([P, NBLK, H]), ALU.mult))
                st.do(dve.tensor_tensor(z, z, b2v[:, :].unsqueeze(1).to_broadcast([P, NBLK, H]), ALU.add))

                def exp():
                    dve.sem_inc(s_min, 1)
                    dve.wait_ge(s_exp, 1)
                elu_nodes(dve, st, z, e2[:, :, :], exp)

            @block.scalar
            def _(act):
                act.wait_ge(s_min, 1)
                act.activation(e2[:, :, :], e2[:, :, :], ACT.Exp).then_inc(s_exp, 1)

    NG = NBLK // 4
    hT, h3 = sb("h2T", [H, NBLK * P]), sb("h3", [H, NBLK * P])
    e3 = hT
    w3, b3, w4, b4 = sb("w3", [H, H]), sb("b3", [H, 1]), sb("w4", [H, 3]), sb("b4", [P, 3])
    t = sb("t", [P, NBLK, 3])
    rest = sb("t_rest", [P, NBLK, 3])
    s_w, s_tr, s_hT, s_d3, s_h3 = sem("s_w34"), sem("s_tr2"), sem("s_hT"), sem("s_dense3"), sem("s_h3pre")
    s_dve, s_min, s_exp, s_elu, s_t = sem("s_dve_h"), sem("s_min3"), sem("s_exp3"), sem("s_elu3"), sem("s_t")
    with ExitStack() as c1:
        pt = c1.enter_context(nc.psum_tensor("pt2", [P, 2, 512], F32))
        pd = c1.enter_context(nc.psum_tensor("pd2", [P, 2, 512], F32))
        pf = c1.enter_context(nc.psum_tensor("pf2", [P, 512], F32))
        with nc.Block() as block:
            @block.sync
            def _(sp):
                with nc.allow_non_contiguous_dma(reason="a bias column"):
                    sp.dma_start(b3[:, :], stn3_b.rearrange("(f o) -> f o", o=1)).then_inc(s_w, 16)
                sp.dma_start(w3[:, :], stn3_w).then_inc(s_w, 16)
                sp.dma_start(w4[:, :], stn4_w).then_inc(s_w, 16)
                sp.dma_start(b4[:, :], stn4_b.rearrange("(o f) -> o f", o=1).to_broadcast([P, 3])).then_inc(s_w, 16)

            @block.tensor
            def _(pe):
                pe.wait_ge(s_w, 64)

                def dense(n):
                    pe.wait_ge(s_hT, n + 1)
                    if n >= 2:
                        pe.wait_ge(s_h3, n - 1)
                    pe.matmul(pd[0:H, n % 2, :], w3[:, :], hT[:, n * 512:(n + 1) * 512], start=True,
                              stop=True).then_inc(s_d3, 1)
                for n in range(NG):
                    if n >= 2:
                        pe.wait_ge(s_hT, n - 1)
                    for b in range(4):
                        last = pe.transpose(pt[0:H, n % 2, b * P:(b + 1) * P], ph[:, n * 4 + b, :], g.ident[:, :])
                    last.then_inc(s_tr, 1)
                    if n:
                        dense(n - 1)
                dense(NG - 1)
                pe.wait_ge(s_elu, 1)
                for b in range(NBLK):
                    last = pe.matmul(pf[:, b * 3:(b + 1) * 3], h3[:, b * P:(b + 1) * P], w4[:, :], start=True, stop=True)
                last.then_inc(s_t, 1)

            @block.scalar
            def _(act):
                act.wait_ge(s_w, 64)
                for n in range(NG):
                    act.wait_ge(s_tr, n + 1)
                    act.activation(hT[:, n * 512:(n + 1) * 512], pt[0:H, n % 2, :], ACT.Copy).then_inc(s_hT, 1)
                    if n:
                        act.wait_ge(s_d3, n)
                        act.activation(h3[:, (n - 1) * 512:n * 512], pd[0:H, (n - 1) % 2, :], ACT.Identity,
                                       bias=b3[:, :]).then_inc(s_h3, 1)
                act.wait_ge(s_d3, NG)
                act.activation(h3[:, (NG - 1) * 512:NG * 512], pd[0:H, (NG - 1) % 2, :], ACT.Identity,
                               bias=b3[:, :]).then_inc(s_h3, 1)
                act.wait_ge(s_min, 1)
                act.activation(e3[:, :], e3[:, :], ACT.Exp).then_inc(s_exp, 1)

            @block.vector
            def _(dve):
                st = Steps(dve, s_dve)
                dve.wait_ge(s_w, 64)
                dve.wait_ge(s_h3, NG)

                def exp():
                    dve.sem_inc(s_min, 1)
                    dve.wait_ge(s_exp, 1)
                elu_nodes(dve, st, h3[:, :], e3[:, :], exp)
                dve.sem_inc(s_elu, 1)
                dve.wait_ge(s_t, 1)
                st.do(dve.tensor_tensor(t[:, :, :], pf[:, 0:NBLK * 3].rearrange("p (b f) -> p b f", f=3),
                                        b4[:, :].unsqueeze(1).to_broadcast([P, NBLK, 3]), ALU.add))
                split_parts(dve, st, [g.tparts[:, :, k, :] for k in range(3)], t[:, :, :], rest[:, :, :])
                st.do(dve.tensor_scalar(g.tparts_neg[:, :, :, :], g.tparts[:, :, :, :], -1.0, None, ALU.mult))


def to_cells_2(g, c):
    nc, sem = g.nc, g.sem
    sb = lambda n, s, d=F32: g.sb(n, s, d, c)
    NJD, NJS = DST_SB // P, SRC_SB // P
    CHAIN = NT // CHAINS
    LOOP = NCHK_B // 2
    rows = sb("both_rows", [P, 2, 2, CH * P], F16)
    hot_d = sb("hot_d", [P, NJD, CH * P], BF16)
    hot_s = sb("hot_s", [P, NJS, CH * P], BF16)
    frac, cell = sb("frac2", [P, NT, 3]), sb("cell2", [P, NT])
    pos, base = sb("pos2", [P, CH, 3]), sb("base2", [P, CH, 3])
    real, cl = sb("real", [P, CH]), sb("cl", [P, CH])
    hot_c = sb("hot_c2", [P, 2, CH, NCELL], F16)
    by_chain = g.edges[:, :, :].rearrange("p (c t) w -> p c t w", c=CHAINS)

    def chain_tiles(view, k):
        return view[:, :, ds(k * PER, PER)]

    def load_rows(sp, k, half, s_row, kinds):
        for kind in kinds:
            sp.dma_start(rows[:, half, kind, :].rearrange("p (c n) -> p c n", c=CHAINS),
                         g.local_rows[kind:kind + 1, 0:NT, :].rearrange("o (c t) e -> o c (t e)", c=CHAINS)
                         [:, :, ds(k * (PER * P), PER * P)].to_broadcast([P, CHAINS, PER * P])).then_inc(s_row, 16)

    s_row, s_row_free = [sem(f"s_both_rows{h}") for h in range(2)], sem("s_both_rows_free")
    s_hot, s_gat, s_sum = sem("s_hot_ds"), sem("s_shift_read"), sem("s_shift_summed")
    s_hotc, s_tot, s_dve = sem("s_hot_c2"), sem("s_tot_c2"), sem("s_dve_i")
    with ExitStack() as c1:
        pdel = c1.enter_context(nc.psum_tensor("pdel", [P, 2, 512], F32))
        pacc = c1.enter_context(nc.psum_tensor("pacc2", [P, 2, 512], F32))
        with nc.Block() as block:
            @block.sync
            def _(sp):
                with sp.Fori(0, LOOP) as i:
                    for half in range(2):
                        k = i * 2 + half
                        sp.wait_ge(s_row_free, k + 1)
                        load_rows(sp, k, half, s_row[half], (0, 1))

            @block.vector
            def _(dve):
                dve.sem_inc(s_row_free, 2)
                dve.sem_inc(s_sum, 2)
                S = 12
                with dve.Fori(0, LOOP) as i:
                    for half in range(2):
                        k = i * 2 + half
                        st = Steps(dve, s_dve, i * (2 * S) + half * S)
                        dve.wait_ge(s_row[half], i * 32 + 32)
                        dve.wait_ge(s_gat, k + 1)
                        for j in range(NJD):
                            dve.tensor_scalar(hot_d[:, j, :], rows[:, half, 1, :], g.nodecol[:, j:j + 1], None, ALU.is_equal)
                        for j in range(NJS):
                            last = dve.tensor_scalar(hot_s[:, j, :], rows[:, half, 0, :], g.nodecol[:, j:j + 1], None, ALU.is_equal)
                        last.then_inc(s_hot, 1)
                        dve.wait_ge(s_hot, k + 1)
                        dve.sem_inc(s_row_free, 1)
                        dve.wait_ge(s_gat, k + 2)
                        st.do(dve.tensor_reduce(pos[:, :, :],
                                                pdel[:, half, 0:CH * 9].rearrange("p (t k f) -> p t f k", k=3, f=3),
                                                AX, ALU.add))
                        dve.sem_inc(s_sum, 1)
                        pos4 = pos[:, :, :].rearrange("p (c t) f -> p c t f", c=CHAINS)
                        st.do(dve.tensor_tensor(pos4, pos4, by_chain[:, :, ds(k * PER, PER), 2:5], ALU.add))
                        st.do(dve.tensor_scalar(pos[:, :, :], pos[:, :, :], 0.0, 1.0, ALU.max, ALU.min))
                        st.do(dve.tensor_scalar(pos[:, :, :], pos[:, :, :], float(KS - 1), None, ALU.mult))
                        st.do(dve.tensor_scalar(base[:, :, :], pos[:, :, :], 1.0, None, ALU.is_ge))
                        for knot in (2.0, 3.0):
                            st.do(dve.scalar_tensor_tensor(base[:, :, :], pos[:, :, :], knot, base[:, :, :], ALU.is_ge, ALU.add))
                        st.add(dve.tensor_tensor(frac[:, ds(k * CH, CH), :], pos[:, :, :], base[:, :, :], ALU.subtract))
                        st.do(dve.scalar_tensor_tensor(cl[:, :], base[:, :, 0], 4.0, base[:, :, 1], ALU.mult, ALU.add))
                        st.do(dve.scalar_tensor_tensor(cl[:, :], cl[:, :], 4.0, base[:, :, 2], ALU.mult, ALU.add))
                        st.do(dve.tensor_scalar(real[:, :].rearrange("p (c t) -> p c t", c=CHAINS),
                                                by_chain[:, :, ds(k * PER, PER), 0], 0.0, None, ALU.is_lt))
                        st.do(dve.scalar_tensor_tensor(cell[:, ds(k * CH, CH)], real[:, :], -1000.0, cl[:, :], ALU.mult, ALU.add))
                        for q in range(CH):
                            last = dve.tensor_scalar(hot_c[:, half, q, :], g.iota16[:, 0:NCELL], cell[:, ds(k * CH + q, 1)], None, ALU.is_equal)
                        last.then_inc(s_hotc, 1)
                        assert st.n == S, st.n

            @block.tensor
            def _(pe):
                pe.matmul(pacc[:, 0, :], g.ident[:, :], g.zero512[:, :], start=True, stop=True)
                pe.sem_inc(s_gat, 1)
                with pe.Fori(0, LOOP) as i:
                    for half in range(2):
                        k = i * 2 + half
                        pe.wait_ge(s_hot, k + 1)
                        pe.wait_ge(s_sum, k + 1)
                        for q in range(CH):
                            if q % PER == 0:
                                tile = (q // PER) * CHAIN + k * PER
                                src_sb = load_values(nc, PE, g.table_b[0:1, 0, ds(tile, PER)], NA - 1)
                                dst_sb = load_values(nc, PE, g.table_b[0:1, 1, ds(tile, PER)], ND - 1)
                            a, d = src_sb[q % PER], dst_sb[q % PER]
                            at = pdel[:, half, q * 9:(q + 1) * 9]
                            for j in range(NJD):
                                pe.matmul(at, hot_d[:, j, q * P:(q + 1) * P],
                                          g.tparts[:, ds(d * NJD + j, 1), :, :].rearrange("p a k f -> p (a k f)"),
                                          start=(j == 0), stop=False)
                            for j in range(NJS):
                                last = pe.matmul(at, hot_s[:, j, q * P:(q + 1) * P],
                                                 g.tparts_neg[:, ds(a * NJS + j, 1), :, :].rearrange("p a k f -> p (a k f)"),
                                                 start=False, stop=(j == NJS - 1))
                        last.then_inc(s_gat, 1)
                        pe.wait_ge(s_hotc, k + 1)
                        for q in range(CH):
                            ch = q // PER
                            pe.matmul(pacc[:, 0, ch * NCELL:(ch + 1) * NCELL], g.ones16[:, :], hot_c[:, half, q, :],
                                      start=False, stop=True, skip_group_check=True)

        tot, start = sb("tot2", [P, CHAINS, NCELL]), sb("start2", [P, CHAINS, NCELL])
        cum = sb("cum2", [P, NCELL])
        tab = TableBuffers(ones=sb("ones2", [P, NCELL]), t_i=sb("t_i2", [P, NCELL], I32), hit=sb("hit2", [P, NCELL]))
        count, count_i = sb("count2", [P, NQC]), sb("count_i2", [P, NQC], I32)
        s_start, s_tabs, s_tab_out, s_dve2 = sem("s_starts2"), sem("s_tables2"), sem("s_tables2_out"), sem("s_dve_j")
        with nc.Block() as block:
            @block.vector
            def _(dve):
                st = Steps(dve, s_dve2)
                st.add(dve.memset(tab.ones[:, :], 1.0))
                st.do(dve.tensor_copy(tot[:, :, :], pacc[:, 0, 0:CHAINS * NCELL].rearrange("p (c n) -> p c n", c=CHAINS)))
                bucket_starts(dve, st, tab, tot, start, cum, NCELL)
                dve.sem_inc(s_start, 1)
                cell_table(dve, st, g, tab, cum, count, count_i)
                dve.sem_inc(s_tabs, 1)

            @block.tensor
            def _(pe):
                pe.wait_ge(s_start, 1)
                for j in range(2):
                    pe.matmul(pacc[:, j, 0:2 * NCELL], g.onesf[:, :],
                              start[0:1, 2 * j:2 * j + 2, :].rearrange("p c n -> p (c n)"), start=True, stop=True)

            @block.sync
            def _(sp):
                sp.wait_ge(s_tabs, 1)
                with nc.allow_non_contiguous_dma(reason="small table"):
                    sp.dma_start(g.tab_c2[0, :].rearrange("(q p) -> p q", p=P), count_i[:, :]).then_inc(s_tab_out, 16)
                sp.wait_ge(s_tab_out, 16)

        place = sb("place2", [P, CH])
        place_i, low_i, high_i = (sb(n, [P, CH], I32) for n in ("place_i2", "low_i2", "high_i2"))
        skip = sb("skip2", [P, CH])
        hit = sb("hit_c2", [P, CHAINS, NCELL], BF16)
        stage, idx = sb("c2_stage", [P, 2, CH, C2_W]), sb("c2_idx", [P, 2, CH], U32)
        s_row2, s_row2_free = [sem(f"s_dst_rows2{h}") for h in range(2)], sem("s_dst_rows2_free")
        s_hot2, s_gat2, s_out2 = sem("s_dst_hot2"), sem("s_gathered2"), sem("s_gathered2_out")
        s_hotc2, s_ranked = sem("s_hot_c22"), sem("s_ranked2")
        s_before, s_read = [sem(f"s_before2{j}") for j in range(2)], [sem(f"s_read2{j}") for j in range(2)]
        s_rest, s_sent = sem("s_c2_rest"), [sem(f"s_c2_sent{h}") for h in range(2)]
        s_dve3, s_tick = sem("s_dve_k"), sem("s_pool_turns_k")
        with nc.Block() as block:
            @block.sync
            def _(sp):
                with sp.Fori(0, LOOP) as i:
                    for half in range(2):
                        k = i * 2 + half
                        sp.wait_ge(s_row2_free, k + 1)
                        load_rows(sp, k, half, s_row2[half], (1,))

            @block.vector
            def _(dve):
                dve.sem_inc(s_row2_free, 2)
                S = 5
                with dve.Fori(0, LOOP) as i:
                    for half in range(2):
                        k = i * 2 + half
                        st = Steps(dve, s_dve3, i * (2 * S) + half * S)
                        dve.wait_ge(s_ranked, k + 1)
                        for q in range(CH):
                            last = dve.tensor_scalar(hot_c[:, half, q, :], g.iota16[:, 0:NCELL], cell[:, ds(k * CH + q, 1)], None, ALU.is_equal)
                        last.then_inc(s_hotc2, 1)
                        dve.wait_ge(s_row2[half], i * 16 + 16)
                        dve.wait_ge(s_gat2, k + 1)
                        for j in range(NJD):
                            last = dve.tensor_scalar(hot_d[:, j, :], rows[:, half, 1, :], g.nodecol[:, j:j + 1], None, ALU.is_equal)
                        last.then_inc(s_hot2, 1)
                        dve.wait_ge(s_hot2, k + 1)
                        dve.sem_inc(s_row2_free, 1)
                        for step in range(PER):
                            for j in range(2):
                                dve.wait_ge(s_before[j], k * PER + step + 1)
                                dve.wait_ge(s_read[j], k * PER + step)
                                for m in range(2):
                                    ch = 2 * j + m
                                    q = ch * PER + step
                                    last = dve.scalar_tensor_tensor(
                                        hit[:, ch, :], hot_c[:, half, q, :], 1.0,
                                        pacc[:, j, m * NCELL:(m + 1) * NCELL], ALU.mult, ALU.mult,
                                        accum_out=place[:, q:q + 1])
                                last.then_inc(s_read[j], 1)
                        for j in range(2):
                            dve.wait_ge(s_read[j], (k + 1) * PER)
                        dve.wait_ge(s_sent[half], i * CH * 16)
                        st.add(dve.tensor_scalar(skip[:, :], cell[:, ds(k * CH, CH)], 0.0, NOWHERE, ALU.is_lt, ALU.mult))
                        st.do(dve.tensor_copy(place_i[:, :], place[:, :]))
                        st.add(dve.tensor_scalar(low_i[:, :], place_i[:, :], P - 1, None, ALU.bitwise_and))
                        st.do(dve.tensor_scalar(high_i[:, :], place_i[:, :], 7, None, ALU.logical_shift_right))
                        st.do(dve.scalar_tensor_tensor(place[:, :], low_i[:, :], float(NTC), high_i[:, :], ALU.mult, ALU.add))
                        dve.tensor_tensor(idx[:, half, :], place[:, :], skip[:, :], ALU.add)
                        dve.tensor_copy(stage[:, half, :, F:F + 3], frac[:, ds(k * CH, CH), :])
                        dve.tensor_copy(stage[:, half, :, F + 3].rearrange("p (c t) -> p c t", c=CHAINS),
                                        by_chain[:, :, ds(k * PER, PER), 7]).then_inc(s_rest, 1)
                        assert st.n == S
                        dve.wait_ge(s_rest, k + 1)

            @block.tensor
            def _(pe):
                pe.sem_inc(s_gat2, 1)
                pe.sem_inc(s_ranked, 2)
                with pe.Fori(0, LOOP) as i:
                    for half in range(2):
                        k = i * 2 + half
                        pe.wait_ge(s_hotc2, k + 1)

                        def add_up(j, step, matrix):
                            for m in range(2):
                                q = (2 * j + m) * PER + step
                                last = pe.matmul(pacc[:, j, m * NCELL:(m + 1) * NCELL], matrix[:, :],
                                                 hot_c[:, half, q, :], start=False, stop=True, skip_group_check=True)
                            return last
                        for j in range(2):
                            add_up(j, 0, g.before).then_inc(s_before[j], 1)
                        for step in range(PER):
                            for j in range(2):
                                pe.wait_ge(s_read[j], k * PER + step + 1)
                                last = add_up(j, step, g.from_on)
                                if step + 1 < PER:
                                    add_up(j, step + 1, g.before).then_inc(s_before[j], 1)
                        last.then_inc(s_ranked, 1)
                        pe.wait_ge(s_hot2, k + 1)
                        pe.wait_ge(s_out2, k + 1)
                        for q in range(CH):
                            if q % PER == 0:
                                tile = (q // PER) * CHAIN + k * PER
                                dst_sb = load_values(nc, PE, g.table_b[0:1, 1, ds(tile, PER)], ND - 1)
                            d = dst_sb[q % PER]
                            for j in range(NJD):
                                for part in range(3):
                                    last = pe.matmul(pdel[:, half, q * F:(q + 1) * F], hot_d[:, j, q * P:(q + 1) * P],
                                                     g.hparts[:, ds(d * NJD + j, 1), part, :].rearrange("p a f -> p (a f)"),
                                                     start=(j == 0 and part == 0), stop=(j == NJD - 1 and part == 2))
                        last.then_inc(s_gat2, 1)

            @block.scalar
            def _(act):
                act.sem_inc(s_out2, 2)
                with act.Fori(0, LOOP) as i:
                    for half in range(2):
                        k = i * 2 + half
                        act.wait_ge(s_gat2, k + 2)
                        act.wait_ge(s_sent[half], i * CH * 16)
                        act.activation(stage[:, half, :, 0:F], pdel[:, half, :].rearrange("p (t f) -> p t f", f=F),
                                       ACT.Copy).then_inc(s_out2, 1)

            @block.gpsimd
            def _(pool):
                with pool.Fori(0, LOOP) as i:
                    for half in range(2):
                        k = i * 2 + half
                        pool.wait_ge(s_rest, k + 1)
                        pool.wait_ge(s_out2, k + 3)
                        pool.sem_inc(s_tick, 1)
                        for q in range(CH):
                            pool.indirect_dma_start(g.rows_c2, bass.IndirectOffsetOnAxis(idx[:, half, q:q + 1], 0),
                                                    stage[:, half, q, :], None, bounds_check=P * NTC - 1,
                                                    oob_is_err=False).then_inc(s_sent[half], 16)
                for half in range(2):
                    pool.wait_ge(s_sent[half], LOOP * CH * 16)


def end_first_layer(g, c, conv_b):
    nc, sem = g.nc, g.sem
    sb = lambda n, s, d=F32: g.sb(n, s, d, c)
    acc = c.enter_context(nc.psum_tensor("acc_conv", [P, 4 * 512], F32))
    with ExitStack() as c2:
        add_up_by_source(g, c2, "r2", g.msg2, F, acc)
    z, bv = sb("z3", [P, NBLK, F]), sb("conv_bv", [P, F])
    ln = NormBuffers(mean=g.mean, var=g.var, std=g.std, sq=sb("ln_sq2", [P, NBLK, F]))
    s_b, s_dve, s_var, s_std = sem("s_conv_b"), sem("s_dve_l"), sem("s_var2"), sem("s_std2")
    with nc.Block() as block:
        @block.sync
        def _(sp):
            sp.dma_start(bv[:, :], conv_b.rearrange("(o f) -> o f", o=1).to_broadcast([P, F])).then_inc(s_b, 16)

        @block.vector
        def _(dve):
            st = Steps(dve, s_dve)
            dve.wait_ge(s_b, 16)
            st.do(dve.tensor_tensor(z[:, :, :], acc[:, 0:NBLK * F].rearrange("p (b f) -> p b f", f=F),
                                    g.rdeg[:, :].unsqueeze(2).to_broadcast([P, NBLK, F]), ALU.mult))
            st.do(dve.tensor_tensor(z[:, :, :], z[:, :, :], bv[:, :].unsqueeze(1).to_broadcast([P, NBLK, F]), ALU.add))
            st.do(dve.tensor_tensor(g.x[:, :, :], g.x[:, :, :], z[:, :, :], ALU.add))

            def root():
                dve.sem_inc(s_var, 1)
                dve.wait_ge(s_std, 1)
            layer_norm(dve, root, st, ln, g.x, g.h)
            st.do(dve.tensor_scalar(g.h[:, :, :], g.h[:, :, :], 0.0, None, ALU.max))
            split_parts(dve, st, [g.hparts[:, :, k, :] for k in range(3)], g.h[:, :, :], ln.sq[:, :, :])

        @block.scalar
        def _(act):
            act.wait_ge(s_var, 1)
            act.activation(g.std[:, :], g.var[:, :], ACT.Sqrt).then_inc(s_std, 1)


def second_layer(g, c, W1, b1, W2, b2, W3, b3, W4, b4, out):
    nc, sem = g.nc, g.sem
    sb = lambda n, s, d=F32: g.sb(n, s, d, c)
    NJD, NJS = DST_SB // P, SRC_SB // P
    LOOP = NCHK_B // 2
    cat = sb("cat", [P, NBLK, 3 * F])
    NBS = NA * NJS
    G = 4
    with ExitStack() as c1:
        sb1 = lambda n, s, d=F32: g.sb(n, s, d, c1)
        rows = sb1("rows3", [P, 2, 2, CH * P], F16)
        hot_d = sb1("hot_d3", [P, NJD, CH * P], BF16)
        hot_s = sb1("hot_s3", [P, NJS, CH * P], BF16)
        hot_e = sb1("hot_e3", [P, 2, G, DST_SB + SRC_SB])
        msg = sb1("msg3", [P, 2, G, 2, F])
        acc = c1.enter_context(nc.psum_tensor("acc_mi_mo", [P, 7 * 512], F32))
        pg = c1.enter_context(nc.psum_tensor("pg3", [P, G, 2, F], F32))
        MO = NBLK * F
        s_row, s_row_free = [sem(f"s_rows3{h}") for h in range(2)], sem("s_rows3_free")
        s_hot, s_gat, s_msg = sem("s_hot3"), sem("s_gathered3"), sem("s_msg3")
        s_hote, s_used, s_all = sem("s_hot_e3"), sem("s_msg3_used"), sem("s_hots3_used")
        with nc.Block() as block:
            @block.sync
            def _(sp):
                with sp.Fori(0, LOOP) as i:
                    for half in range(2):
                        k = i * 2 + half
                        sp.wait_ge(s_row_free, k + 1)
                        for kind in range(2):
                            sp.dma_start(rows[:, half, kind, :],
                                         g.local_rows[kind:kind + 1, ds(k * CH, CH), :].rearrange("o t e -> o (t e)")
                                         .to_broadcast([P, CH * P])).then_inc(s_row[half], 16)

            @block.vector
            def _(dve):
                dve.sem_inc(s_row_free, 2)
                with dve.Fori(0, LOOP) as i:
                    for half in range(2):
                        k = i * 2 + half
                        dve.wait_ge(s_row[half], i * 32 + 32)
                        dve.wait_ge(s_all, k + 1)
                        for j in range(NJD):
                            dve.tensor_scalar(hot_d[:, j, :], rows[:, half, 1, :], g.nodecol[:, j:j + 1], None, ALU.is_equal)
                        for j in range(NJS):
                            last = dve.tensor_scalar(hot_s[:, j, :], rows[:, half, 0, :], g.nodecol[:, j:j + 1], None, ALU.is_equal)
                        last.then_inc(s_hot, 1)
                        dve.wait_ge(s_hot, k + 1)
                        dve.sem_inc(s_row_free, 1)
                        for gr in range(CH // G):
                            n = k * (CH // G) + gr
                            dve.wait_ge(s_used, n + 1)
                            for q in range(G):
                                t = k * CH + gr * G + q
                                dve.tensor_scalar(hot_e[:, gr % 2, q, 0:DST_SB], g.iotaf[:, :],
                                                  g.edges[:, ds(t, 1), 1:2].rearrange("p a b -> p (a b)"), None, ALU.is_equal)
                                dve.tensor_scalar(hot_e[:, gr % 2, q, DST_SB:], g.iotaf[:, 0:SRC_SB],
                                                  g.edges[:, ds(t, 1), 0:1].rearrange("p a b -> p (a b)"), None, ALU.is_equal)
                            dve.wait_ge(s_gat, n + 1)
                            dve.tensor_tensor(msg[:, gr % 2, :, :, :].rearrange("p g s f -> p g (s f)"),
                                              pg[:, :, :, :].rearrange("p g s f -> p g (s f)"),
                                              g.edges[:, ds(k * CH + gr * G, G), 5].unsqueeze(2).to_broadcast([P, G, 2 * F]),
                                              ALU.mult).then_inc(s_msg, 1)

            @block.tensor
            def _(pe):
                for b in range(7):
                    pe.matmul(acc[:, b * 512:(b + 1) * 512], g.ident[:, :], g.zero512[:, :], start=True, stop=True)
                pe.sem_inc(s_used, 2)
                pe.sem_inc(s_all, 1)
                with pe.Fori(0, LOOP) as i:
                    for half in range(2):
                        k = i * 2 + half
                        pe.wait_ge(s_hot, k + 1)
                        for gr in range(CH // G):
                            n = k * (CH // G) + gr
                            pe.wait_ge(s_msg, n)
                            t = k * CH + gr * G
                            src_sb = load_values(nc, PE, g.table_b[0:1, 0, ds(t, G)], NA - 1)
                            dst_sb = load_values(nc, PE, g.table_b[0:1, 1, ds(t, G)], ND - 1)
                            for q in range(G):
                                a, d = src_sb[q], dst_sb[q]
                                e = slice((gr * G + q) * P, (gr * G + q + 1) * P)
                                for side, hot, nj, sb0 in ((0, hot_s, NJS, a), (1, hot_d, NJD, d)):
                                    for j in range(nj):
                                        for part in range(3):
                                            last = pe.matmul(
                                                pg[:, q, side, :], hot[:, j, e],
                                                g.hparts[:, ds(sb0 * nj + j, 1), part, :].rearrange("p a f -> p (a f)"),
                                                start=(j == 0 and part == 0), stop=(j == nj - 1 and part == 2))
                            last.then_inc(s_gat, 1)
                            if gr == CH // G - 1:
                                pe.wait_ge(s_gat, n + 1)
                                pe.sem_inc(s_all, 1)
                            pe.wait_ge(s_msg, n + 1)
                            for q in range(G):
                                a, d = src_sb[q], dst_sb[q]
                                for j in range(NJD):
                                    pe.matmul(acc[:, ds((d * NJD + j) * F, F)], hot_e[:, gr % 2, q, j * P:(j + 1) * P],
                                              msg[:, gr % 2, q, 0, :], start=False, stop=True, skip_group_check=True)
                                for j in range(NJS):
                                    last = pe.matmul(acc[:, ds((a * NJS + j) * F + MO, F)],
                                                     hot_e[:, gr % 2, q, DST_SB + j * P:DST_SB + (j + 1) * P],
                                                     msg[:, gr % 2, q, 1, :], start=False, stop=True, skip_group_check=True)
                            last.then_inc(s_used, 1)
        s_cat = sem("s_cat")
        with nc.Block() as block:
            @block.vector
            def _(dve):
                dve.memset(cat[:, NBS:NBLK, F:2 * F], 0.0)
                dve.tensor_copy(cat[:, :, 0:F], acc[:, 0:NBLK * F].rearrange("p (b f) -> p b f", f=F))
                dve.tensor_copy(cat[:, 0:NBS, F:2 * F], acc[:, MO:MO + NBS * F].rearrange("p (b f) -> p b f", f=F))
                dve.tensor_copy(cat[:, :, 2 * F:3 * F], g.h[:, :, :]).then_inc(s_cat, 1)
                dve.wait_ge(s_cat, 1)

    NG = NBLK // 4
    layers = [(W1, b1, 3 * F), (W2, b2, F), (W3, b3, F), (W4, b4, F)]
    ws = [sb(f"mlp_w{n}", [k, F]) for n, (_, _, k) in enumerate(layers)]
    bs = [sb(f"mlp_b{n}", [F, 1]) for n in range(4)]
    catT = sb("catT", [3 * F, 2, 512])
    act_t = sb("act_t", [F, 4, 2, 512])
    res = sb("res", [P, NBLK, F])
    s_w, s_tr, s_in = sem("s_mlp_w"), sem("s_mlp_tr"), sem("s_mlp_in")
    s_mm, s_act = [sem(f"s_mlp_mm{n}") for n in range(4)], [sem(f"s_mlp_act{n}") for n in range(4)]
    s_back, s_res, s_out, s_dve = sem("s_mlp_back"), sem("s_mlp_res"), sem("s_out"), sem("s_dve_m")
    pt = c.enter_context(nc.psum_tensor("pt4", [P, 2, 512], F32))
    pd = c.enter_context(nc.psum_tensor("pd4", [P, 4, 512], F32))
    pb = c.enter_context(nc.psum_tensor("pb4", [P, 2, 512], F32))
    with nc.Block() as block:
        @block.sync
        def _(sp):
            for n, (w, b, k) in enumerate(layers):
                sp.dma_start(ws[n][:, :], w).then_inc(s_w, 16)
                with nc.allow_non_contiguous_dma(reason="a bias column"):
                    sp.dma_start(bs[n][:, :], b.rearrange("(f o) -> f o", o=1)).then_inc(s_w, 16)
            sp.wait_ge(s_res, NG)
            sp.dma_start(out[0:FULL_BLK * P, :].rearrange("(b p) f -> p b f", p=P),
                         res[:, 0:FULL_BLK, :]).then_inc(s_out, 16)
            sp.dma_start(out[FULL_BLK * P:N, :], res[0:REST, FULL_BLK, :]).then_inc(s_out, 16)
            sp.wait_ge(s_out, 32)

        @block.tensor
        def _(pe):
            pe.wait_ge(s_w, 128)
            for n in range(NG):
                if n >= 2:
                    pe.wait_ge(s_in, n - 1)
                for b in range(4):
                    last = pe.transpose(pt[0:3 * F, n % 2, b * P:(b + 1) * P], cat[:, n * 4 + b, :], g.ident[:, :])
                last.then_inc(s_tr, 1)
                for layer in range(4):
                    if layer == 0:
                        pe.wait_ge(s_in, n + 1)
                        rhs = catT[:, n % 2, :]
                    else:
                        pe.wait_ge(s_act[layer - 1], n + 1)
                        rhs = act_t[:, layer - 1, n % 2, :]
                    if n:
                        pe.wait_ge(s_act[layer], n)
                    pe.matmul(pd[0:F, layer, :], ws[layer][:, :], rhs, start=True, stop=True).then_inc(s_mm[layer], 1)
                pe.wait_ge(s_act[3], n + 1)
                if n >= 2:
                    pe.wait_ge(s_res, n - 1)
                for b in range(4):
                    last = pe.transpose(pb[:, n % 2, b * F:(b + 1) * F], act_t[:, 3, n % 2, b * P:(b + 1) * P],
                                        g.ident[0:F, 0:F])
                last.then_inc(s_back, 1)

        @block.scalar
        def _(act):
            act.wait_ge(s_w, 128)
            for n in range(NG):
                for layer in range(4):
                    act.wait_ge(s_mm[layer], n + 1)
                    if n >= 2 and layer == 3:
                        act.wait_ge(s_back, n - 1)
                    act.activation(act_t[:, layer, n % 2, :], pd[0:F, layer, :], ACT.Tanh,
                                   bias=bs[layer][:, :]).then_inc(s_act[layer], 1)

        @block.vector
        def _(dve):
            for n in range(NG):
                dve.wait_ge(s_tr, n + 1)
                if n >= 2:
                    dve.wait_ge(s_mm[0], n - 1)
                dve.tensor_copy(catT[:, n % 2, :], pt[0:3 * F, n % 2, :]).then_inc(s_in, 1)
                if n:
                    dve.wait_ge(s_back, n)
                    m = n - 1
                    dve.tensor_tensor(res[:, 4 * m:4 * m + 4, :], g.x[:, 4 * m:4 * m + 4, :],
                                      pb[:, m % 2, 0:4 * F].rearrange("p (b f) -> p b f", f=F), ALU.add).then_inc(s_res, 1)
            m = NG - 1
            dve.wait_ge(s_back, NG)
            dve.tensor_tensor(res[:, 4 * m:4 * m + 4, :], g.x[:, 4 * m:4 * m + 4, :],
                              pb[:, m % 2, 0:4 * F].rearrange("p (b f) -> p b f", f=F), ALU.add).then_inc(s_res, 1)


_INS = ['x', 'src', 'dst', 'edge_attr_3', 'edge_weight1', 'L0_gnn_stn1_w', 'L0_gnn_stn1_b',
        'L0_gnn_stn2_w', 'L0_gnn_stn2_b', 'L0_gnn_stn3_w', 'L0_gnn_stn3_b', 'L0_gnn_stn4_w',
        'L0_gnn_stn4_b', 'L0_gnn_conv_w', 'L0_gnn_conv_b', 'L1_gnn_W1', 'L1_gnn_b1', 'L1_gnn_W2',
        'L1_gnn_b2', 'L1_gnn_W3', 'L1_gnn_b3', 'L1_gnn_W4', 'L1_gnn_b4']


def kernel(**inputs):
    import concourse.bacc as _bacc
    from concourse.bass_utils import run_bass_kernel_spmd as _run

    nc = _bacc.Bacc("TRN2", target_bir_lowering=False, num_devices=1)
    arrays, args = {}, []
    for name in _INS:
        a = np.ascontiguousarray(inputs[name])
        arrays[f"in_{name}"] = a
        args.append(nc.dram_tensor(f"in_{name}", a.shape, mybir.dt.from_np(a.dtype), kind="ExternalInput").ap())
    out = nc.dram_tensor("out_0", (N, F), F32, kind="ExternalOutput").ap()
    program(nc, *args, out)
    r = _run(nc, [arrays], core_ids=[0])
    return np.asarray(r.results[0]["out_0"])
```

```python
from contextlib import ExitStack

import numpy as np
import concourse.bass as bass
from concourse import mybir

F32 = mybir.dt.float32
F16 = mybir.dt.float16
BF16 = mybir.dt.bfloat16
I32 = mybir.dt.int32
U32 = mybir.dt.uint32
ALU = mybir.AluOpType
ACT = mybir.ActivationFunctionType
AX = mybir.AxisListType.X
PE, DVE, ACTE, POOL = (mybir.EngineType.PE, mybir.EngineType.DVE, mybir.EngineType.Activation,
                       mybir.EngineType.Pool)
ds = bass.ds

P = 128
N, F, H = 6250, 32, 64
E = 200000
EP, ET = 125, 1600
SRC_SB, DST_SB = 256, 512
SRC_SHIFT, DST_SHIFT = 8, 9
NA, ND = -(-N // SRC_SB), -(-N // DST_SB)
NBUCK = NA * ND
NBUCK2 = NBUCK + NBUCK % 2
NBLK = ND * DST_SB // P
FULL_BLK, REST = N // P, N % P
KS, K3 = 5, 125
NCELL = 64
CH = 16
CHAINS = 4
PER = CH // CHAINS


def chunks_for(buckets):
    tiles = (E + (P - 1) * buckets) // P
    step = 2 * CH
    return -(-tiles // step) * 2


NCHK_B = chunks_for(NBUCK)
NCHK_C = chunks_for(NCELL)
NT, NTC = NCHK_B * CH, NCHK_C * CH
EDGE_W = 8
C1_W, C2_W = H + 4, F + 4
NOWHERE = 1.0e7
NQ = -(-NT // P)
NQC = -(-NTC // P)
EPS = 1e-5


class Program:

    def __init__(self, nc):
        self.nc = nc


class NormBuffers:

    def __init__(self, mean, var, std, sq):
        self.mean, self.var, self.std, self.sq = mean, var, std, sq


class TableBuffers:

    def __init__(self, ones, t_i, hit):
        self.ones, self.t_i, self.hit = ones, t_i, hit


class Steps:

    def __init__(self, eng, sem, base=0, turns=None):
        self.eng, self.sem, self.base, self.n, self.turns = eng, sem, base, 0, turns

    def add(self, ins):
        ins.then_inc(self.sem, 1)
        self.n += 1

    def wait(self):
        self.eng.wait_ge(self.sem, self.base + self.n)
        if self.turns is not None:
            self.eng.sem_inc(self.turns, 1)

    def do(self, ins):
        self.add(ins)
        self.wait()


def load_values(nc, engine, ap, most):
    _, values = nc.values_load_multi_w_load_instructions(
        ap, engines=(engine,), min_val=0, max_val=most,
        skip_runtime_bounds_check_because="the tables are clamped where they are made")
    return values


def layer_norm(dve, act_sqrt, st, v, xin, out):
    st.do(dve.tensor_reduce(v.mean[:, :], xin[:, :, :], AX, ALU.add))
    st.do(dve.tensor_scalar(v.mean[:, :], v.mean[:, :], 1.0 / F, None, ALU.mult))
    st.do(dve.tensor_tensor(out[:, :, :], xin[:, :, :],
                            v.mean[:, :].unsqueeze(2).to_broadcast([P, NBLK, F]), ALU.subtract))
    st.do(dve.tensor_tensor(v.sq[:, :, :], out[:, :, :], out[:, :, :], ALU.mult))
    st.do(dve.tensor_reduce(v.var[:, :], v.sq[:, :, :], AX, ALU.add))
    st.do(dve.tensor_scalar(v.var[:, :], v.var[:, :], 1.0 / F, EPS, ALU.mult, ALU.add))
    act_sqrt()
    st.do(dve.reciprocal(v.var[:, :], v.std[:, :]))
    st.do(dve.tensor_tensor(out[:, :, :], out[:, :, :],
                            v.var[:, :].unsqueeze(2).to_broadcast([P, NBLK, F]), ALU.mult))


def split_parts(dve, st, parts, val, rest):
    st.do(dve.tensor_copy(parts[0], val))
    st.do(dve.tensor_tensor(rest, val, parts[0], ALU.subtract))
    st.do(dve.tensor_copy(parts[1], rest))
    st.do(dve.tensor_tensor(rest, rest, parts[1], ALU.subtract))
    st.do(dve.tensor_copy(parts[2], rest))


def program(nc, x, src, dst, attr, wt, stn1_w, stn1_b, stn2_w, stn2_b, stn3_w, stn3_b, stn4_w,
            stn4_b, conv_w, conv_b, W1, b1, W2, b2, W3, b3, W4, b4, out):
    root = ExitStack()
    with root:
        g = Program(nc=nc)

        def sb(name, shape, dt=F32, ctx=root):
            return ctx.enter_context(nc.sbuf_tensor(name, shape, dt))

        used = []

        def sem(name):
            used.append(nc.alloc_semaphore(name=name))
            return used[-1]

        def recycle():
            done = [s for s in used if "sent" not in s.name]
            used.clear()
            nc.all_engine_barrier()
            nc.clear_and_free_semaphores(done)
            nc.all_engine_barrier()

        g.sb, g.sem = sb, sem
        g.spare = sb("spare", [1, 2])

        def open_sent(pool, sent):
            for half in range(2):
                pool.dma_start(g.spare[0:1, half:half + 1], wt[0:1, 0:1]).then_inc(sent[half], 16)

        g.open_sent = open_sent
        g.edges_b = nc.dram_tensor("edges_b", (P * NT, EDGE_W), F32).ap()
        g.rows_c1 = nc.dram_tensor("rows_c1", (P * NTC, C1_W), F32).ap()
        g.rows_c2 = nc.dram_tensor("rows_c2", (P * NTC, C2_W), F32).ap()
        g.msg1 = nc.dram_tensor("msg1", (P * NT, H), F32).ap()
        g.msg2 = nc.dram_tensor("msg2", (P * NT, F), F32).ap()
        g.local_rows = nc.dram_tensor("local_rows", (2, NQ * P, P), F16).ap()
        g.tab_b = nc.dram_tensor("tab_b", (2, NQ * P), I32).ap()
        g.tab_c1 = nc.dram_tensor("tab_c1", (1, NQC * P), I32).ap()
        g.tab_c2 = nc.dram_tensor("tab_c2", (1, NQC * P), I32).ap()
        g.iota = sb("iota", [P, DST_SB], I32)
        g.iota16 = sb("iota16", [P, DST_SB], F16)
        g.iotaf = sb("iotaf", [P, DST_SB])
        g.nodecol_i = sb("nodecol_i", [P, NQ], I32)
        g.nodecol = sb("nodecol", [P, NQ])
        g.ident = sb("ident", [P, P])
        g.before = sb("before", [P, P], F16)
        g.from_on = sb("from_on", [P, P], F16)
        g.ones16 = sb("ones16", [P, P], F16)
        g.onesf = sb("onesf", [1, P])
        g.zero512 = sb("zero512", [P, 512])
        g.x = sb("x_nodes", [P, NBLK, F])
        g.h = sb("h_nodes", [P, NBLK, F])
        g.rdeg = sb("rdeg", [P, NBLK])
        g.hparts = sb("hparts", [P, NBLK, 3, F], BF16)
        g.table_b = sb("table_b", [1, 2, NQ * P], I32)
        g.table_c = sb("table_c", [1, NQC * P], I32)
        g.mean, g.var, g.std = (sb(n, [P, NBLK]) for n in ("ln_mean", "ln_var", "ln_std"))
        with ExitStack() as c:
            order_edges(g, c, x, src, dst, attr, wt)
        with ExitStack() as c:
            g.edges = sb("edges", [P, NT, EDGE_W], F32, c)
            g.tparts = sb("tparts", [P, NBLK, 3, 3], BF16, c)
            g.tparts_neg = sb("tparts_neg", [P, NBLK, 3, 3], BF16, c)
            with ExitStack() as c1:
                g.h1parts = sb("h1parts", [P, NBLK, 3, H], BF16, c1)
                with ExitStack() as c2:
                    degree_and_first_conv(g, c2, stn1_w, stn1_b)
                with ExitStack() as c2:
                    to_cells_1(g, c2)
            with ExitStack() as c2:
                cell_products(g, c2, "c1", g.rows_c1, g.tab_c1, g.msg1, stn2_w, H)
            with ExitStack() as c2:
                shift_network(g, c2, stn2_b, stn3_w, stn3_b, stn4_w, stn4_b)
            recycle()
            with ExitStack() as c2:
                to_cells_2(g, c2)
            with ExitStack() as c2:
                cell_products(g, c2, "c2", g.rows_c2, g.tab_c2, g.msg2, conv_w, F)
            with ExitStack() as c2:
                end_first_layer(g, c2, conv_b)
            with ExitStack() as c2:
                second_layer(g, c2, W1, b1, W2, b2, W3, b3, W4, b4, out)


def order_edges(g, c, x, src, dst, attr, wt):
    nc, sem = g.nc, g.sem
    sb = lambda n, s, d=F32: g.sb(n, s, d, c)
    edge = sb("edge", [EP, ET, 6])
    bucket, cell = sb("bucket", [EP, ET]), sb("cell", [EP, ET])
    no_edge = sb("no_edge", [P, NT // 32, EDGE_W])
    no_c1 = sb("no_c1", [P, NTC // 96, C1_W])
    no_c2 = sb("no_c2", [P, NTC // 48, C2_W])
    zeros = sb("zeros", [P, NT, 1])
    loads = ExitStack()
    src_i, dst_i, tmp_i = (g.sb(n, [EP, ET], I32, loads) for n in ("src_i", "dst_i", "tmp_i"))
    attr_in, base3 = (g.sb(n, [EP, ET, 3], F32, loads) for n in ("attr_in", "base3"))
    wt_in = g.sb("wt_in", [EP, ET], F32, loads)
    ln = NormBuffers(mean=g.mean, var=g.var, std=g.std, sq=g.sb("ln_sq", [P, NBLK, F], F32, loads))

    s_load, s_nodes, s_id = sem("s_edge_loads"), sem("s_node_loads"), sem("s_iota")
    s_dve, s_pool, s_fill = sem("s_dve_a"), sem("s_pool_a"), sem("s_fill")
    s_var, s_std, s_copied, s_blank = sem("s_var"), sem("s_std"), sem("s_copied"), sem("s_blank")
    s_xz = sem("s_x_zeroed")

    with nc.Block() as block:
        @block.sync
        def _(sp):
            sp.dma_start(src_i[:, :], src.rearrange("(p t) -> p t", p=EP)).then_inc(s_load, 16)
            sp.dma_start(dst_i[:, :], dst.rearrange("(p t) -> p t", p=EP)).then_inc(s_load, 16)
            sp.dma_start(attr_in[:, :, :], attr.rearrange("(p t) k -> p t k", p=EP)).then_inc(s_load, 16)
            sp.dma_start(wt_in[:, :], wt.rearrange("(p t) k -> p (t k)", p=EP)).then_inc(s_load, 16)
            sp.wait_ge(s_xz, 1)
            sp.dma_start(g.x[:, 0:FULL_BLK, :],
                         x[0:FULL_BLK * P, :].rearrange("(b p) f -> p b f", p=P)).then_inc(s_nodes, 16)
            sp.dma_start(g.x[0:REST, FULL_BLK, :], x[FULL_BLK * P:N, :]).then_inc(s_nodes, 16)
            sp.wait_ge(s_blank, 1)
            for buf, blank, times in ((g.edges_b, no_edge, 32), (g.rows_c1, no_c1, 96),
                                      (g.rows_c2, no_c2, 48)):
                view = buf.rearrange("(p t) w -> p t w", p=P)
                n = blank.shape[1]
                for k in range(times):
                    sp.dma_start(view[:, k * n:(k + 1) * n, :], blank[:, :, :]).then_inc(s_fill, 16)
            for buf, width in ((g.msg1, H), (g.msg2, F)):
                view = buf.rearrange("(p t) w -> p (t w)", p=P)
                for k in range(width):
                    sp.dma_start(view[:, k * NT:(k + 1) * NT], zeros[:, :, 0]).then_inc(s_fill, 16)

        @block.gpsimd
        def _(pool):
            pool.iota(g.iota[:, :], [[1, DST_SB]], 0, 0).then_inc(s_id, 1)
            pool.iota(g.nodecol_i[:, :], [[P, NQ]], 0, 1).then_inc(s_id, 1)
            st = Steps(pool, s_pool)
            st.add(pool.memset(g.onesf[:, :], 1.0))
            st.add(pool.memset(g.zero512[:, :], 0.0))
            st.add(pool.memset(g.ones16[:, :], 1.0))
            st.add(pool.memset(no_edge[:, :, :], 0.0))
            st.add(pool.memset(no_c1[:, :, :], 0.0))
            st.add(pool.memset(no_c2[:, :, :], 0.0))
            st.do(pool.memset(zeros[:, :, :], 0.0))
            st.add(pool.memset(no_edge[:, :, 0:2], -1.0))
            st.add(pool.memset(no_edge[:, :, 6:7], NOWHERE))
            st.add(pool.memset(no_c1[:, :, C1_W - 1:C1_W], NOWHERE))
            st.do(pool.memset(no_c2[:, :, C2_W - 1:C2_W], NOWHERE))
            pool.sem_inc(s_blank, 1)

        @block.scalar
        def _(act):
            act.wait_ge(s_load, 64)
            act.activation(edge[:, :, 2:5], attr_in[:, :, :], ACT.Copy).then_inc(s_copied, 1)
            act.activation(edge[:, :, 5], wt_in[:, :], ACT.Copy).then_inc(s_copied, 1)
            act.wait_ge(s_var, 1)
            act.activation(g.std[:, :], g.var[:, :], ACT.Sqrt).then_inc(s_std, 1)

        @block.vector
        def _(dve):
            st = Steps(dve, s_dve)
            st.do(dve.memset(g.x[:, :, :], 0.0))
            dve.sem_inc(s_xz, 1)
            dve.wait_ge(s_id, 2)
            st.add(dve.tensor_copy(g.iota16[:, :], g.iota[:, :]))
            st.add(dve.tensor_copy(g.nodecol[:, :], g.nodecol_i[:, :]))
            st.do(dve.tensor_copy(g.iotaf[:, :], g.iota[:, :]))
            st.add(dve.tensor_scalar(g.ident[:, :], g.iotaf[:, 0:P], g.nodecol[:, 0:1], None, ALU.is_equal))
            st.add(dve.tensor_scalar(g.before[:, :], g.iotaf[:, 0:P], g.nodecol[:, 0:1], None, ALU.is_gt))
            st.add(dve.tensor_scalar(g.from_on[:, :], g.iotaf[:, 0:P], g.nodecol[:, 0:1], None, ALU.is_le))
            dve.wait_ge(s_load, 64)
            st.do(dve.tensor_scalar(tmp_i[:, :], src_i[:, :], SRC_SB - 1, None, ALU.bitwise_and))
            st.do(dve.tensor_copy(edge[:, :, 0], tmp_i[:, :]))
            st.do(dve.tensor_scalar(src_i[:, :], src_i[:, :], SRC_SHIFT, None, ALU.logical_shift_right))
            st.do(dve.tensor_scalar(tmp_i[:, :], dst_i[:, :], DST_SB - 1, None, ALU.bitwise_and))
            st.do(dve.tensor_copy(edge[:, :, 1], tmp_i[:, :]))
            st.do(dve.tensor_scalar(dst_i[:, :], dst_i[:, :], DST_SHIFT, None, ALU.logical_shift_right))
            st.do(dve.scalar_tensor_tensor(bucket[:, :], src_i[:, :], float(ND), dst_i[:, :], ALU.mult, ALU.add))
            dve.wait_ge(s_copied, 2)
            st.do(dve.tensor_scalar(attr_in[:, :, :], attr_in[:, :, :], float(KS - 1), None, ALU.mult))
            st.do(dve.tensor_scalar(base3[:, :, :], attr_in[:, :, :], 1.0, None, ALU.is_ge))
            for knot in (2.0, 3.0):
                st.do(dve.scalar_tensor_tensor(base3[:, :, :], attr_in[:, :, :], knot, base3[:, :, :],
                                               ALU.is_ge, ALU.add))
            st.do(dve.scalar_tensor_tensor(cell[:, :], base3[:, :, 0], 4.0, base3[:, :, 1], ALU.mult, ALU.add))
            st.do(dve.scalar_tensor_tensor(cell[:, :], cell[:, :], 4.0, base3[:, :, 2], ALU.mult, ALU.add))
            dve.wait_ge(s_nodes, 32)

            def root():
                dve.sem_inc(s_var, 1)
                dve.wait_ge(s_std, 1)
            layer_norm(dve, root, st, ln, g.x, g.h)
            st.do(dve.tensor_scalar(g.h[:, :, :], g.h[:, :, :], 0.0, None, ALU.max))
            split_parts(dve, st, [g.hparts[:, :, k, :] for k in range(3)], g.h[:, :, :], ln.sq[:, :, :])

    loads.close()

    LOOP = ET // CH // 2
    chain_len = ET // CHAINS
    BOTH = NBUCK2 + NCELL
    hot = sb("hot", [EP, 2, CH, BOTH], F16)
    acc = c.enter_context(nc.psum_tensor("acc", [P, CHAINS, 512], F32))
    s_hot, s_hot_free = sem("s_hot"), sem("s_hot_free")

    def tile_of(k, q):
        return (q // PER) * chain_len + k * PER + q % PER

    def bucket_hots(eng, k, half):
        for q in range(CH):
            last = eng.tensor_scalar(hot[:, half, q, 0:NBUCK2], g.iota16[0:EP, 0:NBUCK2],
                                     bucket[:, ds(tile_of(k, q), 1)], None, ALU.is_equal)
        return last

    def cell_hots(eng, k, half):
        shape = [EP, CHAINS, PER, NCELL]
        return eng.tensor_tensor(
            hot[:, half, :, NBUCK2:BOTH].rearrange("p (c t) n -> p c t n", c=CHAINS),
            g.iota16[0:EP, 0:NCELL].unsqueeze(1).unsqueeze(1).to_broadcast(shape),
            cell[:, :].rearrange("p (c t) -> p c t", c=CHAINS)[:, :, ds(k * PER, PER)].unsqueeze(3).to_broadcast(shape),
            ALU.is_equal)

    with nc.Block() as block:
        @block.vector
        def _(dve):
            with dve.Fori(0, LOOP) as i:
                for half in range(2):
                    k = i * 2 + half
                    dve.wait_ge(s_hot_free, k + 1)
                    bucket_hots(dve, k, half)
                    cell_hots(dve, k, half).then_inc(s_hot, 1)

        @block.tensor
        def _(pe):
            for ch in range(CHAINS):
                pe.matmul(acc[:, ch, :], g.ident[:, :], g.zero512[:, :], start=True, stop=True)
            pe.sem_inc(s_hot_free, 2)
            with pe.Fori(0, LOOP) as i:
                for half in range(2):
                    pe.wait_ge(s_hot, i * 2 + half + 1)
                    for q in range(CH):
                        last = pe.matmul(acc[:, q // PER, 0:BOTH], g.ones16[0:EP, :],
                                         hot[:, half, q, :], start=False, stop=True,
                                         skip_group_check=True)
                    last.then_inc(s_hot_free, 1)

    tot_b, tot_c = sb("tot_b", [P, CHAINS, NBUCK2]), sb("tot_c", [P, CHAINS, NCELL])
    start = sb("start", [P, CHAINS, BOTH])
    start_b, start_c = start[:, :, 0:NBUCK2], start[:, :, NBUCK2:BOTH]
    cum_b, cum_c = sb("cum_b", [P, NBUCK2]), sb("cum_c", [P, NCELL])
    t_i = sb("t_i", [P, NBUCK2], I32)
    ones_b = sb("ones_b", [P, NBUCK2])
    count_b, count_a, count_c = sb("count_b", [P, NQ]), sb("count_a", [P, NQ]), sb("count_c", [P, NQC])
    count_i = sb("count_i", [P, 2, NQ], I32)
    count_ci = sb("count_ci", [P, NQC], I32)
    tab = TableBuffers(ones=ones_b, t_i=t_i, hit=sb("hit_b", [P, NBUCK2]))
    s_start, s_tabs, s_tab_out = sem("s_starts"), sem("s_tables"), sem("s_tables_out")
    s_dve_b = sem("s_dve_b")
    with nc.Block() as block:
        @block.vector
        def _(dve):
            st = Steps(dve, s_dve_b)
            st.add(dve.memset(ones_b[:, :], 1.0))
            st.add(dve.tensor_copy(tot_b[:, :, :], acc[:, :, 0:NBUCK2]))
            st.do(dve.tensor_copy(tot_c[:, :, :], acc[:, :, NBUCK2:BOTH]))
            bucket_starts(dve, st, tab, tot_b, start_b, cum_b, NBUCK2)
            bucket_starts(dve, st, tab, tot_c, start_c, cum_c, NCELL)
            dve.sem_inc(s_start, 1)
            for q in range(NQ):
                st.do(dve.tensor_scalar(tab.hit[:, 0:NBUCK], cum_b[:, 0:NBUCK], g.nodecol[:, q:q + 1], None,
                                        ALU.is_le, ALU.add, accum_out=count_b[:, q:q + 1]))
                st.do(dve.tensor_scalar(tab.hit[:, 0:NA], cum_b[:, ND - 1:NBUCK:ND], g.nodecol[:, q:q + 1],
                                        None, ALU.is_le, ALU.add, accum_out=count_a[:, q:q + 1]))
            st.do(dve.tensor_scalar(count_b[:, :], count_b[:, :], float(NBUCK - 1), None, ALU.min))
            st.do(dve.tensor_scalar(count_a[:, :], count_a[:, :], float(NA - 1), None, ALU.min))
            st.do(dve.tensor_copy(count_i[:, 0, :], count_a[:, :]))
            st.do(dve.scalar_tensor_tensor(count_i[:, 1, :], count_a[:, :], -float(ND), count_b[:, :],
                                           ALU.mult, ALU.add))
            cell_table(dve, st, g, tab, cum_c, count_c, count_ci)
            dve.sem_inc(s_tabs, 1)

        @block.tensor
        def _(pe):
            pe.wait_ge(s_start, 1)
            for ch in range(CHAINS):
                pe.matmul(acc[:, ch, 0:BOTH], g.onesf[:, :], start[0:1, ch, :], start=True, stop=True)

        @block.sync
        def _(sp):
            sp.wait_ge(s_tabs, 1)
            with nc.allow_non_contiguous_dma(reason="small tables"):
                sp.dma_start(g.tab_b.rearrange("k (q p) -> p k q", p=P), count_i[:, :, :]).then_inc(s_tab_out, 16)
                sp.dma_start(g.tab_c1[0, :].rearrange("(q p) -> p q", p=P), count_ci[:, :]).then_inc(s_tab_out, 16)
            sp.wait_ge(s_tab_out, 32)
            sp.dma_start(g.table_b[0:1, :, :], g.tab_b.rearrange("(o k) n -> o k n", o=1)).then_inc(s_tab_out, 16)
            sp.wait_ge(s_tab_out, 48)
            sp.wait_ge(s_fill, 16 * (32 + 96 + 48 + H + F))

    place = sb("place", [EP, 2, CH])
    place_i, low_i, high_i = (sb(n, [EP, 2, CH], I32) for n in ("place_i", "low_i", "high_i"))
    hit = sb("hit", [EP, CHAINS, BOTH], BF16)
    row_stage = sb("row_stage", [EP, 2, CH, EDGE_W])
    idx_stage = sb("idx_stage", [EP, 2, CH], U32)
    s_hot2, s_pe_done = sem("s_hot2"), sem("s_hot2_free")
    s_before = [sem(f"s_before{j}") for j in range(2)]
    s_read = [sem(f"s_read{j}") for j in range(2)]
    s_rows, s_sent = sem("s_rows_ready"), [sem(f"s_rows_sent{j}") for j in range(2)]
    s_dve_c, s_tick = sem("s_dve_c"), sem("s_pool_turns")
    STEPS_C = 6
    with nc.Block() as block:
        @block.vector
        def _(dve):
            for j in range(2):
                dve.sem_inc(s_read[j], 1)
            dve.memset(row_stage[:, :, :, :], 0.0).then_inc(s_dve_c, 1)
            dve.wait_ge(s_dve_c, 1)
            with dve.Fori(0, LOOP) as i:
                for half in range(2):
                    st = Steps(dve, s_dve_c, i * (2 * STEPS_C) + half * STEPS_C + 1)
                    k = i * 2 + half
                    dve.wait_ge(s_pe_done, k + 1)
                    bucket_hots(dve, k, half)
                    cell_hots(dve, k, half).then_inc(s_hot2, 1)
                    dve.wait_ge(s_hot2, k + 1)
                    for step in range(PER):
                        for j in range(2):
                            dve.wait_ge(s_before[j], k * PER + step + 1)
                            dve.wait_ge(s_read[j], k * PER + step + 1)
                            for ch in (2 * j, 2 * j + 1):
                                q = ch * PER + step
                                dve.scalar_tensor_tensor(
                                    hit[:, ch, 0:NBUCK2], hot[:, half, q, 0:NBUCK2], 1.0, acc[0:EP, ch, 0:NBUCK2],
                                    ALU.mult, ALU.mult, accum_out=place[:, 0, q:q + 1])
                                last = dve.scalar_tensor_tensor(
                                    hit[:, ch, NBUCK2:BOTH], hot[:, half, q, NBUCK2:BOTH], 1.0,
                                    acc[0:EP, ch, NBUCK2:BOTH],
                                    ALU.mult, ALU.mult, accum_out=place[:, 1, q:q + 1])
                            last.then_inc(s_read[j], 1)
                    dve.wait_ge(s_sent[half], i * (CH * 16) + 16)
                    for j in range(2):
                        dve.wait_ge(s_read[j], (k + 1) * PER + 1)
                    st.do(dve.tensor_copy(place_i[:, :, :], place[:, :, :]))
                    st.add(dve.tensor_scalar(low_i[:, :, :], place_i[:, :, :], P - 1, None, ALU.bitwise_and))
                    st.do(dve.tensor_scalar(high_i[:, :, :], place_i[:, :, :], 7, None, ALU.logical_shift_right))
                    st.add(dve.scalar_tensor_tensor(idx_stage[:, half, :], low_i[:, 0, :], float(NT),
                                                    high_i[:, 0, :], ALU.mult, ALU.add))
                    st.add(dve.scalar_tensor_tensor(row_stage[:, half, :, 7], low_i[:, 0, :], float(NT),
                                                    high_i[:, 0, :], ALU.mult, ALU.add))
                    st.add(dve.scalar_tensor_tensor(row_stage[:, half, :, 6], low_i[:, 1, :], float(NTC),
                                                    high_i[:, 1, :], ALU.mult, ALU.add))
                    for ch in range(CHAINS):
                        last = dve.tensor_copy(row_stage[:, half, ch * PER:(ch + 1) * PER, 0:6],
                                               edge[:, ds(ch * chain_len + k * PER, PER), :])
                    last.then_inc(s_rows, 1)
                    assert st.n == STEPS_C

        @block.tensor
        def _(pe):
            pe.sem_inc(s_pe_done, 2)
            with pe.Fori(0, LOOP) as i:
                for half in range(2):
                    k = i * 2 + half
                    pe.wait_ge(s_hot2, k + 1)

                    def add_up(j, step, matrix):
                        for ch in (2 * j, 2 * j + 1):
                            q = ch * PER + step
                            last = pe.matmul(acc[:, ch, 0:BOTH], matrix[0:EP, :], hot[:, half, q, :],
                                             start=False, stop=True, skip_group_check=True)
                        return last

                    for j in range(2):
                        add_up(j, 0, g.before).then_inc(s_before[j], 1)
                    for step in range(PER):
                        for j in range(2):
                            pe.wait_ge(s_read[j], k * PER + step + 2)
                            last = add_up(j, step, g.from_on)
                            if step + 1 < PER:
                                add_up(j, step + 1, g.before).then_inc(s_before[j], 1)
                    last.then_inc(s_pe_done, 1)

        @block.gpsimd
        def _(pool):
            g.open_sent(pool, s_sent)
            with pool.Fori(0, LOOP) as i:
                for half in range(2):
                    pool.wait_ge(s_rows, i * 2 + half + 1)
                    pool.sem_inc(s_tick, 1)
                    for q in range(CH):
                        pool.indirect_dma_start(
                            g.edges_b, bass.IndirectOffsetOnAxis(idx_stage[:, half, q:q + 1], 0),
                            row_stage[:, half, q, :], None,
                            bounds_check=P * NT - 1, oob_is_err=False).then_inc(s_sent[half], 16)
            for half in range(2):
                pool.wait_ge(s_sent[half], LOOP * CH * 16 + 16)


def bucket_starts(dve, st, tab, tot, start, cum, n):
    count = tab.hit[:, 0:n]
    st.do(dve.tensor_tensor(count, tot[:, 0, :], tot[:, 1, :], ALU.add))
    for ch in range(2, CHAINS):
        st.do(dve.tensor_tensor(count, count, tot[:, ch, :], ALU.add))
    st.do(dve.tensor_scalar(tab.t_i[:, 0:n], count, float(P - 1), None, ALU.add))
    st.do(dve.tensor_scalar(tab.t_i[:, 0:n], tab.t_i[:, 0:n], 7, None, ALU.logical_shift_right))
    st.do(dve.tensor_copy(count, tab.t_i[:, 0:n]))
    st.do(dve.tensor_tensor_scan(cum[:, :], tab.ones[:, 0:n], count, 0.0, ALU.mult, ALU.add))
    st.do(dve.tensor_tensor(start[:, 0, :], cum[:, :], count, ALU.subtract))
    st.do(dve.tensor_scalar(start[:, 0, :], start[:, 0, :], float(P), None, ALU.mult))
    for ch in range(1, CHAINS):
        st.do(dve.tensor_tensor(start[:, ch, :], start[:, ch - 1, :], tot[:, ch - 1, :], ALU.add))


def cell_table(dve, st, g, tab, cum, count, count_i):
    for q in range(NQC):
        st.do(dve.tensor_scalar(tab.hit[:, 0:NCELL], cum[:, :], g.nodecol[:, q:q + 1], None,
                                ALU.is_le, ALU.add, accum_out=count[:, q:q + 1]))
    st.do(dve.tensor_scalar(count[:, :], count[:, :], float(NCELL - 1), None, ALU.min))
    hi = tab.t_i[:, 0:NQC]
    st.do(dve.tensor_copy(count_i[:, :], count[:, :]))
    st.do(dve.tensor_scalar(hi, count_i[:, :], 2, None, ALU.logical_shift_right))
    st.do(dve.tensor_tensor(count[:, :], count[:, :], hi, ALU.add))
    st.do(dve.tensor_scalar(hi, count_i[:, :], 4, None, ALU.logical_shift_right))
    st.do(dve.scalar_tensor_tensor(count_i[:, :], hi, 5.0, count[:, :], ALU.mult, ALU.add))


def elu_nodes(dve, st, z, e, exp):
    st.do(dve.tensor_scalar(e, z, 0.0, None, ALU.min))
    exp()
    st.do(dve.tensor_scalar(e, e, -1.0, None, ALU.add))
    st.do(dve.scalar_tensor_tensor(z, z, 0.0, e, ALU.max, ALU.add))


def degree_and_first_conv(g, c, stn1_w, stn1_b):
    nc, sem = g.nc, g.sem
    sb = lambda n, s, d=F32: g.sb(n, s, d, c)
    KB = K3 + 1
    sums = sb("basis_sums", [P, 2, NBLK * P])
    w1x = sb("w1x", [KB, H + 1])
    b1v = sb("b1v", [P, H])
    loop_bufs = ExitStack()
    sbl = lambda n, s, d=F32: g.sb(n, s, d, loop_bufs)
    HALF = CH // 2
    hot = sbl("src_hot", [P, HALF, SRC_SB])
    basis = sbl("basis", [P, CH, KB])
    coord = sbl("coord", [P, CH, 3])
    ramp, hats = sbl("ramp", [P, CH * 3, KS + 1]), sbl("hats", [P, CH * 3, KS])
    outer = sbl("outer", [P, CH, KS * KS])
    rows16 = sbl("rows16", [P, 2, P], F16)
    s_pool_turns = sem("s_pool_turns_d")
    s_edges, s_w, s_dve, s_pool = sem("s_edges"), sem("s_w1"), sem("s_dve_d"), sem("s_pool_d")
    s_tr, s_tr16, s_rows_out = sem("s_transposed"), sem("s_rows16"), sem("s_rows_out")
    s_hot, s_basis, s_prod, s_added = sem("s_src_hot"), sem("s_basis"), sem("s_basis_prod"), sem("s_basis_added")
    LOOP = NCHK_B // 2
    QUART = CH // 4
    OPEN = CH + QUART
    with ExitStack() as c_ps:
        ptr = c_ps.enter_context(nc.psum_tensor("ptr", [P, 2, 512], F32))
        pprod = c_ps.enter_context(nc.psum_tensor("pprod", [P, 4, 512], F32))
        with nc.Block() as block:
            @block.sync
            def _(sp):
                sp.dma_start(g.edges[:, :, :], g.edges_b.rearrange("(p t) w -> p t w", p=P)).then_inc(s_edges, 16)
                sp.dma_start(w1x[0:K3, 0:H], stn1_w.rearrange("k o f -> k (o f)")).then_inc(s_w, 16)
                sp.dma_start(b1v[:, :], stn1_b.rearrange("(o f) -> o f", o=1).to_broadcast([P, H])).then_inc(s_w, 16)
                for m in range(2 * NQ):
                    q, kind = m // 2, m % 2
                    n = min(P, NT - q * P)
                    sp.wait_ge(s_tr16, m + 1)
                    sp.dma_start(g.local_rows[kind, q * P:q * P + n, :], rows16[0:n, m % 2, :]).then_inc(s_rows_out, 16)
                    sp.wait_ge(s_rows_out, (m + 1) * 16)
                sp.wait_ge(s_w, 32)

            @block.scalar
            def _(act):
                for m in range(2 * NQ):
                    n = min(P, NT - m // 2 * P)
                    act.wait_ge(s_tr, m + 1)
                    if m >= 2:
                        act.wait_ge(s_rows_out, (m - 1) * 16)
                    act.activation(rows16[0:n, m % 2, :], ptr[0:n, m % 2, 0:P], ACT.Copy).then_inc(s_tr16, 1)

            @block.gpsimd
            def _(pool):
                st = Steps(pool, s_pool)
                st.add(pool.memset(ramp[:, :, 0:1], 1.0))
                st.add(pool.memset(ramp[:, :, KS:KS + 1], 0.0))
                st.do(pool.memset(basis[:, :, K3:KB], 1.0))
                pool.wait_ge(s_edges, 16)
                BASE, S = 3, 10
                assert st.n == BASE

                with pool.Fori(0, LOOP) as i:
                    for half in range(2):
                        k = i * 2 + half
                        st = Steps(pool, s_pool, i * (2 * S) + half * S + BASE, s_pool_turns)
                        st.do(pool.tensor_copy(coord[:, :, :], g.edges[:, ds(k * CH, CH), 2:5]))
                        p1 = coord[:, :, :].rearrange("p t d -> p (t d)")
                        st.add(pool.tensor_scalar(ramp[:, :, 1], p1, float(KS - 1), 1.0, ALU.mult, ALU.min))
                        for n in (2, 3, 4):
                            st.add(pool.tensor_scalar(ramp[:, :, n], p1, float(KS - 1), 1.0 - n, ALU.mult, ALU.add))
                        st.wait()
                        for n in (2, 3):
                            st.add(pool.tensor_scalar(ramp[:, :, n], ramp[:, :, n], 1.0, 0.0, ALU.min, ALU.max))
                        st.do(pool.tensor_scalar(ramp[:, :, 4], ramp[:, :, 4], 0.0, None, ALU.max))
                        hat = hats[:, :, :].rearrange("p (t d) k -> p t d k", d=3)
                        st.do(pool.tensor_tensor(hats[:, :, :], ramp[:, :, 0:KS], ramp[:, :, 1:KS + 1], ALU.subtract))
                        st.do(pool.tensor_tensor(
                            outer[:, :, :].rearrange("p t (a b) -> p t a b", a=KS),
                            hat[:, :, 0, :].unsqueeze(3).to_broadcast([P, CH, KS, KS]),
                            hat[:, :, 1, :].unsqueeze(2).to_broadcast([P, CH, KS, KS]), ALU.mult))
                        for e in range(2):
                            at = slice(e * HALF, (e + 1) * HALF)
                            pool.wait_ge(s_prod, i * 8 + (half * 4 + e * 2 + 2))
                            pool.sem_inc(s_pool_turns, 1)
                            pool.tensor_tensor(
                                basis[:, at, 0:K3].rearrange("p t (a b) -> p t a b", b=KS),
                                outer[:, at, :].unsqueeze(3).to_broadcast([P, HALF, KS * KS, KS]),
                                hat[:, at, 2, :].unsqueeze(2).to_broadcast([P, HALF, KS * KS, KS]),
                                ALU.mult).then_inc(s_basis, 1)
                        pool.wait_ge(s_basis, k * 2 + 2)
                        assert st.n == S

            @block.vector
            def _(dve):
                st = Steps(dve, s_dve)
                st.do(dve.memset(sums[:, :, :], 0.0))
                dve.wait_ge(s_edges, 16)
                dve.sem_inc(s_added, OPEN)
                dve.sem_inc(s_prod, 4)

                def node_hots(k, n):
                    for q in range(n * QUART, (n + 1) * QUART):
                        last = dve.tensor_scalar(hot[:, q % HALF, :], g.iotaf[:, 0:SRC_SB],
                                                 g.edges[:, ds(k * CH + q, 1), 0:1].rearrange("p a b -> p (a b)"),
                                                 None, ALU.is_equal)
                    last.then_inc(s_hot, 1)

                def two_chunks(i, more):
                    for half in range(2):
                        k = i * 2 + half
                        src_sb = load_values(nc, DVE, g.table_b[0:1, 0, ds(k * CH, CH)], NA - 1)
                        for n in range(4):
                            if n < 3:
                                node_hots(k, n + 1)
                            elif half == 0 or more:
                                node_hots(k + 1, 0)
                            dve.wait_ge(s_prod, k * 4 + n + 5)
                            for q in range(n * QUART, (n + 1) * QUART):
                                dve.wait_ge(s_added, k * CH + (q + OPEN - 1))
                                part = sums[0:KB, q % 2, ds(src_sb[q] * SRC_SB, SRC_SB)]
                                dve.tensor_tensor(part, part, pprod[0:KB, q // 2 % 4, q % 2 * SRC_SB:(q % 2 + 1) * SRC_SB],
                                                  ALU.add).then_inc(s_added, 1)

                node_hots(0, 0)
                with dve.Fori(0, LOOP - 1) as i:
                    two_chunks(i, True)
                two_chunks(LOOP - 1, False)

            @block.tensor
            def _(pe):
                pe.wait_ge(s_edges, 16)
                for m in range(2 * NQ):
                    q, kind = m // 2, m % 2
                    n = min(P, NT - q * P)
                    if m >= 2:
                        pe.wait_ge(s_tr16, m - 1)
                    pe.transpose(ptr[0:n, m % 2, 0:P], g.edges[:, q * P:q * P + n, kind], g.ident[:, :]).then_inc(s_tr, 1)
                with pe.Fori(0, LOOP) as i:
                    for half in range(2):
                        k = i * 2 + half
                        for q in range(CH):
                            if q % HALF == 0:
                                pe.wait_ge(s_basis, k * 2 + q // HALF + 1)
                            if q % QUART == 0:
                                pe.wait_ge(s_hot, k * 4 + q // QUART + 1)
                                pe.wait_ge(s_added, k * CH + (q + OPEN - QUART))
                            last = pe.matmul(pprod[0:KB, q // 2 % 4, q % 2 * SRC_SB:(q % 2 + 1) * SRC_SB], basis[:, q, :], hot[:, q % HALF, :],
                                             start=True, stop=True)
                            if q % QUART == QUART - 1:
                                last.then_inc(s_prod, 1)

    loop_bufs.close()
    z = sb("z1", [P, NBLK, H + 1])
    e1 = sums[:, 0, 0:NBLK * H].rearrange("p (b f) -> p b f", f=H)
    w1d = sb("w1d", [KB, H + 1])
    s_dve2, s_w1x, s_node, s_min, s_exp = sem("s_dve_e"), sem("s_w1x"), sem("s_node1"), sem("s_min1"), sem("s_exp1")
    BANK_BLKS = 512 // (H + 1)
    with ExitStack() as c_ps:
        pn = c_ps.enter_context(nc.psum_tensor("pn1", [P, 8, 512], F32))
        with nc.Block() as block:
            @block.vector
            def _(dve):
                st = Steps(dve, s_dve2)
                st.do(dve.memset(w1d[:, :], 0.0))
                st.add(dve.tensor_copy(w1d[0:K3, 0:H], w1x[0:K3, 0:H]))
                st.do(dve.tensor_scalar(w1d[:, H:H + 1], g.nodecol[0:KB, 0:1], float(K3), None, ALU.is_equal))
                dve.sem_inc(s_w1x, 1)
                dve.wait_ge(s_node, 1)
                for b0 in range(0, NBLK, BANK_BLKS):
                    n = min(BANK_BLKS, NBLK - b0)
                    st.do(dve.tensor_copy(z[:, b0:b0 + n, :],
                                          pn[:, b0 // BANK_BLKS, 0:n * (H + 1)].rearrange("p (b f) -> p b f", f=H + 1)))
                st.do(dve.tensor_scalar(g.rdeg[:, :], z[:, :, H], 1.0, None, ALU.max))
                st.do(dve.reciprocal(g.rdeg[:, :], g.rdeg[:, :]))
                zz = z[:, :, 0:H]
                st.do(dve.tensor_tensor(zz, zz, g.rdeg[:, :].unsqueeze(2).to_broadcast([P, NBLK, H]), ALU.mult))
                st.do(dve.tensor_tensor(zz, zz, b1v[:, :].unsqueeze(1).to_broadcast([P, NBLK, H]), ALU.add))

                def exp():
                    dve.sem_inc(s_min, 1)
                    dve.wait_ge(s_exp, 1)
                elu_nodes(dve, st, zz, e1[:, :, :], exp)
                split_parts(dve, st, [g.h1parts[:, :, k, :] for k in range(3)], zz, e1[:, :, :])

            @block.scalar
            def _(act):
                act.wait_ge(s_min, 1)
                act.activation(e1[:, :, :], e1[:, :, :], ACT.Exp).then_inc(s_exp, 1)

            @block.tensor
            def _(pe):
                pe.wait_ge(s_w1x, 1)
                for b in range(NBLK):
                    at = b % BANK_BLKS * (H + 1)
                    for n in range(2):
                        last = pe.matmul(pn[:, b // BANK_BLKS, at:at + H + 1], sums[0:KB, n, b * P:(b + 1) * P],
                                         w1d[:, :], start=(n == 0), stop=(n == 1))
                last.then_inc(s_node, 1)


def to_cells_1(g, c):
    nc, sem = g.nc, g.sem
    sb = lambda n, s, d=F32: g.sb(n, s, d, c)
    NJ = DST_SB // P
    rows = sb("dst_rows", [P, 2, CH * P], F16)
    hot = sb("dst_hot", [P, 2, NJ, CH * P], BF16)
    stage = sb("c1_stage", [P, 2, CH, C1_W])
    idx = sb("c1_idx", [P, 2, CH], U32)
    pos, base = sb("c1_pos", [P, CH, 3]), sb("c1_base", [P, CH, 3])
    s_row, s_row_free = [sem(f"s_dst_rows{h}") for h in range(2)], sem("s_dst_rows_free")
    s_hot, s_gat, s_out = sem("s_dst_hot"), sem("s_gathered"), sem("s_gathered_out")
    s_pair, s_rest, s_sent = sem("s_gathered_pair"), sem("s_c1_rest"), [sem(f"s_c1_sent{h}") for h in range(2)]
    s_dve, s_tick = sem("s_dve_f"), sem("s_pool_turns_f")
    LOOP = NCHK_B // 2
    PAIRS = CH // 2
    pg = c.enter_context(nc.psum_tensor("pg1", [P, PAIRS, 512], F32))
    with nc.Block() as block:
        @block.sync
        def _(sp):
            with sp.Fori(0, LOOP) as i:
                for half in range(2):
                    k = i * 2 + half
                    sp.wait_ge(s_row_free, k + 1)
                    sp.dma_start(rows[:, half, :],
                                 g.local_rows[1:2, ds(k * CH, CH), :].rearrange("o t e -> o (t e)")
                                 .to_broadcast([P, CH * P])).then_inc(s_row[half], 16)

        @block.vector
        def _(dve):
            dve.sem_inc(s_row_free, 2)
            S = 5
            with dve.Fori(0, LOOP) as i:
                for half in range(2):
                    k = i * 2 + half
                    st = Steps(dve, s_dve, i * (2 * S) + half * S)
                    dve.wait_ge(s_row[half], i * 16 + 16)
                    dve.wait_ge(s_gat, k + 1)
                    for j in range(NJ):
                        last = dve.tensor_scalar(hot[:, half, j, :], rows[:, half, :], g.nodecol[:, j:j + 1],
                                                 None, ALU.is_equal)
                    last.then_inc(s_hot, 1)
                    dve.wait_ge(s_hot, k + 1)
                    dve.sem_inc(s_row_free, 1)
                    st.do(dve.tensor_scalar(pos[:, :, :], g.edges[:, ds(k * CH, CH), 2:5], float(KS - 1), None, ALU.mult))
                    st.do(dve.tensor_scalar(base[:, :, :], pos[:, :, :], 1.0, None, ALU.is_ge))
                    for knot in (2.0, 3.0):
                        st.do(dve.scalar_tensor_tensor(base[:, :, :], pos[:, :, :], knot, base[:, :, :],
                                                       ALU.is_ge, ALU.add))
                    dve.wait_ge(s_sent[half], i * (CH * 16) + 16)
                    st.do(dve.tensor_tensor(stage[:, half, :, H:H + 3], pos[:, :, :], base[:, :, :], ALU.subtract))
                    dve.tensor_copy(stage[:, half, :, H + 3], g.edges[:, ds(k * CH, CH), 7])
                    dve.tensor_copy(idx[:, half, :], g.edges[:, ds(k * CH, CH), 6]).then_inc(s_rest, 1)
                    for pair in range(PAIRS):
                        dve.wait_ge(s_pair, k * PAIRS + pair + 1)
                        dve.tensor_reduce(stage[:, half, 2 * pair:2 * pair + 2, 0:H],
                                          pg[:, pair, 0:6 * H].rearrange("p (t k f) -> p t f k", k=3, f=H),
                                          AX, ALU.add).then_inc(s_out, 1)
                    assert st.n == S

        @block.tensor
        def _(pe):
            pe.sem_inc(s_gat, 2)
            pe.sem_inc(s_out, PAIRS)
            h1 = g.h1parts[:, :, :, :].rearrange("p b k f -> p (b k f)")
            with pe.Fori(0, LOOP) as i:
                for half in range(2):
                    k = i * 2 + half
                    dst_sb = load_values(nc, PE, g.table_b[0:1, 1, ds(k * CH, CH)], ND - 1)
                    pe.wait_ge(s_hot, k + 1)
                    for q in range(CH):
                        if q % 2 == 0:
                            pe.wait_ge(s_out, k * PAIRS + q // 2 + 1)
                        d = dst_sb[q]
                        for j in range(NJ):
                            last = pe.matmul(pg[:, q // 2, q % 2 * 3 * H:(q % 2 + 1) * 3 * H],
                                             hot[:, half, j, q * P:(q + 1) * P],
                                             h1[:, ds(d * (NJ * 3 * H) + j * 3 * H, 3 * H)],
                                             start=(j == 0), stop=(j == NJ - 1))
                        if q % 2:
                            last.then_inc(s_pair, 1)
                    pe.wait_ge(s_pair, (k + 1) * PAIRS)
                    pe.sem_inc(s_gat, 1)

        @block.gpsimd
        def _(pool):
            g.open_sent(pool, s_sent)
            with pool.Fori(0, LOOP) as i:
                for half in range(2):
                    k = i * 2 + half
                    pool.wait_ge(s_rest, k + 1)
                    pool.wait_ge(s_out, (k + 2) * PAIRS)
                    pool.sem_inc(s_tick, 1)
                    for q in range(CH):
                        pool.indirect_dma_start(g.rows_c1, bass.IndirectOffsetOnAxis(idx[:, half, q:q + 1], 0),
                                                stage[:, half, q, :], None, bounds_check=P * NTC - 1,
                                                oob_is_err=False).then_inc(s_sent[half], 16)
            for half in range(2):
                pool.wait_ge(s_sent[half], LOOP * CH * 16 + 16)


def cell_products(g, c, tag, rows_dram, tab_dram, msg_dram, w_dram, width):
    nc, sem = g.nc, g.sem
    sb = lambda n, s, d=F32: g.sb(f"{tag}x_{n}", s, d, c)
    sm = lambda n: sem(f"s_{tag}x_{n}")
    corners = [0, KS, KS * KS, KS * KS + KS]
    in_piece = P // width
    shifts, pieces = corners[:in_piece], corners[::in_piece]
    NP = len(pieces)
    KN = K3 - shifts[-1]
    W = width + 4
    HALF = CH // 2
    weights = sb("weights", [P, KN, width])
    rows = sb("rows", [P, 2, CH, W])
    two, four = sb("two", [P, 2, CH, 3, 2]), sb("four", [P, CH, 4])
    GR = 4
    scaled = sb("scaled", [P, 2, GR, 4, width])
    turned = sb("turned", [P, 4, NP * P])
    ends = sb("ends", [P, HALF, 2, width])
    stage = sb("stage", [P, 2, CH, width])
    idx = sb("idx", [P, 2, CH], U32)
    s_w, s_rows, s_rows_free = sm("w"), [sm(f"rows{h}") for h in range(2)], sm("rows_free")
    s_scaled, s_tr, s_turned, s_mm = sm("scaled"), sm("transposed"), sm("turned"), sm("products")
    s_read, s_msg, s_idx = sm("products_read"), sm("msg"), sm("idx")
    s_sent, s_dve, s_tick = [sm(f"sent{h}") for h in range(2)], sm("dve"), sm("turns")
    LOOP = NCHK_C // 2
    PAIRS = CH // 2
    OPEN = 3
    pt = c.enter_context(nc.psum_tensor(f"{tag}_pt", [P, 2, 512], F32))
    pm = c.enter_context(nc.psum_tensor(f"{tag}_pm", [P, 2, HALF, 2 * width], F32))
    with nc.Block() as block:
        @block.sync
        def _(sp):
            sp.dma_start(g.table_c[:, :], tab_dram).then_inc(s_w, 16)
            for n, shift in enumerate(shifts):
                sp.dma_start(weights[n * width:(n + 1) * width, :, :],
                             w_dram[shift:shift + KN, :, :].rearrange("k i o -> i k o")).then_inc(s_w, 16)
            view = rows_dram.rearrange("(p t) w -> p t w", p=P)
            with sp.Fori(0, LOOP) as i:
                for half in range(2):
                    k = i * 2 + half
                    sp.wait_ge(s_rows_free, k + 1)
                    sp.dma_start(rows[:, half, :, :], view[:, ds(k * CH, CH), :]).then_inc(s_rows[half], 16)

        @block.vector
        def _(dve):
            dve.sem_inc(s_rows_free, 2)
            S = 2

            def scale(i, u):
                half = u // 2 % 2
                if u % 2 == 0:
                    dve.wait_ge(s_rows[half], i * 16 + (u // 4 + 1) * 16)
                    st = Steps(dve, s_dve, i * (2 * S) + u // 2 * S)
                    frac = rows[:, half, :, width:width + 3]
                    dve.tensor_scalar(two[:, half, :, :, 0], frac, -1.0, 1.0, ALU.mult, ALU.add)
                    st.do(dve.tensor_copy(two[:, half, :, :, 1], frac))
                    st.do(dve.tensor_tensor(four[:, :, :].rearrange("p t (a b) -> p t a b", a=2),
                                            two[:, half, :, 0, :].unsqueeze(3).to_broadcast([P, CH, 2, 2]),
                                            two[:, half, :, 1, :].unsqueeze(2).to_broadcast([P, CH, 2, 2]), ALU.mult))
                    assert st.n == S
                for n in range(2):
                    gr = u % 2 * 2 + n
                    dve.wait_ge(s_tr, i * (2 * PAIRS) + (u * 4 + n * 2 + OPEN - 2))
                    at = slice(gr * GR, (gr + 1) * GR)
                    dve.tensor_tensor(scaled[:, n, :, :, :],
                                      rows[:, half, at, 0:width].unsqueeze(2).to_broadcast([P, GR, 4, width]),
                                      four[:, at, :].unsqueeze(3).to_broadcast([P, GR, 4, width]),
                                      ALU.mult).then_inc(s_scaled, 1)

            def messages(i, u):
                half, h = u // 2 % 2, u % 2
                at = slice(h * HALF, (h + 1) * HALF)
                if h == 0:
                    dve.wait_ge(s_sent[half], i * (CH * 16) + 16)
                    dve.tensor_copy(idx[:, half, :], rows[:, half, :, width + 3]).then_inc(s_idx, 1)
                dve.wait_ge(s_mm, i * 4 + (u + 1))
                dve.wait_ge(s_msg, i * 4 + (u + 1))
                dve.tensor_tensor(ends[:, :, :, :],
                                  pm[:, h, :, :].rearrange("p t (z f) -> p t z f", z=2),
                                  two[:, half, at, 2, :].unsqueeze(3).to_broadcast([P, HALF, 2, width]),
                                  ALU.mult).then_inc(s_read, 1)
                dve.wait_ge(s_read, i * 4 + (u + 3))
                dve.tensor_tensor(stage[:, half, at, :], ends[:, :, 0, :], ends[:, :, 1, :], ALU.add).then_inc(s_msg, 1)
                if h:
                    dve.wait_ge(s_msg, i * 4 + (u + 2))
                    dve.wait_ge(s_idx, i * 2 + (u // 2 + 1))
                    dve.sem_inc(s_rows_free, 1)

            def two_chunks(i, more):
                for u in range(4):
                    if u < 3 or more:
                        scale(i, u + 1)
                    messages(i, u)

            dve.sem_inc(s_msg, 1)
            dve.sem_inc(s_read, 2)
            scale(0, 0)
            with dve.Fori(0, LOOP - 1) as i:
                two_chunks(i, True)
            two_chunks(LOOP - 1, False)

        @block.tensor
        def _(pe):
            pe.wait_ge(s_w, 16 * (len(shifts) + 1))
            pe.sem_inc(s_tr, OPEN)
            pe.sem_inc(s_turned, 2)

            def transposes(i, m):
                if m % 2 == 0:
                    pe.wait_ge(s_scaled, i * (2 * CH // GR) + (m // 2 + 1))
                pe.wait_ge(s_turned, i * (2 * PAIRS) + (m + 1))
                for q in range(2 * m, 2 * m + 2):
                    flat = scaled[:, q // GR % 2, q % GR, :, :].rearrange("p s f -> p (s f)")
                    for n in range(NP):
                        at = (q % 2 * NP + n) * P
                        last = pe.transpose(pt[:, m % 2, at:at + P], flat[:, n * P:(n + 1) * P], g.ident[:, :])
                last.then_inc(s_tr, 1)

            def products(i, m, bases):
                u = m // (HALF // 2)
                if m % (HALF // 2) == 0:
                    pe.wait_ge(s_read, i * 4 + (u + 1))
                pe.wait_ge(s_turned, i * (2 * PAIRS) + (m + 3))
                for q in range(2 * m, 2 * m + 2):
                    for n, piece in enumerate(pieces):
                        last = pe.matmul(pm[:, u % 2, q % HALF, :], turned[:, q % 4, n * P:(n + 1) * P],
                                         weights[:, ds(bases[q % CH] + piece, 2), :].rearrange("p a f -> p (a f)"),
                                         start=(n == 0), stop=(n == NP - 1))
                if m % (HALF // 2) == HALF // 2 - 1:
                    last.then_inc(s_mm, 1)

            def two_chunks(i, more):
                for m in range(2 * PAIRS):
                    if m % PAIRS == 0:
                        bases = load_values(nc, PE, g.table_c[0:1, ds(i * (2 * CH) + m * 2, CH)], KN - 2 - pieces[-1])
                    if m + 1 < 2 * PAIRS or more:
                        transposes(i, m + 1)
                    products(i, m, bases)

            transposes(0, 0)
            with pe.Fori(0, LOOP - 1) as i:
                two_chunks(i, True)
            two_chunks(LOOP - 1, False)

        @block.scalar
        def _(act):
            with act.Fori(0, LOOP) as i:
                for m in range(2 * PAIRS):
                    at = slice(m % 2 * 2, m % 2 * 2 + 2)
                    act.wait_ge(s_tr, i * (2 * PAIRS) + (m + 1 + OPEN))
                    act.activation(turned[:, at, :], pt[:, m % 2, 0:2 * NP * P].rearrange("p (t n) -> p t n", t=2),
                                   ACT.Copy).then_inc(s_turned, 1)

        @block.gpsimd
        def _(pool):
            g.open_sent(pool, s_sent)
            with pool.Fori(0, LOOP) as i:
                for half in range(2):
                    k = i * 2 + half
                    pool.wait_ge(s_idx, k + 1)
                    pool.wait_ge(s_msg, k * 2 + 3)
                    pool.sem_inc(s_tick, 1)
                    for q in range(CH):
                        pool.indirect_dma_start(msg_dram, bass.IndirectOffsetOnAxis(idx[:, half, q:q + 1], 0),
                                                stage[:, half, q, :], None, bounds_check=P * NT - 1,
                                                oob_is_err=False).then_inc(s_sent[half], 16)
            for half in range(2):
                pool.wait_ge(s_sent[half], LOOP * CH * 16 + 16)


def add_up_by_source(g, c, tag, msg_dram, width, acc):
    nc, sem = g.nc, g.sem
    sb = lambda n, s, d=F32: g.sb(f"{tag}x_{n}", s, d, c)
    sm = lambda n: sem(f"s_{tag}x_{n}")
    msg = sb("msg", [P, 2, CH, width])
    parts = sb("parts", [P, 2, 3, CH, width], BF16)
    hot = sb("hot", [P, 2, CH, SRC_SB], BF16)
    s_in, s_hot, s_used = [sm(f"in{h}") for h in range(2)], sm("hot"), sm("used")
    s_high, s_rest, s_mid, s_low, s_tick = sm("high"), sm("rest"), sm("mid"), sm("low"), sm("turns")
    LOOP = NCHK_B // 2
    NJ = SRC_SB // P
    with nc.Block() as block:
        @block.sync
        def _(sp):
            view = msg_dram.rearrange("(p t) w -> p t w", p=P)
            with sp.Fori(0, LOOP) as i:
                for half in range(2):
                    k = i * 2 + half
                    sp.wait_ge(s_low, k + 1)
                    sp.dma_start(msg[:, half, :, :], view[:, ds(k * CH, CH), :]).then_inc(s_in[half], 16)

        @block.vector
        def _(dve):
            with dve.Fori(0, LOOP) as i:
                for half in range(2):
                    k = i * 2 + half
                    dve.wait_ge(s_used, k + 1)
                    for q in range(CH):
                        last = dve.tensor_scalar(hot[:, half, q, :], g.iota16[:, 0:SRC_SB],
                                                 g.edges[:, ds(k * CH + q, 1), 0:1].rearrange("p a b -> p (a b)"),
                                                 None, ALU.is_equal)
                        if q % 4 == 3:
                            last.then_inc(s_hot, 1)

        @block.scalar
        def _(act):
            with act.Fori(0, LOOP) as i:
                for half in range(2):
                    k = i * 2 + half
                    act.wait_ge(s_in[half], i * 16 + 16)
                    act.wait_ge(s_used, k + 1)
                    act.activation(parts[:, half, 0, :, :], msg[:, half, :, :], ACT.Copy).then_inc(s_high, 1)
                    act.wait_ge(s_rest, k + 1)
                    act.activation(parts[:, half, 1, :, :], msg[:, half, :, :], ACT.Copy).then_inc(s_mid, 1)

        @block.gpsimd
        def _(pool):
            pool.sem_inc(s_low, 2)
            with pool.Fori(0, LOOP) as i:
                for half in range(2):
                    k = i * 2 + half
                    pool.wait_ge(s_high, k + 1)
                    pool.sem_inc(s_tick, 1)
                    pool.tensor_tensor(msg[:, half, :, :], msg[:, half, :, :], parts[:, half, 0, :, :],
                                       ALU.subtract).then_inc(s_rest, 1)
                    pool.wait_ge(s_mid, k + 1)
                    pool.sem_inc(s_tick, 1)
                    pool.tensor_tensor(parts[:, half, 2, :, :], msg[:, half, :, :], parts[:, half, 1, :, :],
                                       ALU.subtract).then_inc(s_low, 1)

        @block.tensor
        def _(pe):
            for b0 in range(0, NBLK * width, 512):
                n = min(512, NBLK * width - b0)
                pe.matmul(acc[:, b0:b0 + n], g.ident[:, :], g.zero512[:, 0:n], start=True, stop=True)
            pe.sem_inc(s_used, 2)
            with pe.Fori(0, LOOP) as i:
                for half in range(2):
                    k = i * 2 + half
                    src_sb = load_values(nc, PE, g.table_b[0:1, 0, ds(k * CH, CH)], NA - 1)
                    pe.wait_ge(s_low, k + 3)
                    for q in range(CH):
                        if q % 4 == 0:
                            pe.wait_ge(s_hot, k * 4 + q // 4 + 1)
                        a = src_sb[q]
                        for j in range(NJ):
                            for part in range(3):
                                last = pe.matmul(acc[:, ds(a * (NJ * width) + j * width, width)],
                                                 hot[:, half, q, j * P:(j + 1) * P], parts[:, half, part, q, :],
                                                 start=False, stop=True, skip_group_check=True)
                    last.then_inc(s_used, 1)


def shift_network(g, c, stn2_b, stn3_w, stn3_b, stn4_w, stn4_b):
    nc, sem = g.nc, g.sem
    sb = lambda n, s, d=F32: g.sb(n, s, d, c)
    ph = sb("h2", [P, NBLK, H])
    with ExitStack() as c1:
        acc = c1.enter_context(nc.psum_tensor("acc_h2", [P, 7 * 512], F32))
        with ExitStack() as c2:
            add_up_by_source(g, c2, "r1", g.msg1, H, acc)
        e2, b2v = g.sb("e2", [P, NBLK, H], F32, c1), g.sb("b2v", [P, H], F32, c1)
        s_b, s_dve, s_min, s_exp = sem("s_b2"), sem("s_dve_g"), sem("s_min2"), sem("s_exp2")
        with nc.Block() as block:
            @block.sync
            def _(sp):
                sp.dma_start(b2v[:, :], stn2_b.rearrange("(o f) -> o f", o=1).to_broadcast([P, H])).then_inc(s_b, 16)

            @block.vector
            def _(dve):
                st = Steps(dve, s_dve)
                dve.wait_ge(s_b, 16)
                z = ph[:, :, :]
                st.do(dve.tensor_tensor(z, acc[:, 0:NBLK * H].rearrange("p (b f) -> p b f", f=H),
                                        g.rdeg[:, :].unsqueeze(2).to_broadcast([P, NBLK, H]), ALU.mult))
                st.do(dve.tensor_tensor(z, z, b2v[:, :].unsqueeze(1).to_broadcast([P, NBLK, H]), ALU.add))

                def exp():
                    dve.sem_inc(s_min, 1)
                    dve.wait_ge(s_exp, 1)
                elu_nodes(dve, st, z, e2[:, :, :], exp)

            @block.scalar
            def _(act):
                act.wait_ge(s_min, 1)
                act.activation(e2[:, :, :], e2[:, :, :], ACT.Exp).then_inc(s_exp, 1)

    NG = NBLK // 4
    hT, h3 = sb("h2T", [H, NBLK * P]), sb("h3", [H, NBLK * P])
    e3 = hT
    w3, b3, w4, b4 = sb("w3", [H, H]), sb("b3", [H, 1]), sb("w4", [H, 3]), sb("b4", [P, 3])
    t = sb("t", [P, NBLK, 3])
    rest = sb("t_rest", [P, NBLK, 3])
    s_w, s_tr, s_hT, s_d3, s_h3 = sem("s_w34"), sem("s_tr2"), sem("s_hT"), sem("s_dense3"), sem("s_h3pre")
    s_dve, s_min, s_exp, s_elu, s_t = sem("s_dve_h"), sem("s_min3"), sem("s_exp3"), sem("s_elu3"), sem("s_t")
    with ExitStack() as c1:
        pt = c1.enter_context(nc.psum_tensor("pt2", [P, 2, 512], F32))
        pd = c1.enter_context(nc.psum_tensor("pd2", [P, 2, 512], F32))
        pf = c1.enter_context(nc.psum_tensor("pf2", [P, 512], F32))
        with nc.Block() as block:
            @block.sync
            def _(sp):
                with nc.allow_non_contiguous_dma(reason="a bias column"):
                    sp.dma_start(b3[:, :], stn3_b.rearrange("(f o) -> f o", o=1)).then_inc(s_w, 16)
                sp.dma_start(w3[:, :], stn3_w).then_inc(s_w, 16)
                sp.dma_start(w4[:, :], stn4_w).then_inc(s_w, 16)
                sp.dma_start(b4[:, :], stn4_b.rearrange("(o f) -> o f", o=1).to_broadcast([P, 3])).then_inc(s_w, 16)

            @block.tensor
            def _(pe):
                pe.wait_ge(s_w, 64)

                def dense(n):
                    pe.wait_ge(s_hT, n + 1)
                    if n >= 2:
                        pe.wait_ge(s_h3, n - 1)
                    pe.matmul(pd[0:H, n % 2, :], w3[:, :], hT[:, n * 512:(n + 1) * 512], start=True,
                              stop=True).then_inc(s_d3, 1)
                for n in range(NG):
                    if n >= 2:
                        pe.wait_ge(s_hT, n - 1)
                    for b in range(4):
                        last = pe.transpose(pt[0:H, n % 2, b * P:(b + 1) * P], ph[:, n * 4 + b, :], g.ident[:, :])
                    last.then_inc(s_tr, 1)
                    if n:
                        dense(n - 1)
                dense(NG - 1)
                pe.wait_ge(s_elu, 1)
                for b in range(NBLK):
                    last = pe.matmul(pf[:, b * 3:(b + 1) * 3], h3[:, b * P:(b + 1) * P], w4[:, :], start=True, stop=True)
                last.then_inc(s_t, 1)

            @block.scalar
            def _(act):
                act.wait_ge(s_w, 64)
                for n in range(NG):
                    act.wait_ge(s_tr, n + 1)
                    act.activation(hT[:, n * 512:(n + 1) * 512], pt[0:H, n % 2, :], ACT.Copy).then_inc(s_hT, 1)
                    if n:
                        act.wait_ge(s_d3, n)
                        act.activation(h3[:, (n - 1) * 512:n * 512], pd[0:H, (n - 1) % 2, :], ACT.Identity,
                                       bias=b3[:, :]).then_inc(s_h3, 1)
                act.wait_ge(s_d3, NG)
                act.activation(h3[:, (NG - 1) * 512:NG * 512], pd[0:H, (NG - 1) % 2, :], ACT.Identity,
                               bias=b3[:, :]).then_inc(s_h3, 1)
                act.wait_ge(s_min, 1)
                act.activation(e3[:, :], e3[:, :], ACT.Exp).then_inc(s_exp, 1)

            @block.vector
            def _(dve):
                st = Steps(dve, s_dve)
                dve.wait_ge(s_w, 64)
                dve.wait_ge(s_h3, NG)

                def exp():
                    dve.sem_inc(s_min, 1)
                    dve.wait_ge(s_exp, 1)
                elu_nodes(dve, st, h3[:, :], e3[:, :], exp)
                dve.sem_inc(s_elu, 1)
                dve.wait_ge(s_t, 1)
                st.do(dve.tensor_tensor(t[:, :, :], pf[:, 0:NBLK * 3].rearrange("p (b f) -> p b f", f=3),
                                        b4[:, :].unsqueeze(1).to_broadcast([P, NBLK, 3]), ALU.add))
                split_parts(dve, st, [g.tparts[:, :, k, :] for k in range(3)], t[:, :, :], rest[:, :, :])
                st.do(dve.tensor_scalar(g.tparts_neg[:, :, :, :], g.tparts[:, :, :, :], -1.0, None, ALU.mult))


def to_cells_2(g, c):
    nc, sem = g.nc, g.sem
    sb = lambda n, s, d=F32: g.sb(n, s, d, c)
    NJD, NJS = DST_SB // P, SRC_SB // P
    LOOP = NCHK_B // 2
    rows = sb("both_rows", [P, 2, 2, CH * P], F16)
    hot_d = sb("hot_d", [P, NJD, CH * P], BF16)
    hot_s = sb("hot_s", [P, NJS, CH * P], BF16)
    frac, cell = sb("frac2", [P, NT, 3]), sb("cell2", [P, NT])
    pos, base = sb("pos2", [P, CH, 3]), sb("base2", [P, CH, 3])
    real, cl = sb("real", [P, CH]), sb("cl", [P, CH])
    hot_c = sb("hot_c2", [P, 2, CH, NCELL], F16)
    by_chain = g.edges[:, :, :].rearrange("p (c t) w -> p c t w", c=CHAINS)

    def chain_tiles(view, k):
        return view[:, :, ds(k * PER, PER)]

    def cell_hots(dve, k, half):
        shape = [P, CH, NCELL]
        return dve.tensor_tensor(hot_c[:, half, :, :], g.iota16[:, 0:NCELL].unsqueeze(1).to_broadcast(shape),
                                 cell[:, ds(k * CH, CH)].unsqueeze(2).to_broadcast(shape), ALU.is_equal)

    def load_rows(sp, k, half, s_row, kinds):
        for kind in kinds:
            sp.dma_start(rows[:, half, kind, :].rearrange("p (c n) -> p c n", c=CHAINS),
                         g.local_rows[kind:kind + 1, 0:NT, :].rearrange("o (c t) e -> o c (t e)", c=CHAINS)
                         [:, :, ds(k * (PER * P), PER * P)].to_broadcast([P, CHAINS, PER * P])).then_inc(s_row, 16)

    s_row, s_row_free = [sem(f"s_both_rows{h}") for h in range(2)], sem("s_both_rows_free")
    s_hot, s_gat, s_sum = sem("s_hot_ds"), sem("s_shift_read"), sem("s_shift_summed")
    s_hotc, s_dve = sem("s_hot_c2"), sem("s_dve_i")
    own_d, own_s = sb("own_d", [P, 2, CH, NJD * 9], BF16), sb("own_s", [P, 2, CH, NJS * 9], BF16)
    s_own_d, s_own_s, s_tick1 = sem("s_own_targets"), sem("s_own_sources"), sem("s_pool_turns_i")
    s_tab = sem("s_chain_tables")
    tparts, tparts_neg = (v[:, :, :, :].rearrange("p b k f -> p (b k f)") for v in (g.tparts, g.tparts_neg))
    hparts = g.hparts[:, :, :, :].rearrange("p b k f -> p (b k f)")
    with ExitStack() as c1:
        pdel = c1.enter_context(nc.psum_tensor("pdel", [P, CHAINS, 512], F32))
        pacc = c1.enter_context(nc.psum_tensor("pacc2", [P, 2, 512], F32))
        with nc.Block() as block:
            @block.sync
            def _(sp):
                with nc.allow_non_contiguous_dma(reason="four values at a time"):
                    for kind in range(2):
                        for ch in range(CHAINS):
                            sp.dma_start(g.table_b[0:1, kind, 0:NT].rearrange("o (k c s) -> o c k s", c=CHAINS, s=PER)[:, ch],
                                         g.tab_b[kind:kind + 1, 0:NT].rearrange("o (c k s) -> o c k s", c=CHAINS, s=PER)[:, ch]
                                         ).then_inc(s_tab, 16)
                with sp.Fori(0, LOOP) as i:
                    for half in range(2):
                        k = i * 2 + half
                        sp.wait_ge(s_row_free, k + 1)
                        load_rows(sp, k, half, s_row[half], (0, 1))

            @block.vector
            def _(dve):
                dve.sem_inc(s_row_free, 2)
                dve.sem_inc(s_sum, 2)
                dve.memset(hot_c[:, 1, :, :], 0.0).then_inc(s_hotc, 1)
                S = 12

                def node_hots(k, half, loads):
                    dve.wait_ge(s_row[half], loads * 32)
                    for j in range(NJD):
                        dve.tensor_scalar(hot_d[:, j, :], rows[:, half, 1, :], g.nodecol[:, j:j + 1], None, ALU.is_equal)
                    for j in range(NJS):
                        last = dve.tensor_scalar(hot_s[:, j, :], rows[:, half, 0, :], g.nodecol[:, j:j + 1], None, ALU.is_equal)
                    last.then_inc(s_hot, 1)

                def rows_read(k):
                    dve.wait_ge(s_hot, k + 1)
                    dve.sem_inc(s_row_free, 1)

                node_hots(0, 0, 1)
                rows_read(0)

                def two_chunks(i, more):
                    for half in range(2):
                        k = i * 2 + half
                        st = Steps(dve, s_dve, i * (2 * S) + half * S)
                        dve.wait_ge(s_gat, k + 3)
                        if half == 0:
                            node_hots(k + 1, 1, i + 1)
                        elif more:
                            node_hots(k + 1, 0, i + 2)
                        if half == 0 or more:
                            rows_read(k + 1)
                        st.do(dve.tensor_reduce(pos[:, :, :],
                                                pdel[:, half, 0:CH * 9].rearrange("p (t k f) -> p t f k", k=3, f=3),
                                                AX, ALU.add))
                        dve.sem_inc(s_sum, 1)
                        pos4 = pos[:, :, :].rearrange("p (c t) f -> p c t f", c=CHAINS)
                        st.do(dve.tensor_tensor(pos4, pos4, by_chain[:, :, ds(k * PER, PER), 2:5], ALU.add))
                        st.do(dve.tensor_scalar(pos[:, :, :], pos[:, :, :], 0.0, 1.0, ALU.max, ALU.min))
                        st.do(dve.tensor_scalar(pos[:, :, :], pos[:, :, :], float(KS - 1), None, ALU.mult))
                        st.do(dve.tensor_scalar(base[:, :, :], pos[:, :, :], 1.0, None, ALU.is_ge))
                        for knot in (2.0, 3.0):
                            st.do(dve.scalar_tensor_tensor(base[:, :, :], pos[:, :, :], knot, base[:, :, :], ALU.is_ge, ALU.add))
                        st.add(dve.tensor_tensor(frac[:, ds(k * CH, CH), :], pos[:, :, :], base[:, :, :], ALU.subtract))
                        st.do(dve.scalar_tensor_tensor(cl[:, :], base[:, :, 0], 4.0, base[:, :, 1], ALU.mult, ALU.add))
                        st.do(dve.scalar_tensor_tensor(cl[:, :], cl[:, :], 4.0, base[:, :, 2], ALU.mult, ALU.add))
                        st.do(dve.tensor_scalar(real[:, :].rearrange("p (c t) -> p c t", c=CHAINS),
                                                by_chain[:, :, ds(k * PER, PER), 0], 0.0, None, ALU.is_lt))
                        st.do(dve.scalar_tensor_tensor(cell[:, ds(k * CH, CH)], real[:, :], -1000.0, cl[:, :], ALU.mult, ALU.add))
                        cell_hots(dve, k, half).then_inc(s_hotc, 1)
                        assert st.n == S

                with dve.Fori(0, LOOP - 1) as i:
                    two_chunks(i, True)
                two_chunks(LOOP - 1, False)

            @block.scalar
            def _(act):
                act.wait_ge(s_tab, 2 * CHAINS * 16)
                with act.Fori(0, LOOP) as i:
                    for half in range(2):
                        k = i * 2 + half
                        dst_sb = load_values(nc, ACTE, g.table_b[0:1, 1, ds(k * CH, CH)], ND - 1)
                        act.wait_ge(s_gat, k + 1)
                        for q in range(CH):
                            last = act.activation(own_d[:, half, q, :], tparts[:, ds(dst_sb[q] * (NJD * 9), NJD * 9)], ACT.Copy)
                        last.then_inc(s_own_d, 1)

            @block.gpsimd
            def _(pool):
                def take_blocks(k, half):
                    src_sb = load_values(nc, POOL, g.table_b[0:1, 0, ds(k * CH, CH)], NA - 1)
                    for q in range(CH):
                        last = pool.tensor_copy(own_s[:, half, q, :], tparts_neg[:, ds(src_sb[q] * (NJS * 9), NJS * 9)])
                    last.then_inc(s_own_s, 1)

                pool.wait_ge(s_tab, 2 * CHAINS * 16)
                take_blocks(0, 0)
                with pool.Fori(0, LOOP) as i:
                    for half in range(2):
                        k = i * 2 + half
                        pool.wait_ge(s_gat, k + 2)
                        pool.sem_inc(s_tick1, 1)
                        take_blocks(k + 1, 1 - half)

            @block.tensor
            def _(pe):
                pe.matmul(pacc[:, 0, :], g.ident[:, :], g.zero512[:, :], start=True, stop=True)
                pe.sem_inc(s_gat, 2)
                with pe.Fori(0, LOOP) as i:
                    for half in range(2):
                        k = i * 2 + half
                        pe.wait_ge(s_own_d, k + 1)
                        pe.wait_ge(s_own_s, k + 1)
                        pe.wait_ge(s_hot, k + 1)
                        pe.wait_ge(s_sum, k + 1)
                        for q in range(CH):
                            at = pdel[:, half, q * 9:(q + 1) * 9]
                            for j in range(NJD):
                                pe.matmul(at, hot_d[:, j, q * P:(q + 1) * P], own_d[:, half, q, j * 9:(j + 1) * 9],
                                          start=(j == 0), stop=False)
                            for j in range(NJS):
                                last = pe.matmul(at, hot_s[:, j, q * P:(q + 1) * P],
                                                 own_s[:, half, q, j * 9:(j + 1) * 9],
                                                 start=False, stop=(j == NJS - 1))
                        last.then_inc(s_gat, 1)
                        pe.wait_ge(s_hotc, k + 1)
                        for q in range(CH):
                            ch = q // PER
                            pe.matmul(pacc[:, 0, ch * NCELL:(ch + 1) * NCELL], g.ones16[:, :], hot_c[:, 1 - half, q, :],
                                      start=False, stop=True, skip_group_check=True)
                pe.wait_ge(s_hotc, 2 * LOOP + 1)
                for q in range(CH):
                    ch = q // PER
                    pe.matmul(pacc[:, 0, ch * NCELL:(ch + 1) * NCELL], g.ones16[:, :], hot_c[:, 1, q, :],
                              start=False, stop=True, skip_group_check=True)

        tot, start = sb("tot2", [P, CHAINS, NCELL]), sb("start2", [P, CHAINS, NCELL])
        cum = sb("cum2", [P, NCELL])
        tab = TableBuffers(ones=sb("ones2", [P, NCELL]), t_i=sb("t_i2", [P, NCELL], I32), hit=sb("hit2", [P, NCELL]))
        count, count_i = sb("count2", [P, NQC]), sb("count_i2", [P, NQC], I32)
        s_start, s_tabs, s_tab_out, s_dve2 = sem("s_starts2"), sem("s_tables2"), sem("s_tables2_out"), sem("s_dve_j")
        with nc.Block() as block:
            @block.vector
            def _(dve):
                st = Steps(dve, s_dve2)
                st.add(dve.memset(tab.ones[:, :], 1.0))
                st.do(dve.tensor_copy(tot[:, :, :], pacc[:, 0, 0:CHAINS * NCELL].rearrange("p (c n) -> p c n", c=CHAINS)))
                bucket_starts(dve, st, tab, tot, start, cum, NCELL)
                dve.sem_inc(s_start, 1)
                cell_table(dve, st, g, tab, cum, count, count_i)
                dve.sem_inc(s_tabs, 1)

            @block.tensor
            def _(pe):
                pe.wait_ge(s_start, 1)
                for j in range(2):
                    pe.matmul(pacc[:, j, 0:2 * NCELL], g.onesf[:, :],
                              start[0:1, 2 * j:2 * j + 2, :].rearrange("p c n -> p (c n)"), start=True, stop=True)

            @block.sync
            def _(sp):
                sp.wait_ge(s_tabs, 1)
                with nc.allow_non_contiguous_dma(reason="small table"):
                    sp.dma_start(g.tab_c2[0, :].rearrange("(q p) -> p q", p=P), count_i[:, :]).then_inc(s_tab_out, 16)
                sp.wait_ge(s_tab_out, 16)

        place = sb("place2", [P, CH])
        place_i, low_i, high_i = (sb(n, [P, CH], I32) for n in ("place_i2", "low_i2", "high_i2"))
        skip = sb("skip2", [P, CH])
        hit = sb("hit_c2", [P, CHAINS, NCELL], BF16)
        stage, idx = sb("c2_stage", [P, 2, CH, C2_W]), sb("c2_idx", [P, 2, CH], U32)
        s_row2, s_row2_free = [sem(f"s_dst_rows2{h}") for h in range(2)], sem("s_dst_rows2_free")
        s_hot2, s_gat2, s_out2 = sem("s_dst_hot2"), sem("s_gathered2"), sem("s_gathered2_out")
        s_hotc2, s_ranked = sem("s_hot_c22"), sem("s_ranked2")
        s_before, s_read = [sem(f"s_before2{j}") for j in range(2)], [sem(f"s_read2{j}") for j in range(2)]
        s_rest, s_sent = sem("s_c2_rest"), [sem(f"s_c2_sent{h}") for h in range(2)]
        s_dve3, s_tick = sem("s_dve_k"), sem("s_pool_turns_k")
        with nc.Block() as block:
            @block.sync
            def _(sp):
                with sp.Fori(0, LOOP) as i:
                    for half in range(2):
                        k = i * 2 + half
                        sp.wait_ge(s_row2_free, k + 1)
                        load_rows(sp, k, half, s_row2[half], (1,))

            @block.vector
            def _(dve):
                dve.sem_inc(s_row2_free, 2)
                for j in range(2):
                    dve.sem_inc(s_read[j], 1)
                S = 5
                with dve.Fori(0, LOOP) as i:
                    for half in range(2):
                        k = i * 2 + half
                        st = Steps(dve, s_dve3, i * (2 * S) + half * S)
                        dve.wait_ge(s_ranked, k + 1)
                        cell_hots(dve, k, half).then_inc(s_hotc2, 1)
                        dve.wait_ge(s_row2[half], i * 16 + 16)
                        for j in range(NJD):
                            last = dve.tensor_scalar(hot_d[:, j, :], rows[:, half, 1, :], g.nodecol[:, j:j + 1], None, ALU.is_equal)
                        last.then_inc(s_hot2, 1)
                        dve.wait_ge(s_hot2, k + 1)
                        dve.sem_inc(s_row2_free, 1)
                        dve.wait_ge(s_sent[half], i * (CH * 16) + 16)

                        def sum_parts(ch):
                            dve.wait_ge(s_gat2, k * CHAINS + ch + 1)
                            dve.tensor_reduce(stage[:, half, ch * PER:(ch + 1) * PER, 0:F],
                                              pdel[:, ch, 0:PER * 3 * F].rearrange("p (t k f) -> p t f k", k=3, f=F),
                                              AX, ALU.add).then_inc(s_out2, 1)

                        for step in range(PER):
                            for j in range(2):
                                dve.wait_ge(s_before[j], k * PER + step + 1)
                                dve.wait_ge(s_read[j], k * PER + step + 1)
                                for m in range(2):
                                    ch = 2 * j + m
                                    q = ch * PER + step
                                    last = dve.scalar_tensor_tensor(
                                        hit[:, ch, :], hot_c[:, half, q, :], 1.0,
                                        pacc[:, j, m * NCELL:(m + 1) * NCELL], ALU.mult, ALU.mult,
                                        accum_out=place[:, q:q + 1])
                                last.then_inc(s_read[j], 1)
                            if step:
                                sum_parts(step - 1)
                        for j in range(2):
                            dve.wait_ge(s_read[j], (k + 1) * PER + 1)
                        st.add(dve.tensor_scalar(skip[:, :], cell[:, ds(k * CH, CH)], 0.0, NOWHERE, ALU.is_lt, ALU.mult))
                        st.do(dve.tensor_copy(place_i[:, :], place[:, :]))
                        st.add(dve.tensor_scalar(low_i[:, :], place_i[:, :], P - 1, None, ALU.bitwise_and))
                        st.do(dve.tensor_scalar(high_i[:, :], place_i[:, :], 7, None, ALU.logical_shift_right))
                        st.do(dve.scalar_tensor_tensor(place[:, :], low_i[:, :], float(NTC), high_i[:, :], ALU.mult, ALU.add))
                        dve.tensor_tensor(idx[:, half, :], place[:, :], skip[:, :], ALU.add)
                        dve.tensor_copy(stage[:, half, :, F:F + 3], frac[:, ds(k * CH, CH), :])
                        dve.tensor_copy(stage[:, half, :, F + 3].rearrange("p (c t) -> p c t", c=CHAINS),
                                        by_chain[:, :, ds(k * PER, PER), 7]).then_inc(s_rest, 1)
                        sum_parts(CHAINS - 1)
                        assert st.n == S
                        dve.wait_ge(s_rest, k + 1)
                        dve.wait_ge(s_out2, (k + 2) * CHAINS)

            @block.tensor
            def _(pe):
                pe.sem_inc(s_ranked, 2)
                pe.sem_inc(s_out2, CHAINS)
                with pe.Fori(0, LOOP) as i:
                    for half in range(2):
                        k = i * 2 + half
                        dst_sb = load_values(nc, PE, g.table_b[0:1, 1, ds(k * CH, CH)], ND - 1)
                        pe.wait_ge(s_hotc2, k + 1)

                        def add_up(j, step, matrix):
                            for m in range(2):
                                q = (2 * j + m) * PER + step
                                last = pe.matmul(pacc[:, j, m * NCELL:(m + 1) * NCELL], matrix[:, :],
                                                 hot_c[:, half, q, :], start=False, stop=True, skip_group_check=True)
                            return last

                        def gather(ch):
                            pe.wait_ge(s_out2, k * CHAINS + ch + 1)
                            for q in range(ch * PER, (ch + 1) * PER):
                                d, at = dst_sb[q], q % PER * 3 * F
                                for j in range(NJD):
                                    last = pe.matmul(pdel[:, ch, at:at + 3 * F], hot_d[:, j, q * P:(q + 1) * P],
                                                     hparts[:, ds(d * (NJD * 3 * F) + j * 3 * F, 3 * F)],
                                                     start=(j == 0), stop=(j == NJD - 1))
                            last.then_inc(s_gat2, 1)

                        for j in range(2):
                            add_up(j, 0, g.before).then_inc(s_before[j], 1)
                        pe.wait_ge(s_hot2, k + 1)
                        for step in range(PER):
                            for j in range(2):
                                pe.wait_ge(s_read[j], k * PER + step + 2)
                                last = add_up(j, step, g.from_on)
                                if step + 1 < PER:
                                    add_up(j, step + 1, g.before).then_inc(s_before[j], 1)
                            if step + 1 == PER:
                                last.then_inc(s_ranked, 1)
                            gather(step)

            @block.gpsimd
            def _(pool):
                g.open_sent(pool, s_sent)
                with pool.Fori(0, LOOP) as i:
                    for half in range(2):
                        k = i * 2 + half
                        pool.wait_ge(s_rest, k + 1)
                        pool.wait_ge(s_out2, (k + 2) * CHAINS)
                        pool.sem_inc(s_tick, 1)
                        for q in range(CH):
                            pool.indirect_dma_start(g.rows_c2, bass.IndirectOffsetOnAxis(idx[:, half, q:q + 1], 0),
                                                    stage[:, half, q, :], None, bounds_check=P * NTC - 1,
                                                    oob_is_err=False).then_inc(s_sent[half], 16)
                for half in range(2):
                    pool.wait_ge(s_sent[half], LOOP * CH * 16 + 16)

        s_tab_back = sem("s_tables_back")
        with nc.Block() as block:
            @block.sync
            def _(sp):
                sp.dma_start(g.table_b[0:1, :, :], g.tab_b.unsqueeze(0)).then_inc(s_tab_back, 16)

            @block.vector
            def _(dve):
                dve.wait_ge(s_tab_back, 16)
                dve.scalar_tensor_tensor(g.table_b[0:1, 1, :], g.table_b[0:1, 0, :], 16.0, g.table_b[0:1, 1, :],
                                         ALU.mult, ALU.add)


def end_first_layer(g, c, conv_b):
    nc, sem = g.nc, g.sem
    sb = lambda n, s, d=F32: g.sb(n, s, d, c)
    acc = c.enter_context(nc.psum_tensor("acc_conv", [P, 4 * 512], F32))
    with ExitStack() as c2:
        add_up_by_source(g, c2, "r2", g.msg2, F, acc)
    z, bv = sb("z3", [P, NBLK, F]), sb("conv_bv", [P, F])
    ln = NormBuffers(mean=g.mean, var=g.var, std=g.std, sq=sb("ln_sq2", [P, NBLK, F]))
    s_b, s_dve, s_var, s_std = sem("s_conv_b"), sem("s_dve_l"), sem("s_var2"), sem("s_std2")
    with nc.Block() as block:
        @block.sync
        def _(sp):
            sp.dma_start(bv[:, :], conv_b.rearrange("(o f) -> o f", o=1).to_broadcast([P, F])).then_inc(s_b, 16)

        @block.vector
        def _(dve):
            st = Steps(dve, s_dve)
            dve.wait_ge(s_b, 16)
            st.do(dve.tensor_tensor(z[:, :, :], acc[:, 0:NBLK * F].rearrange("p (b f) -> p b f", f=F),
                                    g.rdeg[:, :].unsqueeze(2).to_broadcast([P, NBLK, F]), ALU.mult))
            st.do(dve.tensor_tensor(z[:, :, :], z[:, :, :], bv[:, :].unsqueeze(1).to_broadcast([P, NBLK, F]), ALU.add))
            st.do(dve.tensor_tensor(g.x[:, :, :], g.x[:, :, :], z[:, :, :], ALU.add))

            def root():
                dve.sem_inc(s_var, 1)
                dve.wait_ge(s_std, 1)
            layer_norm(dve, root, st, ln, g.x, g.h)
            st.do(dve.tensor_scalar(g.h[:, :, :], g.h[:, :, :], 0.0, None, ALU.max))
            split_parts(dve, st, [g.hparts[:, :, k, :] for k in range(3)], g.h[:, :, :], ln.sq[:, :, :])

        @block.scalar
        def _(act):
            act.wait_ge(s_var, 1)
            act.activation(g.std[:, :], g.var[:, :], ACT.Sqrt).then_inc(s_std, 1)


def second_layer(g, c, W1, b1, W2, b2, W3, b3, W4, b4, out):
    nc, sem = g.nc, g.sem
    sb = lambda n, s, d=F32: g.sb(n, s, d, c)
    NJD, NJS = DST_SB // P, SRC_SB // P
    LOOP = NCHK_B // 2
    NBS = NA * NJS
    G = 4
    AHEAD = 3
    with ExitStack() as c_ps:
        bufs = ExitStack()
        sb1 = lambda n, s, d=F32: g.sb(n, s, d, bufs)
        NG_CH, NPAIR = CH // G, CH // 2
        rows = sb1("rows3", [P, 2, 2, CH * P], F16)
        hot_d = sb1("hot_d3", [P, 2, NJD, CH * P], BF16)
        hot_s = sb1("hot_s3", [P, 2, NJS, CH * P], BF16)
        hot_e = sb1("hot_e3", [P, 2, G, DST_SB + SRC_SB], BF16)
        got = sb1("got3", [P, 2, G, 2 * F])
        msg = sb1("msg3", [P, 2, 3, G, 2 * F], BF16)
        acc = c_ps.enter_context(nc.psum_tensor("acc_mi_mo", [P, 7 * 512], F32))
        own_d = sb1("own_d3", [P, 2, G, NJD * 3 * F], BF16)
        own_s = sb1("own_s3", [P, 2, G, NJS * 3 * F], BF16)
        s_own = sem("s_own_blocks3")
        pg = c_ps.enter_context(nc.psum_tensor("pg3", [P, 512], F32))
        hparts = g.hparts[:, :, :, :].rearrange("p b k f -> p (b k f)")
        MI = P
        MO = MI + NBLK * F
        s_row, s_row_free = [sem(f"s_rows3{h}") for h in range(2)], sem("s_rows3_free")
        s_hot, s_gat, s_read = sem("s_hot3"), sem("s_gathered3"), sem("s_gathered3_read")
        s_hote, s_used, s_all = sem("s_hot_e3"), sem("s_msg3_used"), sem("s_hots3_used")
        s_prod, s_rest = sem("s_msg3_times_weight"), sem("s_msg3_rest")
        s_high, s_mid, s_low, s_tick = sem("s_msg3_high"), sem("s_msg3_mid"), sem("s_msg3_low"), sem("s_pool_turns3")
        with nc.Block() as block:
            @block.sync
            def _(sp):
                with sp.Fori(0, LOOP) as i:
                    for half in range(2):
                        k = i * 2 + half
                        sp.wait_ge(s_row_free, k + 1)
                        for kind in range(2):
                            sp.dma_start(rows[:, half, kind, :],
                                         g.local_rows[kind:kind + 1, ds(k * CH, CH), :].rearrange("o t e -> o (t e)")
                                         .to_broadcast([P, CH * P])).then_inc(s_row[half], 16)

            @block.vector
            def _(dve):
                dve.sem_inc(s_row_free, 2)
                dve.sem_inc(s_low, 2)

                def node_hot(half, n):
                    hot, kind, j = (hot_d, 1, n) if n < NJD else (hot_s, 0, n - NJD)
                    return dve.tensor_scalar(hot[:, half, j, :], rows[:, half, kind, :], g.nodecol[:, j:j + 1],
                                             None, ALU.is_equal)

                dve.wait_ge(s_row[0], 32)
                for n in range(NJD + NJS):
                    last = node_hot(0, n)
                last.then_inc(s_hot, 1)
                dve.wait_ge(s_hot, 1)
                dve.sem_inc(s_row_free, 1)

                def two_chunks(i, more):
                    for half in range(2):
                        k = i * 2 + half
                        follows = half == 0 or more
                        if follows:
                            dve.wait_ge(s_row[1 - half], (i + 1 + half) * 32)
                            dve.wait_ge(s_all, k + 1)
                        for pair in range(NPAIR):
                            gr = pair // 2
                            n = k * NG_CH + gr
                            if follows and pair < NJD + NJS:
                                last = node_hot(1 - half, pair)
                                if pair == NJD + NJS - 1:
                                    last.then_inc(s_hot, 1)
                            dve.wait_ge(s_gat, k * NPAIR + pair + 3)
                            if pair % 2 == 0:
                                dve.wait_ge(s_low, n + 1)
                            dve.tensor_reduce(got[:, gr % 2, pair % 2 * 2:pair % 2 * 2 + 2, :]
                                              .rearrange("p t (s f) -> p (t s) f", s=2),
                                              pg[:, 0:12 * F].rearrange("p (t k f) -> p t f k", k=3, f=F),
                                              AX, ALU.add).then_inc(s_read, 1)
                            if pair % 2 == 0:
                                dve.wait_ge(s_used, n + 1)
                            for q in range(pair % 2 * 2, pair % 2 * 2 + 2):
                                t = k * CH + gr * G + q
                                dve.tensor_scalar(hot_e[:, gr % 2, q, 0:DST_SB], g.iota16[:, :],
                                                  g.edges[:, ds(t, 1), 1:2].rearrange("p a b -> p (a b)"), None, ALU.is_equal)
                                last = dve.tensor_scalar(hot_e[:, gr % 2, q, DST_SB:], g.iota16[:, 0:SRC_SB],
                                                         g.edges[:, ds(t, 1), 0:1].rearrange("p a b -> p (a b)"), None, ALU.is_equal)
                            last.then_inc(s_hote, 1)
                        if follows:
                            dve.wait_ge(s_hot, k + 2)
                            dve.sem_inc(s_row_free, 1)

                with dve.Fori(0, LOOP - 1) as i:
                    two_chunks(i, True)
                two_chunks(LOOP - 1, False)

            @block.scalar
            def _(act):
                def take_blocks(n, b):
                    both = load_values(nc, ACTE, g.table_b[0:1, 1, ds(n * G, G)], NA * 16 - 1)
                    for q in range(G):
                        a = both[q] >> 4
                        d = nc.s_assert_within(both[q] & 15, min_val=0, max_val=ND - 1,
                                               skip_runtime_bounds_check_because="the table's blocks are clamped")
                        act.activation(own_s[:, b, q, :], hparts[:, ds(a * (NJS * 3 * F), NJS * 3 * F)], ACT.Copy)
                        last = act.activation(own_d[:, b, q, :], hparts[:, ds(d * (NJD * 3 * F), NJD * 3 * F)], ACT.Copy)
                    last.then_inc(s_own, 1)

                take_blocks(0, 0)
                with act.Fori(0, LOOP) as i:
                    for half in range(2):
                        for gr in range(NG_CH):
                            n = i * (2 * NG_CH) + (half * NG_CH + gr)
                            b = gr % 2
                            act.wait_ge(s_gat, n * 2 + 2)
                            take_blocks(n + 1, 1 - b)
                            act.wait_ge(s_prod, n + 1)
                            act.wait_ge(s_used, n + 1)
                            act.activation(msg[:, b, 0, :, :], got[:, b, :, :], ACT.Copy).then_inc(s_high, 1)
                            act.wait_ge(s_rest, n + 1)
                            act.activation(msg[:, b, 1, :, :], got[:, b, :, :], ACT.Copy).then_inc(s_mid, 1)

            @block.gpsimd
            def _(pool):
                with pool.Fori(0, LOOP) as i:
                    for half in range(2):
                        for gr in range(NG_CH):
                            n = i * (2 * NG_CH) + (half * NG_CH + gr)
                            b = gr % 2
                            pool.wait_ge(s_read, n * 2 + 3)
                            pool.sem_inc(s_tick, 1)
                            pool.tensor_tensor(got[:, b, :, :], got[:, b, :, :],
                                               g.edges[:, ds(i * (2 * CH) + (half * CH + gr * G), G), 5].unsqueeze(2)
                                               .to_broadcast([P, G, 2 * F]), ALU.mult).then_inc(s_prod, 1)
                            pool.wait_ge(s_high, n + 1)
                            pool.sem_inc(s_tick, 1)
                            pool.tensor_tensor(got[:, b, :, :], got[:, b, :, :], msg[:, b, 0, :, :],
                                               ALU.subtract).then_inc(s_rest, 1)
                            pool.wait_ge(s_mid, n + 1)
                            pool.sem_inc(s_tick, 1)
                            pool.tensor_tensor(msg[:, b, 2, :, :], got[:, b, :, :], msg[:, b, 1, :, :],
                                               ALU.subtract).then_inc(s_low, 1)

            @block.tensor
            def _(pe):
                for b in range(7):
                    pe.matmul(acc[:, b * 512:(b + 1) * 512], g.ident[:, :], g.zero512[:, :], start=True, stop=True)
                pe.sem_inc(s_used, 2)
                pe.sem_inc(s_all, 1)
                pe.sem_inc(s_read, 1)
                pe.sem_inc(s_gat, 2)

                def gather(i, m):
                    half, pair = m // NPAIR % 2, m % NPAIR
                    if pair == 0:
                        pe.wait_ge(s_hot, i * 2 + (m // NPAIR + 1))
                    if m % 2 == 0:
                        pe.wait_ge(s_own, i * (2 * NG_CH) + (m // 2 + 1))
                    pe.wait_ge(s_read, i * (2 * NPAIR) + (m + 1))
                    for q in range(2):
                        e = slice((pair * 2 + q) * P, (pair * 2 + q + 1) * P)
                        for side, hot, nj, own in ((0, hot_s, NJS, own_s), (1, hot_d, NJD, own_d)):
                            at = (q * 2 + side) * 3 * F
                            for j in range(nj):
                                last = pe.matmul(pg[:, at:at + 3 * F], hot[:, half, j, e],
                                                 own[:, m // 2 % 2, m % 2 * 2 + q, j * 3 * F:(j + 1) * 3 * F],
                                                 start=(j == 0), stop=(j == nj - 1))
                    last.then_inc(s_gat, 1)
                    if pair == NPAIR - 1:
                        pe.wait_ge(s_gat, i * (2 * NPAIR) + (m + 3))
                        pe.sem_inc(s_all, 1)

                def add_up(i, m, both):
                    pair = m % NPAIR
                    b = pair // 2 % 2
                    pe.wait_ge(s_hote, i * (2 * NPAIR) + (m + 1))
                    if m % 2 == 0:
                        pe.wait_ge(s_low, i * (2 * NG_CH) + (m // 2 + 3))
                    for p in range(2):
                        a, d = both[pair % 4 * 2 + p] >> 4, both[pair % 4 * 2 + p] & 15
                        q = pair % 2 * 2 + p
                        for side, nj, sb0, col, hot0 in ((0, NJD, d, MI, 0), (1, NJS, a, MO, DST_SB)):
                            for j in range(nj):
                                for part in range(3):
                                    last = pe.matmul(
                                        acc[:, ds(sb0 * (nj * F) + (j * F + col), F)],
                                        hot_e[:, b, q, hot0 + j * P:hot0 + (j + 1) * P],
                                        msg[:, b, part, q, side * F:(side + 1) * F],
                                        start=False, stop=True, skip_group_check=True)
                    if m % 2:
                        last.then_inc(s_used, 1)

                def two_chunks(i, more):
                    for m in range(2 * NPAIR):
                        if m + AHEAD < 2 * NPAIR or more:
                            gather(i, m + AHEAD)
                        if m % 4 == 0:
                            both = load_values(nc, PE, g.table_b[0:1, 1, ds(i * (2 * CH) + 2 * m, 8)], NA * 16 - 1)
                        add_up(i, m, both)

                for m in range(AHEAD):
                    gather(0, m)
                with pe.Fori(0, LOOP - 1) as i:
                    two_chunks(i, True)
                two_chunks(LOOP - 1, False)
        bufs.close()
        cat = sb("cat", [P, NBLK, 3 * F])
        s_cat = sem("s_cat")
        with nc.Block() as block:
            @block.vector
            def _(dve):
                dve.memset(cat[:, NBS:NBLK, F:2 * F], 0.0)
                dve.tensor_copy(cat[:, :, 0:F], acc[:, MI:MO].rearrange("p (b f) -> p b f", f=F))
                dve.tensor_copy(cat[:, 0:NBS, F:2 * F], acc[:, MO:MO + NBS * F].rearrange("p (b f) -> p b f", f=F))
                dve.tensor_copy(cat[:, :, 2 * F:3 * F], g.h[:, :, :]).then_inc(s_cat, 1)
                dve.wait_ge(s_cat, 1)

    NG = NBLK // 4
    layers = [(W1, b1, 3 * F), (W2, b2, F), (W3, b3, F), (W4, b4, F)]
    ws = [sb(f"mlp_w{n}", [k, F]) for n, (_, _, k) in enumerate(layers)]
    bs = [sb(f"mlp_b{n}", [F, 1]) for n in range(4)]
    catT = sb("catT", [3 * F, 2, 512])
    act_t = sb("act_t", [F, 4, 2, 512])
    res = sb("res", [P, NBLK, F])
    s_w, s_tr, s_in = sem("s_mlp_w"), sem("s_mlp_tr"), sem("s_mlp_in")
    s_mm, s_act = [sem(f"s_mlp_mm{n}") for n in range(4)], [sem(f"s_mlp_act{n}") for n in range(4)]
    s_back, s_res, s_out, s_dve = sem("s_mlp_back"), sem("s_mlp_res"), sem("s_out"), sem("s_dve_m")
    pt = c.enter_context(nc.psum_tensor("pt4", [P, 2, 512], F32))
    pd = c.enter_context(nc.psum_tensor("pd4", [P, 4, 512], F32))
    pb = c.enter_context(nc.psum_tensor("pb4", [P, 2, 512], F32))
    with nc.Block() as block:
        @block.sync
        def _(sp):
            for n, (w, b, k) in enumerate(layers):
                sp.dma_start(ws[n][:, :], w).then_inc(s_w, 16)
                with nc.allow_non_contiguous_dma(reason="a bias column"):
                    sp.dma_start(bs[n][:, :], b.rearrange("(f o) -> f o", o=1)).then_inc(s_w, 16)
            sp.wait_ge(s_res, NG)
            sp.dma_start(out[0:FULL_BLK * P, :].rearrange("(b p) f -> p b f", p=P),
                         res[:, 0:FULL_BLK, :]).then_inc(s_out, 16)
            sp.dma_start(out[FULL_BLK * P:N, :], res[0:REST, FULL_BLK, :]).then_inc(s_out, 16)
            sp.wait_ge(s_out, 32)

        @block.tensor
        def _(pe):
            pe.wait_ge(s_w, 128)
            for n in range(NG):
                if n >= 2:
                    pe.wait_ge(s_in, n - 1)
                for b in range(4):
                    last = pe.transpose(pt[0:3 * F, n % 2, b * P:(b + 1) * P], cat[:, n * 4 + b, :], g.ident[:, :])
                last.then_inc(s_tr, 1)
                for layer in range(4):
                    if layer == 0:
                        pe.wait_ge(s_in, n + 1)
                        rhs = catT[:, n % 2, :]
                    else:
                        pe.wait_ge(s_act[layer - 1], n + 1)
                        rhs = act_t[:, layer - 1, n % 2, :]
                    if n:
                        pe.wait_ge(s_act[layer], n)
                    pe.matmul(pd[0:F, layer, :], ws[layer][:, :], rhs, start=True, stop=True).then_inc(s_mm[layer], 1)
                pe.wait_ge(s_act[3], n + 1)
                if n >= 2:
                    pe.wait_ge(s_res, n - 1)
                for b in range(4):
                    last = pe.transpose(pb[:, n % 2, b * F:(b + 1) * F], act_t[:, 3, n % 2, b * P:(b + 1) * P],
                                        g.ident[0:F, 0:F])
                last.then_inc(s_back, 1)

        @block.scalar
        def _(act):
            act.wait_ge(s_w, 128)
            for n in range(NG):
                for layer in range(4):
                    act.wait_ge(s_mm[layer], n + 1)
                    if n >= 2 and layer == 3:
                        act.wait_ge(s_back, n - 1)
                    act.activation(act_t[:, layer, n % 2, :], pd[0:F, layer, :], ACT.Tanh,
                                   bias=bs[layer][:, :]).then_inc(s_act[layer], 1)

        @block.vector
        def _(dve):
            for n in range(NG):
                dve.wait_ge(s_tr, n + 1)
                if n >= 2:
                    dve.wait_ge(s_mm[0], n - 1)
                dve.tensor_copy(catT[:, n % 2, :], pt[0:3 * F, n % 2, :]).then_inc(s_in, 1)
                if n:
                    dve.wait_ge(s_back, n)
                    m = n - 1
                    dve.tensor_tensor(res[:, 4 * m:4 * m + 4, :], g.x[:, 4 * m:4 * m + 4, :],
                                      pb[:, m % 2, 0:4 * F].rearrange("p (b f) -> p b f", f=F), ALU.add).then_inc(s_res, 1)
            m = NG - 1
            dve.wait_ge(s_back, NG)
            dve.tensor_tensor(res[:, 4 * m:4 * m + 4, :], g.x[:, 4 * m:4 * m + 4, :],
                              pb[:, m % 2, 0:4 * F].rearrange("p (b f) -> p b f", f=F), ALU.add).then_inc(s_res, 1)


_INS = ['x', 'src', 'dst', 'edge_attr_3', 'edge_weight1', 'L0_gnn_stn1_w', 'L0_gnn_stn1_b',
        'L0_gnn_stn2_w', 'L0_gnn_stn2_b', 'L0_gnn_stn3_w', 'L0_gnn_stn3_b', 'L0_gnn_stn4_w',
        'L0_gnn_stn4_b', 'L0_gnn_conv_w', 'L0_gnn_conv_b', 'L1_gnn_W1', 'L1_gnn_b1', 'L1_gnn_W2',
        'L1_gnn_b2', 'L1_gnn_W3', 'L1_gnn_b3', 'L1_gnn_W4', 'L1_gnn_b4']


def kernel(**inputs):
    import concourse.bacc as _bacc
    from concourse.bass_utils import run_bass_kernel_spmd as _run

    nc = _bacc.Bacc("TRN2", target_bir_lowering=False, num_devices=1)
    arrays, args = {}, []
    for name in _INS:
        a = np.ascontiguousarray(inputs[name])
        arrays[f"in_{name}"] = a
        args.append(nc.dram_tensor(f"in_{name}", a.shape, mybir.dt.from_np(a.dtype), kind="ExternalInput").ap())
    out = nc.dram_tensor("out_0", (N, F), F32, kind="ExternalOutput").ap()
    program(nc, *args, out)
    r = _run(nc, [arrays], core_ids=[0])
    return np.asarray(r.results[0]["out_0"])
```
